# Optimizing a Trainium2 kernel written in Bass

```python
import numpy as np
import jax
import jax.numpy as jnp

def _softmax(x, axis=-1):
    return jax.nn.softmax(x, axis=axis)

def _gelu(x):
    return jax.nn.gelu(x, approximate=True)

def _silu(x):
    return jax.nn.silu(x)

def _sigmoid(x):
    return jax.nn.sigmoid(x)

def _layernorm(x, axis=-1, eps=1e-05):
    m = jnp.mean(x, axis=axis, keepdims=True)
    v = jnp.var(x, axis=axis, keepdims=True)
    return (x - m) / jnp.sqrt(v + eps)

def _scatter_add(tgt, idx, src, axis=0):
    return tgt.at[idx].add(src)

def _segment_sum(src, seg, n):
    return jax.ops.segment_sum(src, seg, n)
kernel_name = 'mk_seq_postln_d2_jaxref_r8_5571ab'

def setup_inputs(seed: int=0):
    np.random.seed(seed)
    _w = jnp.asarray

    def _L0_attn_setup():
        import jax, jax.numpy as jnp
        import numpy as np
        B, T, HID = (4, 256, 128)
        H, DK, DV, K = (8, 64, 128, 4)
        EPS = 1e-05

        def _dw_causal_conv(x, w, b):
            xt = jnp.transpose(x, (0, 2, 1))
            y = jax.lax.conv_general_dilated(xt, w, window_strides=(1,), padding=[(K - 1, 0)], dimension_numbers=('NCH', 'OIH', 'NCH'), feature_group_count=x.shape[-1])
            y = y + b[None, :, None]
            return jnp.transpose(y, (0, 2, 1))

        def _forward(x, Wq, Wk, Wv, Wa, ba, Wb, bb, Wg, Wo, qc_w, qc_b, kc_w, kc_b, vc_w, vc_b, ln_w, ln_b):
            b, t = (x.shape[0], x.shape[1])
            scale = DK ** (-0.5)
            q = x @ Wq.T
            k = x @ Wk.T
            v = x @ Wv.T
            q = jax.nn.silu(_dw_causal_conv(q, qc_w, qc_b))
            k = jax.nn.silu(_dw_causal_conv(k, kc_w, kc_b))
            v = jax.nn.silu(_dw_causal_conv(v, vc_w, vc_b))
            q = q.reshape(b, t, H, DK)
            k = (k * scale).reshape(b, t, H, DK)
            v = v.reshape(b, t, H, DV)
            a = jax.nn.sigmoid(x @ Wa.T + ba).reshape(b, t, H, DV)
            beta = jax.nn.sigmoid(x @ Wb.T + bb)

            def step(S, ins):
                q_t, k_t, v_t, a_t, b_t = ins
                read = jnp.einsum('bhk,bhkv->bhv', k_t, S)
                err = read - v_t
                S = a_t[:, :, None, :] * S - b_t[:, :, None, None] * k_t[..., None] * err[:, :, None, :]
                o_t = jnp.einsum('bhk,bhkv->bhv', q_t, S)
                return (S, o_t)
            to_tbh = lambda u: jnp.moveaxis(u, 1, 0)
            S0 = jnp.zeros((b, H, DK, DV), x.dtype)
            _, o = jax.lax.scan(step, S0, (to_tbh(q), to_tbh(k), to_tbh(v), to_tbh(a), to_tbh(beta)))
            o = jnp.moveaxis(o, 0, 1)
            mu = jnp.mean(o, axis=-1, keepdims=True)
            var = jnp.mean((o - mu) ** 2, axis=-1, keepdims=True)
            o = (o - mu) * jax.lax.rsqrt(var + EPS) * ln_w + ln_b
            g = jax.nn.sigmoid(x @ Wg.T).reshape(b, t, H, DV)
            o = (o * g).reshape(b, t, H * DV)
            return o @ Wo.T
        key = jax.random.key(seed)
        ks = jax.random.split(key, 20)
        s = 0.02
        inp = {'x': jax.random.normal(ks[0], (B, T, HID), jnp.float32), 'Wq': jax.random.normal(ks[1], (H * DK, HID), jnp.float32) * s, 'Wk': jax.random.normal(ks[2], (H * DK, HID), jnp.float32) * s, 'Wv': jax.random.normal(ks[3], (H * DV, HID), jnp.float32) * s, 'Wa': jax.random.normal(ks[4], (H * DV, HID), jnp.float32) * s, 'ba': jax.random.normal(ks[5], (H * DV,), jnp.float32) * s, 'Wb': jax.random.normal(ks[6], (H, HID), jnp.float32) * s, 'bb': jax.random.normal(ks[7], (H,), jnp.float32) * s, 'Wg': jax.random.normal(ks[8], (H * DV, HID), jnp.float32) * s, 'Wo': jax.random.normal(ks[9], (HID, H * DV), jnp.float32) * s, 'qc_w': jax.random.normal(ks[10], (H * DK, 1, K), jnp.float32) * 0.3, 'qc_b': jnp.zeros((H * DK,), jnp.float32), 'kc_w': jax.random.normal(ks[11], (H * DK, 1, K), jnp.float32) * 0.3, 'kc_b': jnp.zeros((H * DK,), jnp.float32), 'vc_w': jax.random.normal(ks[12], (H * DV, 1, K), jnp.float32) * 0.3, 'vc_b': jnp.zeros((H * DV,), jnp.float32), 'ln_w': jnp.ones((DV,), jnp.float32), 'ln_b': jnp.zeros((DV,), jnp.float32)}
        return inp
    _L0_attn_in = _L0_attn_setup()

    def _L0_ffn_setup():
        import jax, jax.numpy as jnp
        import numpy as np
        N_EMBD = 128
        EXPERT_SIZES = [(4, 128), (4, 256)]
        TOP_K = 2
        B, S = (1, 256)
        WIDTHS = []
        for count, size in EXPERT_SIZES:
            WIDTHS += [size] * count
        OFFSETS = np.concatenate([[0], np.cumsum(WIDTHS)]).astype(np.int64)
        E = len(WIDTHS)
        TOTAL_W = int(OFFSETS[-1])
        MAX_W = max(WIDTHS)

        def _stack_experts(w1, w2):
            W1e, W2e = ([], [])
            for e in range(E):
                off, wd = (int(OFFSETS[e]), WIDTHS[e])
                pad = MAX_W - wd
                W1e.append(jnp.pad(w1[:, off:off + wd], ((0, 0), (0, pad))))
                W2e.append(jnp.pad(w2[off:off + wd, :], ((0, pad), (0, 0))))
            return (jnp.stack(W1e), jnp.stack(W2e))
        key = jax.random.key(seed)
        k1, k2, k3, k4 = jax.random.split(key, 4)
        x = jax.random.normal(k1, (B, S, N_EMBD), jnp.float32)
        router_w = jax.random.normal(k2, (E, N_EMBD), jnp.float32) * 0.02
        w1 = jax.random.truncated_normal(k3, -3.0, 3.0, (N_EMBD, TOTAL_W), jnp.float32) * 0.02
        w2 = jax.random.truncated_normal(k4, -3.0, 3.0, (TOTAL_W, N_EMBD), jnp.float32) * 0.02
        return {'x': x, 'router_w': router_w, 'w1': w1, 'w2': w2}
    _L0_ffn_in = _L0_ffn_setup()

    def _L1_attn_setup():
        import jax, jax.numpy as jnp
        import numpy as np
        B, T, C = (64, 32, 128)
        N_HEAD, HEAD_SIZE, KV_RANK = (16, 64, 128)
        BLOCK_SIZE = 32
        key = jax.random.key(seed)
        ks = jax.random.split(key, 5)
        HD = N_HEAD * HEAD_SIZE

        def init(k, shape):
            fan_in = shape[0]
            bound = 1.0 / np.sqrt(fan_in)
            return jax.random.uniform(k, shape, jnp.float32, -bound, bound)
        return {'x': jax.random.normal(ks[0], (B, T, C), jnp.float32), 'w_kv_down': init(ks[1], (C, KV_RANK)), 'w_kv_up': init(ks[2], (KV_RANK, 2 * HD)), 'w_q': init(ks[3], (C, HD)), 'w_out': init(ks[4], (HD, C))}
    _L1_attn_in = _L1_attn_setup()

    def _L1_ffn_setup():
        import jax, jax.numpy as jnp
        import numpy as np
        N_EMBD = 128
        NUM_EXPERTS = 8
        TOP_K = 2
        D_FF = 4 * N_EMBD
        B, S = (4, 256)
        key = jax.random.key(seed)
        ks = jax.random.split(key, 7)
        scale = lambda fan_in: 1.0 / np.sqrt(fan_in)
        x = jax.random.normal(ks[0], (B, S, N_EMBD), dtype=jnp.float32)
        W_router = jax.random.normal(ks[1], (N_EMBD, NUM_EXPERTS), dtype=jnp.float32) * scale(N_EMBD)
        b_router = jnp.zeros((NUM_EXPERTS,), dtype=jnp.float32)
        W1 = jax.random.normal(ks[2], (NUM_EXPERTS, N_EMBD, D_FF), dtype=jnp.float32) * scale(N_EMBD)
        b1 = jnp.zeros((NUM_EXPERTS, D_FF), dtype=jnp.float32)
        W2 = jax.random.normal(ks[3], (NUM_EXPERTS, D_FF, N_EMBD), dtype=jnp.float32) * scale(D_FF)
        b2 = jnpp = jnp.zeros((NUM_EXPERTS, N_EMBD), dtype=jnp.float32)
        return {'x': x, 'W_router': W_router, 'b_router': b_router, 'W1': W1, 'b1': b1, 'W2': W2, 'b2': b2}
    _L1_ffn_in = _L1_ffn_setup()
    _d = {'L0_attn_x': _L0_attn_in['x'], 'L0_attn_Wq': _L0_attn_in['Wq'], 'L0_attn_Wk': _L0_attn_in['Wk'], 'L0_attn_Wv': _L0_attn_in['Wv'], 'L0_attn_Wa': _L0_attn_in['Wa'], 'L0_attn_ba': _L0_attn_in['ba'], 'L0_attn_Wb': _L0_attn_in['Wb'], 'L0_attn_bb': _L0_attn_in['bb'], 'L0_attn_Wg': _L0_attn_in['Wg'], 'L0_attn_Wo': _L0_attn_in['Wo'], 'L0_attn_qc_w': _L0_attn_in['qc_w'], 'L0_attn_qc_b': _L0_attn_in['qc_b'], 'L0_attn_kc_w': _L0_attn_in['kc_w'], 'L0_attn_kc_b': _L0_attn_in['kc_b'], 'L0_attn_vc_w': _L0_attn_in['vc_w'], 'L0_attn_vc_b': _L0_attn_in['vc_b'], 'L0_attn_ln_w': _L0_attn_in['ln_w'], 'L0_attn_ln_b': _L0_attn_in['ln_b'], 'L0_ffn_router_w': _L0_ffn_in['router_w'], 'L0_ffn_w1': _L0_ffn_in['w1'], 'L0_ffn_w2': _L0_ffn_in['w2'], 'L1_attn_w_kv_down': _L1_attn_in['w_kv_down'], 'L1_attn_w_kv_up': _L1_attn_in['w_kv_up'], 'L1_attn_w_q': _L1_attn_in['w_q'], 'L1_attn_w_out': _L1_attn_in['w_out'], 'L1_ffn_W_router': _L1_ffn_in['W_router'], 'L1_ffn_b_router': _L1_ffn_in['b_router'], 'L1_ffn_W1': _L1_ffn_in['W1'], 'L1_ffn_b1': _L1_ffn_in['b1'], 'L1_ffn_W2': _L1_ffn_in['W2'], 'L1_ffn_b2': _L1_ffn_in['b2']}
    _x0 = _d['L0_attn_x']
    _d['L0_attn_x'] = jax.random.normal(jax.random.fold_in(jax.random.key(seed), 1), (2, 1024, 128), dtype=_x0.dtype)
    del _x0
    return _d

def reference(L0_attn_x, L0_attn_Wq, L0_attn_Wk, L0_attn_Wv, L0_attn_Wa, L0_attn_ba, L0_attn_Wb, L0_attn_bb, L0_attn_Wg, L0_attn_Wo, L0_attn_qc_w, L0_attn_qc_b, L0_attn_kc_w, L0_attn_kc_b, L0_attn_vc_w, L0_attn_vc_b, L0_attn_ln_w, L0_attn_ln_b, L0_ffn_router_w, L0_ffn_w1, L0_ffn_w2, L1_attn_w_kv_down, L1_attn_w_kv_up, L1_attn_w_q, L1_attn_w_out, L1_ffn_W_router, L1_ffn_b_router, L1_ffn_W1, L1_ffn_b1, L1_ffn_W2, L1_ffn_b2):

    def _L0_attn_ref(x, Wq, Wk, Wv, Wa, ba, Wb, bb, Wg, Wo, qc_w, qc_b, kc_w, kc_b, vc_w, vc_b, ln_w, ln_b):
        import jax, jax.numpy as jnp
        import numpy as np
        B, T, HID = (4, 256, 128)
        H, DK, DV, K = (8, 64, 128, 4)
        EPS = 1e-05

        def _dw_causal_conv(x, w, b):
            xt = jnp.transpose(x, (0, 2, 1))
            y = jax.lax.conv_general_dilated(xt, w, window_strides=(1,), padding=[(K - 1, 0)], dimension_numbers=('NCH', 'OIH', 'NCH'), feature_group_count=x.shape[-1])
            y = y + b[None, :, None]
            return jnp.transpose(y, (0, 2, 1))

        def _forward(x, Wq, Wk, Wv, Wa, ba, Wb, bb, Wg, Wo, qc_w, qc_b, kc_w, kc_b, vc_w, vc_b, ln_w, ln_b):
            b, t = (x.shape[0], x.shape[1])
            scale = DK ** (-0.5)
            q = x @ Wq.T
            k = x @ Wk.T
            v = x @ Wv.T
            q = jax.nn.silu(_dw_causal_conv(q, qc_w, qc_b))
            k = jax.nn.silu(_dw_causal_conv(k, kc_w, kc_b))
            v = jax.nn.silu(_dw_causal_conv(v, vc_w, vc_b))
            q = q.reshape(b, t, H, DK)
            k = (k * scale).reshape(b, t, H, DK)
            v = v.reshape(b, t, H, DV)
            a = jax.nn.sigmoid(x @ Wa.T + ba).reshape(b, t, H, DV)
            beta = jax.nn.sigmoid(x @ Wb.T + bb)

            def step(S, ins):
                q_t, k_t, v_t, a_t, b_t = ins
                read = jnp.einsum('bhk,bhkv->bhv', k_t, S)
                err = read - v_t
                S = a_t[:, :, None, :] * S - b_t[:, :, None, None] * k_t[..., None] * err[:, :, None, :]
                o_t = jnp.einsum('bhk,bhkv->bhv', q_t, S)
                return (S, o_t)
            to_tbh = lambda u: jnp.moveaxis(u, 1, 0)
            S0 = jnp.zeros((b, H, DK, DV), x.dtype)
            _, o = jax.lax.scan(step, S0, (to_tbh(q), to_tbh(k), to_tbh(v), to_tbh(a), to_tbh(beta)))
            o = jnp.moveaxis(o, 0, 1)
            mu = jnp.mean(o, axis=-1, keepdims=True)
            var = jnp.mean((o - mu) ** 2, axis=-1, keepdims=True)
            o = (o - mu) * jax.lax.rsqrt(var + EPS) * ln_w + ln_b
            g = jax.nn.sigmoid(x @ Wg.T).reshape(b, t, H, DV)
            o = (o * g).reshape(b, t, H * DV)
            return o @ Wo.T
        return _forward(x, Wq, Wk, Wv, Wa, ba, Wb, bb, Wg, Wo, qc_w, qc_b, kc_w, kc_b, vc_w, vc_b, ln_w, ln_b)

    def _L0_ffn_ref(x, router_w, w1, w2):
        import jax, jax.numpy as jnp
        import numpy as np
        N_EMBD = 128
        EXPERT_SIZES = [(4, 128), (4, 256)]
        TOP_K = 2
        B, S = (1, 256)
        WIDTHS = []
        for count, size in EXPERT_SIZES:
            WIDTHS += [size] * count
        OFFSETS = np.concatenate([[0], np.cumsum(WIDTHS)]).astype(np.int64)
        E = len(WIDTHS)
        TOTAL_W = int(OFFSETS[-1])
        MAX_W = max(WIDTHS)

        def _stack_experts(w1, w2):
            W1e, W2e = ([], [])
            for e in range(E):
                off, wd = (int(OFFSETS[e]), WIDTHS[e])
                pad = MAX_W - wd
                W1e.append(jnp.pad(w1[:, off:off + wd], ((0, 0), (0, pad))))
                W2e.append(jnp.pad(w2[off:off + wd, :], ((0, pad), (0, 0))))
            return (jnp.stack(W1e), jnp.stack(W2e))
        b, s, d = x.shape
        xf = x.reshape(-1, d)
        logits = xf @ router_w.T
        probs = jax.nn.sigmoid(logits.astype(jnp.float32))
        topw, sel = jax.lax.top_k(probs, TOP_K)
        topw = topw / (topw.sum(-1, keepdims=True) + 1e-20)
        topw = topw.astype(x.dtype)
        onehot = sel[:, :, None] == jnp.arange(E)[None, None, :]
        combine = jnp.sum(topw[:, :, None] * onehot, axis=1)
        W1e, W2e = _stack_experts(w1, w2)
        h = jnp.einsum('td,edw->tew', xf, W1e)
        h = jnp.square(jax.nn.relu(h))
        y = jnp.einsum('tew,ewd->ted', h, W2e)
        out = jnp.einsum('ted,te->td', y, combine)
        return out.reshape(b, s, d)

    def _L1_attn_ref(x, w_kv_down, w_kv_up, w_q, w_out):
        import jax, jax.numpy as jnp
        import numpy as np
        B, T, C = (64, 32, 128)
        N_HEAD, HEAD_SIZE, KV_RANK = (16, 64, 128)
        BLOCK_SIZE = 32
        Bx, Tx, Cx = x.shape
        HD = N_HEAD * HEAD_SIZE
        latent_kv = x @ w_kv_down
        kv = latent_kv @ w_kv_up
        k, v = (kv[..., :HD], kv[..., HD:])
        k = k.reshape(Bx, Tx, N_HEAD, HEAD_SIZE)
        v = v.reshape(Bx, Tx, N_HEAD, HEAD_SIZE)
        q = (x @ w_q).reshape(Bx, Tx, N_HEAD, HEAD_SIZE)
        scale = HEAD_SIZE ** (-0.5)
        att = jnp.einsum('bqhd,bkhd->bhqk', q, k) * scale
        causal = jnp.tril(jnp.ones((Tx, Tx), dtype=bool))
        att = jnp.where(causal, att, -jnp.inf)
        att = jax.nn.softmax(att, axis=-1)
        y = jnp.einsum('bhqk,bkhd->bqhd', att, v)
        y = y.reshape(Bx, Tx, HD)
        return y @ w_out

    def _L1_ffn_ref(x, W_router, b_router, W1, b1, W2, b2):
        import jax, jax.numpy as jnp
        import numpy as np
        N_EMBD = 128
        NUM_EXPERTS = 8
        TOP_K = 2
        D_FF = 4 * N_EMBD
        B, S = (4, 256)
        Bv, Sv, D = x.shape
        flat_x = x.reshape(-1, D)
        T = flat_x.shape[0]
        logits = flat_x @ W_router + b_router
        top_vals, top_idx = jax.lax.top_k(logits, TOP_K)
        neg_inf = jnp.full_like(logits, -jnp.inf)
        sparse_logits = neg_inf.at[jnp.arange(T)[:, None], top_idx].set(top_vals)
        router_weights = jax.nn.softmax(sparse_logits, axis=-1)
        final_output = jnp.zeros_like(flat_x)
        for e in range(NUM_EXPERTS):
            expert_mask = jnp.any(top_idx == e, axis=-1)
            h = jax.nn.relu(flat_x @ W1[e] + b1[e])
            y = h @ W2[e] + b2[e]
            w = router_weights[:, e] * expert_mask.astype(x.dtype)
            final_output = final_output + y * w[:, None]
        return final_output.reshape(Bv, Sv, D)
    x = L0_attn_x
    x = _layernorm(x + _L0_attn_ref(x, L0_attn_Wq, L0_attn_Wk, L0_attn_Wv, L0_attn_Wa, L0_attn_ba, L0_attn_Wb, L0_attn_bb, L0_attn_Wg, L0_attn_Wo, L0_attn_qc_w, L0_attn_qc_b, L0_attn_kc_w, L0_attn_kc_b, L0_attn_vc_w, L0_attn_vc_b, L0_attn_ln_w, L0_attn_ln_b), axis=-1)
    x = _layernorm(x + _L0_ffn_ref(x, L0_ffn_router_w, L0_ffn_w1, L0_ffn_w2), axis=-1)
    x = _layernorm(x + _L1_attn_ref(x, L1_attn_w_kv_down, L1_attn_w_kv_up, L1_attn_w_q, L1_attn_w_out), axis=-1)
    x = _layernorm(x + _L1_ffn_ref(x, L1_ffn_W_router, L1_ffn_b_router, L1_ffn_W1, L1_ffn_b1, L1_ffn_W2, L1_ffn_b2), axis=-1)
    return x

_drawn_inputs = setup_inputs


def setup_inputs(seed=0):
    import zlib

    import numpy as np

    out = dict(_drawn_inputs(seed))
    spreads = {'L0_attn_qc_b': (0.0, 0.1),
     'L0_attn_kc_b': (0.0, 0.1),
     'L0_attn_vc_b': (0.0, 0.1),
     'L0_attn_ln_w': (1.0, 0.598),
     'L0_attn_ln_b': (0.0, 0.1),
     'L1_ffn_b_router': (0.0, 0.1),
     'L1_ffn_b1': (0.0, 0.1),
     'L1_ffn_b2': (0.0, 0.1)}
    factors = {'L0_attn_Wa': 3.353,
     'L0_attn_ba': 21.519,
     'L0_attn_Wb': 2.985,
     'L0_attn_bb': 20.128,
     'L1_attn_w_q': 3.059}
    for name, (base, spread) in spreads.items():
        noise = np.random.default_rng([zlib.crc32(name.encode()), seed]).standard_normal(out[name].shape)
        drawn = base * np.exp(spread * noise) if base else spread * noise
        out[name] = jnp.asarray(drawn.astype(out[name].dtype))
    for name, factor in factors.items():
        out[name] = (out[name] * factor).astype(out[name].dtype)
    return out
```

```python
from contextlib import ExitStack

import concourse.bass as bass
from concourse import mybir

F32 = mybir.dt.float32
BF16 = mybir.dt.bfloat16
ALU = mybir.AluOpType
ACT = mybir.ActivationFunctionType
AX = mybir.AxisListType

P = 128
B, T, C = 2, 1024, 128
NT = B * T // P
H, DK, DV, TAPS = 8, 64, 128, 4
G = H * DK // P
TS = 128
NS = T // TS
CH = 16
NC = TS // CH
BK = 4
NB = CH // BK
EPS = 1e-5
LOOK = TAPS - 1


class Chain:

    def __init__(self, engine, semaphore):
        self.engine, self.semaphore, self.count = engine, semaphore, 0

    def step(self, instruction):
        self.count += 1
        instruction.then_inc(self.semaphore, 1)
        self.engine.wait_ge(self.semaphore, self.count)


def stage_end(nc, sems):
    for s in sems:
        nc.gpsimd.sem_clear(s)
    nc.all_engine_barrier()


def constants(nc, cst):
    with nc.semaphore("cst_made") as made, nc.Block() as block:
        @block.gpsimd
        def _(pool):
            ch = Chain(pool, made)
            select = nc.gpsimd.affine_select
            for name, value in (("ident", 1.0), ("centre", 1.0 - 1.0 / P)):
                fill = 0.0 if name == "ident" else -1.0 / P
                ch.step(nc.gpsimd.memset(cst[name][:, :], value))
                ch.step(select(out=cst[name][:, :], in_=cst[name][:, :], pattern=[[-1, P]], compare_op=ALU.is_equal,
                               fill=fill, base=0, channel_multiplier=1))
            nc.gpsimd.memset(cst["eps"][:, :], EPS)
            nc.gpsimd.memset(cst["mean"][:, :], 1.0 / P)
            ch.step(nc.gpsimd.memset(cst["head_sum"][:, :, :], 0.0))
            for h in range(2):
                ch.step(nc.gpsimd.memset(cst["head_sum"][DK * h:DK * h + DK, h, :], 1.0))
            for name in ("same_head", "causal_head"):
                ch.step(nc.gpsimd.memset(cst[name][:, :], -1.0))
                for i in range(NB):
                    rows = slice(BK * H * i, BK * H * (i + 1))
                    v = cst[name][rows, :].rearrange("p (i h s) -> p i h s", i=NB, h=H)
                    ch.step(select(out=v, in_=v, pattern=[[0, NB], [-BK, H], [0, BK]], compare_op=ALU.is_ge, fill=0.0,
                                   base=0, channel_multiplier=1))
                    ch.step(select(out=v, in_=v, pattern=[[0, NB], [BK, H], [0, BK]], compare_op=ALU.is_ge, fill=0.0,
                                   base=BK - 1, channel_multiplier=-1))
                    if name == "causal_head":
                        if i:
                            ch.step(nc.gpsimd.memset(v[:, 0:i], 0.0))
                        ch.step(select(out=v[:, i], in_=v[:, i], pattern=[[BK, H], [1, BK]], compare_op=ALU.is_ge,
                                       fill=0.0, base=0, channel_multiplier=-1))
            ch.step(nc.gpsimd.memset(cst["pair_rows"][:, :], -1.0))
            for i in range(NB):
                v = cst["pair_rows"][BK * H * i:BK * H * (i + 1), :]
                ch.step(select(out=v, in_=v, pattern=[[-2 * BK, G]], compare_op=ALU.is_ge, fill=0.0, base=0,
                               channel_multiplier=1))
                ch.step(select(out=v, in_=v, pattern=[[2 * BK, G]], compare_op=ALU.is_ge, fill=0.0, base=2 * BK - 1,
                               channel_multiplier=-1))
            ch.step(nc.gpsimd.memset(cst["above_diag"][:, :], 0.0))
            ch.step(select(out=cst["above_diag"][:, :], in_=cst["above_diag"][:, :], pattern=[[-1, P]],
                           compare_op=ALU.is_ge, fill=-1e30, base=0, channel_multiplier=1))
            ch.step(nc.gpsimd.memset(cst["lower"][:, :, :], 1.0))
            ch.step(select(out=cst["lower"][:, :, :], in_=cst["lower"][:, :, :], pattern=[[1, NE], [-1, NE]],
                           compare_op=ALU.is_gt, fill=0.0, base=0, channel_multiplier=0))
            ch.step(nc.gpsimd.memset(cst["ident16"][:, :], 1.0))
            ch.step(select(out=cst["ident16"][:, :], in_=cst["ident16"][:, :], pattern=[[-1, P]],
                           compare_op=ALU.is_equal, fill=0.0, base=0, channel_multiplier=1))
    return


def delta_attention(nc, cst, ps, d, res):
    with ExitStack() as ctx:
        def sb(name, shape, dt=F32):
            return ctx.enter_context(nc.sbuf_tensor(name, shape, dt))

        def sem(name):
            return ctx.enter_context(nc.semaphore(name))

        HB = H * B
        NBLK = TS // BK
        xT = sb("xT", [P, B, LOOK + T])
        taps = sb("taps", [P, TAPS, 2 * G * P + H * DV])
        wa = sb("wa", [P, H * DV])
        wg = sb("wg", [P, H * DV])
        wb = sb("wb", [P, H, P])
        wo = sb("wo", [P, H, C])
        conv_b = sb("conv_b", [P, 2 * G + H])
        bias_a = sb("bias_a", [P, H])
        bias_b = sb("bias_b", [P, H])
        ln_w = sb("ln_w", [P, 1])
        ln_b = sb("ln_b", [P, 1])

        load_x, load_w, scaled = sem("a_load_x"), sem("a_load_w"), sem("a_scaled")
        zeroed = sem("a_zeroed")
        state = sb("state", [P, B, G, DV])
        kq = sb("kq", [P, NC, B, 2, NB, G, 2, BK])
        inv_dp = sb("inv_dp", [P, HB, NC, CH])
        mt = sb("mt", [P, HB * NBLK, BK, BK])
        kfull = sb("kfull", [P, 2, G, P])

        with ExitStack() as once:
            wraw = once.enter_context(nc.sbuf_tensor("wraw", [P, 2 * G * P + H * DV], F32))
            wtap = once.enter_context(nc.sbuf_tensor("wtap", [P, TAPS, 2 * G * P + H * DV], F32))
            wb_raw = once.enter_context(nc.sbuf_tensor("wb_raw", [P, H], F32))
            with nc.Block() as block:
                @block.sync
                def _(sp):
                    for b in range(B):
                        sp.dma_start(xT[:, b, LOOK:], d["xT"][:, b, :]).then_inc(load_w, 16)
                    sp.dma_start(wraw[:, 0:G * P], d["WqT"]).then_inc(load_x, 16)
                    sp.dma_start(wraw[:, G * P:2 * G * P], d["WkT"]).then_inc(load_x, 16)
                    sp.dma_start(wraw[:, 2 * G * P:], d["WvT"]).then_inc(load_x, 16)
                    sp.dma_start(wtap[:, :, :], d["taps"].partition_broadcast(P)).then_inc(load_x, 16)
                    for dst, name in ((wa, "WaT"), (wg, "WgT"), (wo, "WoT"), (conv_b, "conv_b"), (bias_a, "ba"),
                                      (ln_w, "ln_w"), (ln_b, "ln_b"), (res, "x_tok")):
                        dst = dst[:, :] if len(dst.shape) == 2 else dst[:, :, :]
                        sp.dma_start(dst, d[name]).then_inc(load_w, 16)
                    sp.dma_start(wb_raw[:, :], d["WbT"]).then_inc(load_x, 16)
                    sp.dma_start(bias_b[:, :], d["bb"].partition_broadcast(P)).then_inc(load_w, 16)
                    sp.wait_ge(load_w, 16 * 11)

                @block.gpsimd
                def _(pool):
                    nc.gpsimd.memset(xT[:, :, 0:LOOK], 0.0)
                    nc.gpsimd.memset(state[:, :, :, :], 0.0)
                    nc.gpsimd.memset(kq[:, :, :, :, :, :, :, :].rearrange("p c b q i g h s -> p (c b q i g h s)"), 0.0)
                    nc.gpsimd.memset(inv_dp[:, :, :, 0:1], 1.0)
                    nc.gpsimd.memset(mt[:, :, :, :], 0.0)
    
                @block.vector
                def _(dve):
                    dve.wait_ge(load_x, 16 * 5)
                    for j in range(TAPS):
                        nc.vector.tensor_tensor(taps[:, j, :], wraw[:, :], wtap[:, j, :], ALU.mult)
                    nc.vector.tensor_copy(wb[:, :, :], wb_raw[:, :].unsqueeze(2).to_broadcast([P, H, P]))

        qk = sb("qk", [P, 2 * G, B, TS])
        vd = sb("vd", [P, H, B, TS])
        aa = sb("aa", [P, H, B, TS])
        dd = sb("dd", [P, HB, NC, CH])
        rr = sb("rr", [P, H, B, TS])
        near = sb("near", [P, G, B, NBLK, 6])
        gn = sb("gn", [P, H, B, NBLK, 6])
        tmp = qk[:, :, :, :].rearrange("p g b (n i) -> p (g b n) i", i=BK).rearrange("p m (i j) -> p m i j", i=2)
        gm = sb("gm", [BK * H, 2, NB - 1, P])
        qkm = sb("qkm", [P, 2, P])
        last = sb("last", [P, 2, H, DK])
        decay = sb("decay", [P, 2, G, P])
        prod = sb("prod", [P, B, H, BK, BK])
        w = sb("w", [P, B, NB, H, BK])
        wtb = sb("wtb", [BK * H, B, P])
        wtf = sb("wtf", [P, B, P])
        gflat = gn[:, :, :, :, :].rearrange("p h b n e -> p (h b n e)")
        grown = gflat[:, 0:B * G * P].rearrange("p (b g v) -> p b g v", b=B, g=G)
        o = vd
        sq = rr[:, :, :, :].rearrange("p h b t -> p (h b t)").rearrange("p (m e) -> p m e", m=4)
        gate = aa
        yT = gflat[:, 0:B * TS].rearrange("p (b t) -> p b t", b=B)

        names = "tile_done tile_kept near_done gn_done gn_kept decays_done pool_done dve_chain act_chain"
        pre = {n: sem("pre_" + n) for n in names.split()}
        two = lambda n: [sem(f"{n}{b}") for b in range(B)]
        z_ready, w_ready, wt_ready, wt_kept = two("z_ready"), two("w_ready"), two("wt_ready"), two("wt_kept")
        p_ready, p_used, s_ready, o_ready, o_kept = (two("p_ready"), two("p_used"), two("s_ready"), two("o_ready"),
                                                     two("o_kept"))
        g_ready, g_kept, q_kept, k_ready, k_kept, f_ready, f_kept = (
            sem(n) for n in ("g_ready", "g_kept", "q_kept", "k_ready", "k_kept", "f_ready", "f_kept"))
        dve_chain, last_done = sem("chain_dve"), sem("last_done")
        post = {n: sem("post_" + n) for n in
                "gate_done gate_kept centred squared var_done std_done normed y_done y_kept yt_done dve_chain pool_done act_chain".split()}
        every = (list(pre.values()) + z_ready + w_ready + wt_ready + wt_kept + p_ready + p_used + s_ready + o_ready
                 + o_kept + [g_ready, g_kept, q_kept, k_ready, k_kept, f_ready, f_kept, dve_chain, last_done]
                 + list(post.values()))

        NQ, NK, NV = G, 2 * G, 2 * G + H
        NTILE = NV + 2 * H

        with nc.Fori(0, NS) as s:
            with nc.Block() as block:
                @block.tensor
                def _(pe):
                    def out(n):
                        return ps[:, n % 8, 0:B * TS].rearrange("p (b t) -> p b t", b=B)

                    for n in range(NTILE):
                        if n >= 8:
                            pe.wait_ge(pre["tile_kept"], n - 7)
                        if n < NV:
                            for j in range(TAPS):
                                mm = pe.matmul(out(n), lhsT=taps[:, j, n * P:(n + 1) * P],
                                               rhs=xT[:, :, bass.ds(s * TS + j, TS)], start=(j == 0), stop=(j == TAPS - 1))
                        else:
                            h = (n - NV) % H
                            lhs = wa[:, h * P:(h + 1) * P] if n < NV + H else wb[:, h, :]
                            mm = pe.matmul(out(n), lhsT=lhs, rhs=xT[:, :, bass.ds(s * TS + LOOK, TS)], start=True, stop=True)
                        mm.then_inc(pre["tile_done"], 1)
                    pe.wait_ge(pre["near_done"], 3)
                    pe.wait_ge(pre["tile_kept"], NTILE)
                    for h in range(H):
                        pe.matmul(ps[:, h, 0:B * NBLK * 6], lhsT=cst["head_sum"][:, h % 2, :],
                                  rhs=near[:, h // 2, :, :, :].rearrange("p b n e -> p (b n e)"), start=True,
                                  stop=True).then_inc(pre["gn_done"], 1)

                @block.scalar
                def _(act):
                    def src(n):
                        return ps[:, n % 8, 0:B * TS].rearrange("p (b t) -> p b t", b=B)

                    for n in range(NTILE):
                        act.wait_ge(pre["tile_done"], n + 1)
                        if n < NK:
                            nc.scalar.activation(qk[:, n, :, :], src(n), ACT.Silu, bias=conv_b[:, n:n + 1]).then_inc(pre["tile_kept"], 1)
                        elif n < NV:
                            nc.scalar.activation(vd[:, n - NK, :, :], src(n), ACT.Silu, bias=conv_b[:, n:n + 1]).then_inc(pre["tile_kept"], 1)
                        elif n < NV + H:
                            h = n - NV
                            nc.scalar.activation(aa[:, h, :, :], src(n), ACT.Sigmoid, bias=bias_a[:, h:h + 1]).then_inc(pre["tile_kept"], 1)
                        else:
                            h = n - NV - H
                            nc.scalar.activation(rr[:, h, :, :], src(n), ACT.Sigmoid, bias=bias_b[:, h:h + 1]).then_inc(pre["tile_kept"], 1)
                    for h in range(H):
                        act.wait_ge(pre["gn_done"], h + 1)
                        nc.scalar.mul(gn[:, h, :, :, :].rearrange("p b n e -> p (b n e)"), ps[:, h, 0:B * NBLK * 6],
                                      1.0 / DK).then_inc(pre["gn_kept"], 1)

                @block.gpsimd
                def _(pool):
                    pool.wait_ge(pre["tile_kept"], NK)
                    kk = qk[:, NQ:NK, :, :].rearrange("p g b (n i) -> p (g b n) i", i=BK)
                    nn = near[:, :, :, :, :].rearrange("p g b n e -> p (g b n) e")
                    nc.gpsimd.tensor_tensor(nn[:, :, 0:3], kk[:, :, 1:4], kk[:, :, 0:3], ALU.mult).then_inc(pre["near_done"], 1)
                    nc.gpsimd.tensor_tensor(nn[:, :, 3:5], kk[:, :, 2:4], kk[:, :, 0:2], ALU.mult).then_inc(pre["near_done"], 1)
                    nc.gpsimd.tensor_tensor(nn[:, :, 5:6], kk[:, :, 3:4], kk[:, :, 0:1], ALU.mult).then_inc(pre["near_done"], 1)
                    for h in range(2):
                        pool.wait_ge(pre["near_done"], 3)
                        if h:
                            pool.wait_ge(pre["pool_done"], 2 * B * G)
                        rows = slice(DK * h, DK * h + DK)
                        for b in range(B):
                            for i, scale in ((1, 1.0), (0, -DK ** -0.5)):
                                for g in range(G):
                                    src = qk[rows, g + (0 if i else G), b, :].rearrange("p (c i s) -> p c i s", i=NB, s=BK)
                                    nc.gpsimd.tensor_scalar(kq[rows, :, b, i, :, g, h, :], src, scale, None,
                                                            ALU.mult).then_inc(pre["pool_done"], 1)

                @block.vector
                def _(dve):
                    ch = Chain(dve, pre["dve_chain"])
                    dve.wait_ge(pre["tile_kept"], NV + H)
                    av = aa[:, :, :, :].rearrange("p h b (c t) -> p (h b) c t", t=CH)
                    ch.step(nc.vector.tensor_copy(dd[:, :, :, 0:1], av[:, :, :, 0:1]))
                    for t in range(1, CH):
                        ch.step(nc.vector.tensor_tensor(dd[:, :, :, t:t + 1], dd[:, :, :, t - 1:t], av[:, :, :, t:t + 1], ALU.mult))
                    nc.vector.reciprocal(aa[:, :, :, :], aa[:, :, :, :])
                    ch.step(nc.vector.reciprocal(inv_dp[:, :, :, 1:CH], dd[:, :, :, 0:CH - 1]))
                    vv = vd[:, :, :, :].rearrange("p h b t -> p (h b t)")
                    nc.vector.tensor_tensor(vv, vv, inv_dp[:, :, :, :].rearrange("p a c t -> p (a c t)"), ALU.mult)
                    dve.wait_ge(pre["tile_kept"], NTILE)
                    ch.step(nc.vector.tensor_tensor(rr[:, :, :, :], rr[:, :, :, :], aa[:, :, :, :], ALU.mult))
                    R = rr[:, :, :, :].rearrange("p h b (n i) -> p (h b n) i", i=BK)
                    N = gn[:, :, :, :, :].rearrange("p h b n e -> p (h b n) e")
                    M = mt[:, :, :, :].rearrange("p n i j -> p n (i j)")
                    dve.wait_ge(pre["gn_kept"], H)
                    nc.vector.tensor_copy(M[:, :, 0:16:5], R)
                    nc.vector.tensor_tensor(N[:, :, 0:3], N[:, :, 0:3], R[:, :, 1:4], ALU.mult)
                    nc.vector.tensor_tensor(N[:, :, 3:5], N[:, :, 3:5], R[:, :, 2:4], ALU.mult)
                    ch.step(nc.vector.tensor_tensor(N[:, :, 5:6], N[:, :, 5:6], R[:, :, 3:4], ALU.mult))
                    ch.step(nc.vector.scalar_tensor_tensor(out=M[:, :, 4:16:5], in0=N[:, :, 0:3], scalar=-1.0, in1=R[:, :, 0:3],
                                                           op0=ALU.mult, op1=ALU.mult))
                    dve.wait_ge(pre["pool_done"], 2 * 2 * B * G)
                    t0, t1 = tmp[:, :, 0, :], tmp[:, :, 1, :]
                    nc.vector.tensor_tensor(t0, N[:, :, 3:5], R[:, :, 0:2], ALU.mult)
                    ch.step(nc.vector.tensor_tensor(t1, N[:, :, 1:3], M[:, :, 4:10:5], ALU.mult))
                    ch.step(nc.vector.scalar_tensor_tensor(out=M[:, :, 8:14:5], in0=t0, scalar=-1.0, in1=t1, op0=ALU.mult,
                                                           op1=ALU.subtract))
                    nc.vector.tensor_tensor(t0[:, :, 0:1], N[:, :, 5:6], R[:, :, 0:1], ALU.mult)
                    nc.vector.tensor_tensor(t0[:, :, 1:2], N[:, :, 4:5], M[:, :, 4:5], ALU.mult)
                    ch.step(nc.vector.tensor_tensor(t1[:, :, 0:1], N[:, :, 2:3], M[:, :, 8:9], ALU.mult))
                    ch.step(nc.vector.tensor_tensor(t1[:, :, 1:2], t0[:, :, 0:1], t0[:, :, 1:2], ALU.add))
                    ch.step(nc.vector.scalar_tensor_tensor(out=M[:, :, 12:13], in0=t1[:, :, 0:1], scalar=-1.0, in1=t1[:, :, 1:2],
                                                           op0=ALU.mult, op1=ALU.subtract))

            vdc = vd[:, :, :, :].rearrange("p h b (c i s) -> p i h b c s", c=NC, s=BK)
            ddc = dd[:, :, :, :].rearrange("p (h b) c (i s) -> p h b c i s", b=B, s=BK)
            oc = o[:, :, :, :].rearrange("p h b (c i s) -> p h b c i s", c=NC, s=BK)
            mtc = mt[:, :, :, :].rearrange("p (h b n) i j -> p h b n i j", h=H, b=B)
            pairs = [(c, b) for c in range(NC) for b in range(B)]

            def kc(c, b, i):
                return kq[:, c, b, i, :, :, :, :].rearrange("p i g h s -> p (i g h s)")

            def z_of(b):
                return ps[:, b, 0:P].rearrange("p (i h s) -> p i h s", i=NB, h=H)

            with nc.Block() as block:
                @block.tensor
                def _(pe):
                    def prepare(n):
                        c, b = pairs[n]
                        k = kc(c, b, 0)
                        if n >= 1:
                            pe.wait_ge(q_kept, n)
                        for i in range(NB - 1):
                            mm = pe.matmul(ps[0:BK * H, 6, i * P:(i + 1) * P], lhsT=k[:, BK * H * i:BK * H * (i + 1)], rhs=k,
                                           start=True, stop=True, skip_group_check=True)
                        pe.matmul(ps[:, 6, 3 * P:4 * P], lhsT=k, rhs=kc(c, b, 1), start=True, stop=True,
                                  skip_group_check=True).then_inc(g_ready, 1)
                        if n >= 1:
                            pe.wait_ge(k_kept, 4 * n)
                        pe.transpose(ps[:, 7, 0:P], k, cst["ident"][:, :]).then_inc(k_ready, 1)
                        if n >= 1:
                            pe.wait_ge(f_kept, n)
                        pe.wait_ge(last_done, n + 1)
                        for g in range(G):
                            mm = pe.matmul(ps[:, 5, g * P:(g + 1) * P], lhsT=last[:, n % 2, 2 * g:2 * g + 2, :].rearrange(
                                "p h k -> p (h k)"), rhs=cst["ident"][:, :], start=True,
                                           stop=True, skip_group_check=True)
                        mm.then_inc(f_ready, 1)

                    def start(n):
                        c, b = pairs[n]
                        if c >= 1:
                            pe.wait_ge(o_kept[b], c)
                        pe.matmul(z_of(b), lhsT=cst["ident"][:, :], rhs=vdc[:, :, :, b, c, :], start=True, stop=False,
                                  skip_group_check=True)
                        if c >= 1:
                            pe.wait_ge(s_ready[b], c)
                        zo = ps[:, b, 0:2 * P].rearrange("p (i g e) -> p i g e", i=2 * NB, g=G)
                        for g in range(G):
                            mm = pe.matmul(zo[:, :, g, :], lhsT=state[:, b, g, :],
                                           rhs=kq[:, c, b, :, :, g, :, :].rearrange("p q i h s -> p (q i) (h s)"), start=False,
                                           stop=(g == G - 1), skip_group_check=True)
                        mm.then_inc(z_ready[b], 1)

                    def turn(n, i):
                        c, b = pairs[n]
                        pe.wait_ge(w_ready[b], NB * c + i + 1)
                        if i < NB - 1:
                            pe.transpose(ps[0:BK * H, 2 + b, 0:P], w[:, b, i, :, :].rearrange("p h s -> p (h s)"),
                                         cst["ident"][:, :]).then_inc(wt_ready[b], 1)
                        else:
                            pe.transpose(ps[:, 2 + b, P:2 * P], w[:, b, :, :, :].rearrange("p i h s -> p (i h s)"),
                                         cst["ident"][:, :]).then_inc(wt_ready[b], 1)

                    def take_off(n, i):
                        c, b = pairs[n]
                        pe.wait_ge(wt_kept[b], NB * c + i + 1)
                        if i == 0:
                            pe.wait_ge(g_kept, n + 1)
                        later = slice(BK * H * (i + 1), P)
                        pe.matmul(ps[:, b, later], lhsT=wtb[:, b, :], rhs=gm[:, n % 2, i, later], start=False, stop=True,
                                  skip_group_check=True).then_inc(z_ready[b], 1)

                    def finish(n):
                        c, b = pairs[n]
                        pe.wait_ge(wt_kept[b], NB * (c + 1))
                        pe.wait_ge(k_kept, 4 * (n + 1))
                        if n >= 1:
                            pc, pb = pairs[n - 1]
                            pe.wait_ge(p_used[pb], pc + 1)
                        for g in range(G):
                            mm = pe.matmul(ps[:, 4, g * P:(g + 1) * P], lhsT=kfull[:, n % 2, g, :], rhs=wtf[:, b, :],
                                           start=True, stop=True, skip_group_check=True)
                        mm.then_inc(p_ready[b], 1)
                        pe.wait_ge(q_kept, n + 1)
                        pe.matmul(ps[:, b, P:2 * P], lhsT=wtf[:, b, :], rhs=qkm[:, n % 2, :], start=False, stop=True,
                                  skip_group_check=True).then_inc(o_ready[b], 1)

                    prepare(0)
                    prepare(1)
                    for c in range(NC):
                        for b in range(B):
                            start(B * c + b)
                        for i in range(NB - 1):
                            for b in range(B):
                                turn(B * c + b, i)
                            for b in range(B):
                                take_off(B * c + b, i)
                        for b in range(B):
                            turn(B * c + b, NB - 1)
                        for b in range(B):
                            finish(B * c + b)
                        for b in range(B):
                            if c + 1 < NC:
                                prepare(B * (c + 1) + b)

                @block.gpsimd
                def _(pool):
                    for n, (c, b) in enumerate(pairs):
                        if n >= 2:
                            pool.wait_ge(f_ready, n - 1)
                        nc.gpsimd.tensor_copy(last[:, n % 2, :, :], ddc[:, :, b, c, NB - 1, BK - 1:BK].to_broadcast(
                            [P, H, DK])).then_inc(last_done, 1)

                @block.scalar
                def _(act):
                    def prepare(n):
                        c, b = pairs[n]
                        act.wait_ge(k_ready, n + 1)
                        if n >= 2:
                            pc, pb = pairs[n - 2]
                            act.wait_ge(p_ready[pb], pc + 1)
                        for g in range(G):
                            nc.scalar.activation(kfull[:, n % 2, g, :], ps[:, 7, 0:P], ACT.Copy,
                                                 scale=cst["pair_rows"][:, g:g + 1]).then_inc(k_kept, 1)
                        act.wait_ge(f_ready, n + 1)
                        if n >= 2:
                            act.wait_ge(s_ready[pb], pc + 1)
                        nc.scalar.copy(decay[:, n % 2, :, :], ps[:, 5, :].rearrange("p (g v) -> p g v", g=G)).then_inc(f_kept, 1)

                    def keep(n, i):
                        c, b = pairs[n]
                        act.wait_ge(wt_ready[b], NB * c + i + 1)
                        if i < NB - 1:
                            nc.scalar.copy(wtb[:, b, :], ps[0:BK * H, 2 + b, 0:P]).then_inc(wt_kept[b], 1)
                        else:
                            if c >= 1:
                                act.wait_ge(o_ready[b], c)
                            nc.scalar.copy(wtf[:, b, :], ps[:, 2 + b, P:2 * P]).then_inc(wt_kept[b], 1)

                    prepare(0)
                    prepare(1)
                    for c in range(NC):
                        for i in range(NB):
                            for b in range(B):
                                keep(B * c + b, i)
                        if c + 1 < NC:
                            for b in range(B):
                                prepare(B * (c + 1) + b)

                @block.vector
                def _(dve):
                    ch = Chain(dve, dve_chain)

                    def prepare(n):
                        c, b = pairs[n]
                        dve.wait_ge(g_ready, n + 1)
                        if n >= 2:
                            pc, pb = pairs[n - 2]
                            dve.wait_ge(o_ready[pb], pc + 1)
                        nc.vector.tensor_tensor(gm[:, n % 2, :, :], ps[0:BK * H, 6, 0:(NB - 1) * P].rearrange(
                            "p (i e) -> p i e", i=NB - 1), cst["same_head"][0:BK * H, :].unsqueeze(1).to_broadcast(
                                [BK * H, NB - 1, P]), ALU.mult).then_inc(g_kept, 1)
                        nc.vector.tensor_tensor(qkm[:, n % 2, :], ps[:, 6, 3 * P:4 * P], cst["causal_head"][:, :],
                                                ALU.mult).then_inc(q_kept, 1)

                    def solve(n, i):
                        c, b = pairs[n]
                        dve.wait_ge(z_ready[b], NB * c + i + 1)
                        zi = z_of(b)[:, i].unsqueeze(2).to_broadcast([P, H, BK, BK])
                        ch.step(nc.vector.tensor_tensor(prod[:, b, :, :, :], zi, mtc[:, :, b, NB * c + i, :, :], ALU.mult))
                        if i == 0 and c >= 1:
                            dve.wait_ge(wt_ready[b], NB * c)
                        nc.vector.tensor_reduce(w[:, b, i, :, :], prod[:, b, :, :, :], axis=AX.X,
                                                op=ALU.add).then_inc(w_ready[b], 1)

                    def update(n):
                        c, b = pairs[n]
                        dve.wait_ge(p_ready[b], c + 1)
                        nc.vector.tensor_tensor(grown[:, b], ps[:, 4, :].rearrange("p (g v) -> p g v", g=G),
                                                state[:, b, :, :], ALU.add).then_inc(p_used[b], 1)
                        dve.wait_ge(p_used[b], c + 1)
                        dve.wait_ge(f_kept, n + 1)
                        nc.vector.tensor_tensor(state[:, b, :, :], grown[:, b], decay[:, n % 2, :, :],
                                                ALU.mult).then_inc(s_ready[b], 1)
                        dve.wait_ge(o_ready[b], c + 1)
                        nc.vector.tensor_tensor(oc[:, :, b, c], ps[:, b, P:2 * P].rearrange("p (i h s) -> p h i s", i=NB, h=H),
                                                ddc[:, :, b, c], ALU.mult).then_inc(o_kept[b], 1)

                    prepare(0)
                    prepare(1)
                    for c in range(NC):
                        for i in range(NB):
                            for b in range(B):
                                solve(B * c + b, i)
                        for b in range(B):
                            update(B * c + b)
                        if c + 1 < NC:
                            for b in range(B):
                                prepare(B * (c + 1) + b)

            with nc.Block() as block:
                of = o[:, :, :, :].rearrange("p h b t -> p (h b t)")
                gf = gate[:, :, :, :].rearrange("p h b t -> p (h b t)")

                @block.tensor
                def _(pe):
                    for h in range(H):
                        if h >= 4:
                            pe.wait_ge(post["gate_kept"], h - 3)
                        pe.matmul(ps[:, 4 + h % 4, 0:B * TS].rearrange("p (b t) -> p b t", b=B), lhsT=wg[:, h * P:(h + 1) * P],
                                  rhs=xT[:, :, bass.ds(s * TS + LOOK, TS)], start=True, stop=True).then_inc(post["gate_done"], 1)
                    for m in range(4):
                        pe.matmul(ps[:, m, :], lhsT=cst["centre"][:, :], rhs=of[:, m * 512:(m + 1) * 512], start=True,
                                  stop=True).then_inc(post["centred"], 1)
                    for m in range(4):
                        pe.wait_ge(post["squared"], m + 1)
                        if m == 0:
                            pe.wait_ge(post["gate_kept"], H)
                        pe.matmul(ps[:, 4 + m, :], lhsT=cst["mean"][:, :], rhs=sq[:, m, :], start=True,
                                  stop=True).then_inc(post["var_done"], 1)
                    pe.wait_ge(post["normed"], 4)
                    for h in range(H):
                        mm = pe.matmul(ps[:, 0, 0:B * TS].rearrange("p (b t) -> p b t", b=B), lhsT=wo[:, h, :],
                                       rhs=o[:, h, :, :], start=(h == 0), stop=(h == H - 1))
                    mm.then_inc(post["y_done"], 1)
                    pe.wait_ge(post["y_kept"], 1)
                    for b in range(B):
                        pe.transpose(ps[:, 1, b * P:(b + 1) * P], yT[:, b, :], cst["ident"][:, :]).then_inc(post["yt_done"], 1)

                @block.scalar
                def _(act):
                    for h in range(H):
                        act.wait_ge(post["gate_done"], h + 1)
                        nc.scalar.activation(gate[:, h, :, :], ps[:, 4 + h % 4, 0:B * TS].rearrange("p (b t) -> p b t", b=B),
                                             ACT.Sigmoid).then_inc(post["gate_kept"], 1)
                    for m in range(4):
                        act.wait_ge(post["centred"], m + 1)
                        nc.scalar.activation(sq[:, m, :], ps[:, m, :], ACT.Square).then_inc(post["squared"], 1)
                    for m in range(4):
                        act.wait_ge(post["var_done"], m + 1)
                        nc.scalar.activation(sq[:, m, :], ps[:, 4 + m, :], ACT.Sqrt, bias=cst["eps"][:, 0:1]).then_inc(post["std_done"], 1)
                    act.wait_ge(post["y_done"], 1)
                    nc.scalar.copy(yT[:, :, :], ps[:, 0, 0:B * TS].rearrange("p (b t) -> p b t", b=B)).then_inc(post["y_kept"], 1)

                @block.vector
                def _(dve):
                    ch = Chain(dve, post["dve_chain"])
                    for m in range(4):
                        part = of[:, m * 512:(m + 1) * 512]
                        dve.wait_ge(post["std_done"], m + 1)
                        ch.step(nc.vector.reciprocal(sq[:, m, :], sq[:, m, :]))
                        ch.step(nc.vector.tensor_tensor(part, ps[:, m, :], sq[:, m, :], ALU.mult))
                        ch.step(nc.vector.tensor_scalar(part, part, ln_w[:, 0:1], ln_b[:, 0:1], ALU.mult, ALU.add))
                        dve.wait_ge(post["gate_kept"], H)
                        nc.vector.tensor_tensor(part, part, gf[:, m * 512:(m + 1) * 512], ALU.mult).then_inc(post["normed"], 1)
                    dve.wait_ge(post["yt_done"], B)
                    rv = res[:, :, :].rearrange("p (b s) c -> p b s c", b=B)
                    nc.vector.tensor_tensor(rv[:, :, bass.ds(s, 1), :], rv[:, :, bass.ds(s, 1), :],
                                            ps[:, 1, 0:B * P].rearrange("p (b o c) -> p b o c", b=B, o=1), ALU.add)
            stage_end(nc, every)


def layer_norm(nc, ctx, cst, ps, res, xT, name):
    with ExitStack() as own:
        def sb(n, shape, dt=F32):
            return own.enter_context(nc.sbuf_tensor(f"{name}_{n}", shape, dt))
        total, mean, var, std = (sb(n, [P, NT]) for n in ("total", "mean", "var", "std"))
        sq = sb("sq", [P, NT, C])
        centred, squared, summed, rooted, done, turned, kept, chain = (
            ctx.enter_context(nc.semaphore(f"{name}_{n}")) for n in
            ("centred", "squared", "summed", "rooted", "done", "turned", "kept", "chain"))
        wide = [P, NT, C]
        with nc.Block() as block:
            @block.vector
            def _(dve):
                ch = Chain(dve, chain)
                ch.step(nc.vector.tensor_reduce(total[:, :], res[:, :, :], axis=AX.X, op=ALU.add))
                ch.step(nc.vector.tensor_scalar(mean[:, :], total[:, :], 1.0 / C, None, ALU.mult))
                nc.vector.tensor_tensor(res[:, :, :], res[:, :, :], mean[:, :].unsqueeze(2).to_broadcast(wide),
                                        ALU.subtract).then_inc(centred, 1)
                dve.wait_ge(squared, 1)
                nc.vector.tensor_reduce(var[:, :], sq[:, :, :], axis=AX.X, op=ALU.add).then_inc(summed, 1)
                dve.wait_ge(rooted, 1)
                ch.step(nc.vector.reciprocal(std[:, :], std[:, :]))
                nc.vector.tensor_tensor(res[:, :, :], res[:, :, :], std[:, :].unsqueeze(2).to_broadcast(wide),
                                        ALU.mult).then_inc(done, 1)

            @block.scalar
            def _(act):
                act.wait_ge(centred, 1)
                nc.scalar.activation(sq[:, :, :], res[:, :, :], ACT.Square).then_inc(squared, 1)
                act.wait_ge(summed, 1)
                nc.scalar.activation(std[:, :], var[:, :], ACT.Sqrt, bias=cst["eps"][:, 0:1], scale=1.0 / C).then_inc(rooted, 1)
                if xT is not None:
                    for n in range(NT // 4):
                        act.wait_ge(turned, n + 1)
                        nc.scalar.copy(xT[:, n * 512:(n + 1) * 512], ps[:, n, :])

            @block.tensor
            def _(pe):
                if xT is not None:
                    pe.wait_ge(done, 1)
                    for n in range(NT):
                        mm = pe.transpose(ps[:, n // 4, (n % 4) * P:(n % 4 + 1) * P], res[:, n, :], cst["ident"][:, :])
                        if n % 4 == 3:
                            mm.then_inc(turned, 1)


NE = 8
TOP = 2


def route(nc, ctx, cst, ps, xT, wr, bias, comb, name):
    with ExitStack() as own:
        def sb(n, shape):
            return own.enter_context(nc.sbuf_tensor(f"{name}_{n}", shape, F32))
        score, shifted, part = sb("score", [P, NT, NE]), sb("shifted", [P, NT, NE]), sb("part", [P, NT, NE])
        above, equal = sb("above", [P, NT, NE, NE]), sb("equal", [P, NT, NE, NE])
        rank, total = sb("rank", [P, NT, NE]), sb("total", [P, NT])
        logits, scored, shift_done, exp_done, chain = (ctx.enter_context(nc.semaphore(f"{name}_{n}")) for n in
                                                       ("logits", "scored", "shift_done", "exp_done", "chain"))
        out = ps[:, 7, 0:NT * NE].rearrange("p (n e) -> p n e", n=NT)
        square = [P, NT, NE, NE]
        with nc.Block() as block:
            @block.tensor
            def _(pe):
                for n in range(NT):
                    mm = pe.matmul(out[:, n, :], lhsT=xT[:, n * P:(n + 1) * P], rhs=wr[:, :], start=True, stop=True,
                                   skip_group_check=True)
                mm.then_inc(logits, 1)

            @block.scalar
            def _(act):
                if bias is None:
                    act.wait_ge(logits, 1)
                    nc.scalar.activation(score[:, :, :], out, ACT.Sigmoid).then_inc(scored, 1)
                else:
                    act.wait_ge(shift_done, 1)
                    nc.scalar.activation(part[:, :, :], shifted[:, :, :], ACT.Exp).then_inc(exp_done, 1)

            @block.vector
            def _(dve):
                ch = Chain(dve, chain)
                if bias is None:
                    dve.wait_ge(scored, 1)
                    value = score
                else:
                    dve.wait_ge(logits, 1)
                    ch.step(nc.vector.tensor_tensor(score[:, :, :], out, bias[:, :].unsqueeze(1).to_broadcast([P, NT, NE]), ALU.add))
                    ch.step(nc.vector.tensor_reduce(total[:, :], score[:, :, :], axis=AX.X, op=ALU.max))
                    nc.vector.tensor_tensor(shifted[:, :, :], score[:, :, :], total[:, :].unsqueeze(2).to_broadcast([P, NT, NE]),
                                            ALU.subtract).then_inc(shift_done, 1)
                    value = part
                other = score[:, :, :].unsqueeze(2).to_broadcast(square)
                mine = score[:, :, :].unsqueeze(3).to_broadcast(square)
                nc.vector.tensor_tensor(above[:, :, :, :], other, mine, ALU.is_gt)
                ch.step(nc.vector.tensor_tensor(equal[:, :, :, :], other, mine, ALU.is_equal))
                ch.step(nc.vector.tensor_tensor(equal[:, :, :, :], equal[:, :, :, :],
                                                cst["lower"][:, :, :].unsqueeze(1).to_broadcast(square), ALU.mult))
                ch.step(nc.vector.tensor_tensor(above[:, :, :, :], above[:, :, :, :], equal[:, :, :, :], ALU.add))
                ch.step(nc.vector.tensor_reduce(rank[:, :, :], above[:, :, :, :], axis=AX.X, op=ALU.add))
                ch.step(nc.vector.tensor_scalar(rank[:, :, :], rank[:, :, :], TOP - 0.5, None, ALU.is_lt))
                if bias is not None:
                    dve.wait_ge(exp_done, 1)
                ch.step(nc.vector.tensor_tensor(comb[:, :, :], rank[:, :, :], value[:, :, :], ALU.mult))
                ch.step(nc.vector.tensor_reduce(total[:, :], comb[:, :, :], axis=AX.X, op=ALU.add))
                if bias is None:
                    ch.step(nc.vector.tensor_scalar(total[:, :], total[:, :], 1e-20, None, ALU.add))
                ch.step(nc.vector.reciprocal(total[:, :], total[:, :]))
                ch.step(nc.vector.tensor_tensor(comb[:, :, :], comb[:, :, :], total[:, :].unsqueeze(2).to_broadcast([P, NT, NE]),
                                                ALU.mult))


def experts(nc, ctx, cst, ps, xT, res, comb, w1, w2, widths, b1, b2, name):
    tiles = [w // P for w in widths]
    first = [sum(tiles[:e]) for e in range(NE + 1)]
    most = max(tiles)
    QT = 4
    with ExitStack() as own:
        def sb(n, shape):
            return own.enter_context(nc.sbuf_tensor(f"{name}_{n}", shape, F32))
        hT = sb("hT", [P, 2, most, 512])
        relu = sb("relu", [P, 2, 512])
        acc = sb("acc", [P, QT, C])
        now = sb("now", [P, QT, NE])
        nowT = sb("nowT", [NE, QT, P])
        sems = {n: ctx.enter_context(nc.semaphore(f"{name}_{n}")) for n in
                "up rect_a rect_v relu_done kept_v down added start turned turned_kept bias_done chain".split()}
        total = first[NE]
        squared = b1 is None
        with nc.Fori(0, NT // QT) as q:
            with nc.Block() as block:
                @block.tensor
                def _(pe):
                    def up(e):
                        for m in range(first[e], first[e + 1]):
                            if m >= 4:
                                if squared:
                                    pe.wait_ge(sems["rect_v"], m - 3)
                                elif m % 2 == 0:
                                    pe.wait_ge(sems["rect_a"], (m - 4) // 2 + 1)
                                else:
                                    pe.wait_ge(sems["rect_v"], (m - 4) // 2 + 1)
                            pe.matmul(ps[:, m % 4, :], lhsT=w1[:, m * P:(m + 1) * P], rhs=xT[:, bass.ts(q, 512)], start=True,
                                      stop=True).then_inc(sems["up"], 1)

                    def down(e):
                        if squared:
                            pe.wait_ge(sems["rect_v"], first[e + 1])
                        else:
                            pe.wait_ge(sems["rect_a"], (first[e + 1] + 1) // 2)
                            pe.wait_ge(sems["rect_v"], first[e + 1] // 2)
                        if e >= 2:
                            pe.wait_ge(sems["added"], QT * (e - 1))
                        for t in range(QT):
                            for j in range(tiles[e]):
                                mm = pe.matmul(ps[:, 4 + e % 2, t * P:(t + 1) * P], lhsT=hT[:, e % 2, j, t * P:(t + 1) * P],
                                               rhs=w2[:, first[e] + j, :], start=(j == 0), stop=(j == tiles[e] - 1),
                                               skip_group_check=True)
                        mm.then_inc(sems["down"], 1)

                    up(0)
                    if not squared:
                        pe.wait_ge(sems["start"], 1)
                        for t in range(QT):
                            mm = pe.transpose(ps[0:NE, 6, t * P:(t + 1) * P], now[:, t, :], cst["ident"][:, :])
                        mm.then_inc(sems["turned"], 1)
                        pe.wait_ge(sems["turned_kept"], 1)
                        for t in range(QT):
                            mm = pe.matmul(ps[:, 7, t * P:(t + 1) * P], lhsT=nowT[:, t, :], rhs=b2[:, :], start=True, stop=True,
                                           skip_group_check=True)
                        mm.then_inc(sems["bias_done"], 1)
                    for e in range(NE):
                        if e + 1 < NE:
                            up(e + 1)
                        down(e)

                def place(e, m):
                    return hT[:, e % 2, m - first[e], :]

                @block.scalar
                def _(act):
                    if not squared:
                        act.wait_ge(sems["turned"], 1)
                        nc.scalar.copy(nowT[:, :, :], ps[0:NE, 6, :].rearrange("p (t e) -> p t e", t=QT)).then_inc(
                            sems["turned_kept"], 1)
                    for e in range(NE):
                        for m in range(first[e], first[e + 1]):
                            if squared:
                                act.wait_ge(sems["up"], m + 1)
                                if m >= 2:
                                    act.wait_ge(sems["rect_v"], m - 1)
                                nc.scalar.activation(relu[:, m % 2, :], ps[:, m % 4, :], ACT.Relu).then_inc(sems["relu_done"], 1)
                            elif m % 2 == 0:
                                act.wait_ge(sems["up"], m + 1)
                                if e >= 2:
                                    act.wait_ge(sems["down"], e - 1)
                                nc.scalar.activation(place(e, m), ps[:, m % 4, :], ACT.Relu, bias=b1[:, m:m + 1]).then_inc(
                                    sems["rect_a"], 1)

                @block.vector
                def _(dve):
                    ch = Chain(dve, sems["chain"])

                    def rectify(e):
                        for m in range(first[e], first[e + 1]):
                            if not squared and m % 2 == 0:
                                continue
                            if e >= 2:
                                dve.wait_ge(sems["down"], e - 1)
                            if squared:
                                dve.wait_ge(sems["relu_done"], m + 1)
                                nc.vector.tensor_tensor(place(e, m), ps[:, m % 4, :], relu[:, m % 2, :], ALU.mult).then_inc(
                                    sems["rect_v"], 1)
                            else:
                                dve.wait_ge(sems["up"], m + 1)
                                nc.vector.tensor_scalar(place(e, m), ps[:, m % 4, :], b1[:, m:m + 1], 0.0, ALU.add,
                                                        ALU.max).then_inc(sems["rect_v"], 1)

                    nc.vector.tensor_copy(now[:, :, :], comb[:, bass.ts(q, QT), :]).then_inc(sems["start"], 1)
                    if squared:
                        ch.step(nc.vector.tensor_copy(acc[:, :, :], res[:, bass.ts(q, QT), :]))
                        dve.wait_ge(sems["start"], 1)
                        rectify(0)
                    else:
                        rectify(0)
                        dve.wait_ge(sems["bias_done"], 1)
                        ch.step(nc.vector.tensor_tensor(acc[:, :, :], res[:, bass.ts(q, QT), :],
                                                        ps[:, 7, :].rearrange("p (t c) -> p t c", t=QT), ALU.add))
                    for e in range(NE):
                        if e + 1 < NE:
                            rectify(e + 1)
                        dve.wait_ge(sems["down"], e + 1)
                        if e >= 1:
                            dve.wait_ge(sems["added"], QT * e)
                        for t in range(QT):
                            nc.vector.scalar_tensor_tensor(out=acc[:, t, :], in0=ps[:, 4 + e % 2, t * P:(t + 1) * P],
                                                           scalar=now[:, t, e:e + 1], in1=acc[:, t, :], op0=ALU.mult,
                                                           op1=ALU.add).then_inc(sems["added"], 1)
                    dve.wait_ge(sems["added"], QT * NE)
                    ch.step(nc.vector.tensor_copy(res[:, bass.ts(q, QT), :], acc[:, :, :]))
            stage_end(nc, list(sems.values()))


AH, AD = 16, 64
NP = AH // 2
TT = T // P


def softmax_attention(nc, ctx, cst, ps, d, xT, res):
    with ExitStack() as own:
        def sb(n, shape, dt=F32):
            return own.enter_context(nc.sbuf_tensor("b_" + n, shape, dt))

        def sem(n):
            return ctx.enter_context(nc.semaphore("b_" + n))

        wq, wkv, wdown, wout = (sb("wq", [P, AH * AD]), sb("wkv", [P, 2 * AH * AD]), sb("wdown", [C, P]),
                                sb("wout", [P, NP, C]))
        latT = sb("latT", [P, B * T])
        yT = sb("yT", [P, NP, B * T])
        pair_w = sb("pair_w", [P, 3, P])
        qT, kT = sb("qT", [P, B * T]), sb("kT", [P, B * T])
        v = sb("v", [P, NT, P])
        prob = sb("prob", [P, 2, T])
        probT = sb("probT", [P, 2, TT, P])
        nmax, total = sb("nmax", [P, 4]), sb("total", [P, 4])
        y = sb("y", [P, 2, P])
        loaded, lat_done = sem("loaded"), sem("lat_done")
        with nc.Block() as block:
            @block.sync
            def _(sp):
                sp.dma_start(wdown[:, :], d["w_kv_down"]).then_inc(loaded, 16)
                sp.dma_start(wq[:, :], d["w_q"]).then_inc(loaded, 16)
                sp.dma_start(wkv[:, :], d["w_kv_up"]).then_inc(loaded, 16)
                sp.dma_start(wout[:, :, :], d["w_out"]).then_inc(loaded, 16)
                sp.wait_ge(loaded, 64)

            @block.tensor
            def _(pe):
                pe.wait_ge(loaded, 64)
                for m in range(4):
                    pe.matmul(ps[:, m, :], lhsT=wdown[:, :], rhs=xT[:, m * 512:(m + 1) * 512], start=True,
                              stop=True).then_inc(lat_done, 1)

            @block.scalar
            def _(act):
                for m in range(4):
                    act.wait_ge(lat_done, m + 1)
                    nc.scalar.copy(latT[:, m * 512:(m + 1) * 512], ps[:, m, :])

        sems = {n: sem(n) for n in "picked proj_done proj_kept s_done max_done exp_done pt_done pt_kept_v pt_kept_a o_done "
                                   "recip_done y_done yt_done yt_kept chain".split()}
        units = [(b, i, h) for b in range(B) for i in range(TT) for h in range(2)]
        U = len(units)

        def tiles(u):
            return units[u][1] + 1

        two_chunks = [sum(tiles(x) > 4 for x in range(u + 1)) for u in range(U)]

        with nc.Fori(0, NP) as hp:
            with nc.Block() as block:
                @block.gpsimd
                def _(pool):
                    nc.gpsimd.tensor_copy(pair_w[:, 0, :], wq[:, bass.ts(hp, P)]).then_inc(sems["picked"], 1)
                    nc.gpsimd.tensor_copy(pair_w[:, 1, :], wkv[:, bass.ts(hp, P)]).then_inc(sems["picked"], 1)
                    nc.gpsimd.tensor_copy(pair_w[:, 2, :], wkv[:, bass.ds(hp * P + AH * AD, P)]).then_inc(sems["picked"], 1)

                @block.tensor
                def _(pe):
                    for m in range(4):
                        pe.wait_ge(sems["picked"], 1)
                        pe.matmul(ps[:, m, :], lhsT=pair_w[:, 0, :], rhs=xT[:, m * 512:(m + 1) * 512], start=True,
                                  stop=True).then_inc(sems["proj_done"], 1)
                    for m in range(4):
                        pe.wait_ge(sems["picked"], 2)
                        pe.matmul(ps[:, 4 + m, :], lhsT=pair_w[:, 1, :], rhs=latT[:, m * 512:(m + 1) * 512], start=True,
                                  stop=True).then_inc(sems["proj_done"], 1)
                    for m in range(4):
                        pe.wait_ge(sems["picked"], 3)
                        pe.wait_ge(sems["proj_kept"], m + 1)
                        for t in range(4):
                            n = 4 * m + t
                            mm = pe.matmul(ps[:, m, t * P:(t + 1) * P], lhsT=latT[:, n * P:(n + 1) * P], rhs=pair_w[:, 2, :],
                                           start=True, stop=True, skip_group_check=True)
                        mm.then_inc(sems["proj_done"], 1)

                    def scores(u):
                        b, i, h = units[u]
                        if u == 0:
                            pe.wait_ge(sems["proj_kept"], 12)
                        if u >= 2:
                            pe.wait_ge(sems["exp_done"], u - 1)
                        rows = slice(AD * h, AD * h + AD)
                        n = tiles(u) * P
                        for c0 in range(0, n, 512):
                            c1 = min(n, c0 + 512)
                            last = c1 == n
                            bank = ps[:, 2 * (u % 2) + c0 // 512, :]
                            mm = pe.matmul(bank[:, 0:c1 - c0], lhsT=qT[rows, b * T + i * P:b * T + (i + 1) * P],
                                           rhs=kT[rows, b * T + c0:b * T + c1], start=True, stop=not last,
                                           skip_group_check=True)
                            if last:
                                mm = pe.matmul(bank[:, c1 - c0 - P:c1 - c0], lhsT=cst["ident16"][:, :],
                                               rhs=cst["above_diag"][:, :], start=False, stop=True, skip_group_check=True)
                        mm.then_inc(sems["s_done"], 1)

                    def turn(u):
                        pe.wait_ge(sems["exp_done"], u + 1)
                        if u >= 1:
                            pe.wait_ge(sems["pt_kept_v"], u)
                        for j in range(tiles(u)):
                            if j == 4 and two_chunks[u] > 1:
                                pe.wait_ge(sems["pt_kept_a"], two_chunks[u] - 1)
                            mm = pe.transpose(ps[:, 4 + j // 4, (j % 4) * P:(j % 4 + 1) * P], prob[:, u % 2, j * P:(j + 1) * P],
                                              cst["ident"][:, :])
                            if j == min(4, tiles(u)) - 1 or j == tiles(u) - 1:
                                mm.then_inc(sems["pt_done"], 1)

                    def values(u):
                        b, i, h = units[u]
                        pe.wait_ge(sems["pt_kept_v"], u + 1)
                        if tiles(u) > 4:
                            pe.wait_ge(sems["pt_kept_a"], two_chunks[u])
                        if u >= 2:
                            pe.wait_ge(sems["y_done"], u - 1)
                            if h == 1 and u >= 3:
                                pe.wait_ge(sems["yt_kept"], (u - 1) // 2)
                        for j in range(tiles(u)):
                            mm = pe.matmul(ps[:, 6 + u % 2, 0:AD], lhsT=probT[:, u % 2, j, :],
                                           rhs=v[:, b * TT + j, AD * h:AD * h + AD], start=(j == 0), stop=(j == tiles(u) - 1),
                                           skip_group_check=True)
                        mm.then_inc(sems["o_done"], 1)

                    def turn_y(u):
                        pe.wait_ge(sems["y_done"], u + 1)
                        pe.transpose(ps[:, 7, P:2 * P], y[:, (u // 2) % 2, :], cst["ident"][:, :]).then_inc(sems["yt_done"], 1)

                    scores(0)
                    for u in range(U + 2):
                        if u + 1 < U:
                            scores(u + 1)
                        if u >= 2 and u % 2 == 1:
                            turn_y(u - 2)
                        if u < U:
                            turn(u)
                        if 1 <= u <= U:
                            values(u - 1)

                @block.scalar
                def _(act):
                    for m in range(4):
                        act.wait_ge(sems["proj_done"], m + 1)
                        nc.scalar.mul(qT[:, m * 512:(m + 1) * 512], ps[:, m, :], AD ** -0.5).then_inc(sems["proj_kept"], 1)
                    for m in range(4):
                        act.wait_ge(sems["proj_done"], m + 5)
                        nc.scalar.copy(kT[:, m * 512:(m + 1) * 512], ps[:, 4 + m, :]).then_inc(sems["proj_kept"], 1)
                    for m in range(4):
                        act.wait_ge(sems["proj_done"], m + 9)
                        nc.scalar.copy(v[:, 4 * m:4 * m + 4, :], ps[:, m, :].rearrange("p (t c) -> p t c", t=4)).then_inc(
                            sems["proj_kept"], 1)

                    def exponent(u):
                        n = tiles(u) * P
                        act.wait_ge(sems["max_done"], u + 1)
                        if u >= 2:
                            act.wait_ge(sems["pt_done"], u - 1 + two_chunks[u - 2])
                            act.wait_ge(sems["recip_done"], u - 1)
                        src = ps[:, 2 * (u % 2):2 * (u % 2) + 2, :].rearrange("p k e -> p (k e)")[:, 0:n]
                        nc.scalar.activation(prob[:, u % 2, 0:n], src, ACT.Exp, bias=nmax[:, u % 4:u % 4 + 1],
                                             accum_out=total[:, u % 4:u % 4 + 1]).then_inc(sems["exp_done"], 1)

                    for u in range(U + 3):
                        if u < U:
                            exponent(u)
                        if 1 <= u <= U and tiles(u - 1) > 4:
                            w = u - 1
                            act.wait_ge(sems["pt_done"], w + 1 + two_chunks[w])
                            if w >= 2:
                                act.wait_ge(sems["o_done"], w - 1)
                            rest = tiles(w) - 4
                            nc.scalar.copy(probT[:, w % 2, 4:tiles(w), :], ps[:, 5, 0:rest * P].rearrange(
                                "p (j t) -> p j t", j=rest)).then_inc(sems["pt_kept_a"], 1)
                        if u >= 3 and u % 2 == 1 and u - 2 < U:
                            w = u - 2
                            b, i, h = units[w]
                            act.wait_ge(sems["yt_done"], w // 2 + 1)
                            nc.scalar.copy(yT[:, bass.ds(hp, 1), b * T + i * P:b * T + (i + 1) * P],
                                           ps[:, 7, P:2 * P].unsqueeze(1)).then_inc(sems["yt_kept"], 1)

                @block.vector
                def _(dve):
                    ch = Chain(dve, sems["chain"])

                    def row_max(u):
                        n = tiles(u) * P
                        dve.wait_ge(sems["s_done"], u + 1)
                        if u >= 4:
                            dve.wait_ge(sems["exp_done"], u - 3)
                        src = ps[:, 2 * (u % 2):2 * (u % 2) + 2, :].rearrange("p k e -> p (k e)")[:, 0:n]
                        nc.vector.tensor_reduce(nmax[:, u % 4:u % 4 + 1], src, axis=AX.X, op=ALU.max, negate=True).then_inc(
                            sems["max_done"], 1)

                    row_max(0)
                    for u in range(U + 1):
                        if u + 1 < U:
                            row_max(u + 1)
                        if u < U:
                            dve.wait_ge(sems["pt_done"], u + 1 + (two_chunks[u - 1] if u else 0))
                            if u >= 2:
                                dve.wait_ge(sems["o_done"], u - 1)
                            k = min(4, tiles(u))
                            nc.vector.tensor_copy(probT[:, u % 2, 0:k, :], ps[:, 4, 0:k * P].rearrange(
                                "p (j t) -> p j t", j=k)).then_inc(sems["pt_kept_v"], 1)
                        if u >= 1:
                            w = u - 1
                            b, i, h = units[w]
                            dve.wait_ge(sems["exp_done"], w + 1)
                            nc.vector.reciprocal(total[:, w % 4:w % 4 + 1], total[:, w % 4:w % 4 + 1]).then_inc(sems["recip_done"], 1)
                            dve.wait_ge(sems["recip_done"], w + 1)
                            dve.wait_ge(sems["o_done"], w + 1)
                            if w >= 4:
                                dve.wait_ge(sems["yt_done"], (w - 4) // 2 + 1)
                            nc.vector.tensor_scalar(y[:, (w // 2) % 2, AD * h:AD * h + AD], ps[:, 6 + w % 2, 0:AD],
                                                    total[:, w % 4:w % 4 + 1], None, ALU.mult).then_inc(sems["y_done"], 1)
            stage_end(nc, list(sems.values()))

        out_done = sem("out_done")
        with nc.Block() as block:
            @block.tensor
            def _(pe):
                for n in range(NT):
                    for m in range(NP):
                        mm = pe.matmul(ps[:, n // 4, (n % 4) * P:(n % 4 + 1) * P], lhsT=yT[:, m, n * P:(n + 1) * P],
                                       rhs=wout[:, m, :], start=(m == 0), stop=(m == NP - 1), skip_group_check=True)
                    if n % 4 == 3:
                        mm.then_inc(out_done, 1)

            @block.vector
            def _(dve):
                for m in range(NT // 4):
                    dve.wait_ge(out_done, m + 1)
                    part = res[:, 4 * m:4 * m + 4, :]
                    nc.vector.tensor_tensor(part, part, ps[:, m, :].rearrange("p (t c) -> p t c", t=4), ALU.add)


F0_WIDTHS = [128] * 4 + [256] * 4
F1_WIDTHS = [512] * NE


def load(nc, ctx, name, pairs):
    loaded = ctx.enter_context(nc.semaphore(name))
    with nc.Block() as block:
        @block.sync
        def _(sp):
            for dst, src in pairs:
                sp.dma_start(dst, src).then_inc(loaded, 16)
            sp.wait_ge(loaded, 16 * len(pairs))


def program(nc, d, out):
    with ExitStack() as ctx:
        def sb(name, shape, dt=F32):
            return ctx.enter_context(nc.sbuf_tensor(name, shape, dt))
        ps = ctx.enter_context(nc.psum_tensor("ps", [P, 8, 512], F32))
        cst = {"ident": sb("ident", [P, P]), "centre": sb("centre", [P, P]), "mean": sb("mean", [P, P]),
               "head_sum": sb("head_sum", [P, 2, P]), "same_head": sb("same_head", [P, P]), "eps": sb("eps", [P, 1]),
               "pair_rows": sb("pair_rows", [P, G]), "lower": sb("lower", [P, NE, NE]),
               "causal_head": sb("causal_head", [P, P]), "above_diag": sb("above_diag", [P, P], BF16),
               "ident16": sb("ident16", [P, P], BF16)}
        res = sb("res", [P, NT, C])
        constants(nc, cst)
        delta_attention(nc, cst, ps, d, res)
        xT = sb("xTn", [C, B * T])
        comb = sb("comb", [P, NT, NE])
        layer_norm(nc, ctx, cst, ps, res, xT, "n0")
        with ExitStack() as own:
            def wsb(name, shape):
                return own.enter_context(nc.sbuf_tensor(name, shape, F32))
            ff = sum(F0_WIDTHS)
            w1, w2, wr = wsb("f0_w1", [C, ff]), wsb("f0_w2", [P, ff // P, C]), wsb("f0_wr", [C, NE])
            load(nc, ctx, "f0_loaded", [(w1[:, :], d["f0_w1"]), (w2[:, :, :], d["f0_w2"]), (wr[:, :], d["f0_wr"])])
            route(nc, ctx, cst, ps, xT, wr, None, comb, "r0")
            experts(nc, ctx, cst, ps, xT, res, comb, w1, w2, F0_WIDTHS, None, None, "f0")
        layer_norm(nc, ctx, cst, ps, res, xT, "n1")
        softmax_attention(nc, ctx, cst, ps, d, xT, res)
        layer_norm(nc, ctx, cst, ps, res, xT, "n2")
        with ExitStack() as own:
            def wsb(name, shape):
                return own.enter_context(nc.sbuf_tensor(name, shape, F32))
            ff = sum(F1_WIDTHS)
            w1, w2, wr = wsb("f1_w1", [C, ff]), wsb("f1_w2", [P, ff // P, C]), wsb("f1_wr", [C, NE])
            b1, b2, br = wsb("f1_b1", [P, ff // P]), wsb("f1_b2", [NE, C]), wsb("f1_br", [P, NE])
            load(nc, ctx, "f1_loaded", [
                (w1[:, :].rearrange("c (e f) -> c e f", e=NE), d["f1_w1"]), (w2[:, :, :], d["f1_w2"]), (wr[:, :], d["f1_wr"]),
                (b1[:, :], d["f1_b1"]), (b2[:, :], d["f1_b2"]), (br[:, :], d["f1_br"].partition_broadcast(P))])
            route(nc, ctx, cst, ps, xT, wr, br, comb, "r1")
            experts(nc, ctx, cst, ps, xT, res, comb, w1, w2, F1_WIDTHS, b1, b2, "f1")
        layer_norm(nc, ctx, cst, ps, res, None, "n3")
        load(nc, ctx, "stored", [(out, res[:, :, :])])


def lay_out(i):
    import numpy as np
    a = {k: np.asarray(v) for k, v in i.items()}
    x = a["L0_attn_x"]
    pre = "L0_attn_"
    chan = lambda v, n: v.reshape(n, P).T
    taps = np.concatenate([a[pre + n + "_w"][:, 0, :] for n in ("qc", "kc", "vc")], 0).T
    rows = lambda w: w.reshape(-1, P, C).transpose(1, 0, 2)
    return {
        "xT": x.transpose(2, 0, 1), "x_tok": x.reshape(NT, P, C).transpose(1, 0, 2),
        "WqT": a[pre + "Wq"].T, "WkT": a[pre + "Wk"].T, "WvT": a[pre + "Wv"].T, "WaT": a[pre + "Wa"].T,
        "WgT": a[pre + "Wg"].T, "WbT": a[pre + "Wb"].T,
        "WoT": a[pre + "Wo"].reshape(C, H, DV).transpose(2, 1, 0), "taps": taps,
        "conv_b": np.concatenate([chan(a[pre + n + "_b"], m) for n, m in (("qc", G), ("kc", G), ("vc", H))], 1),
        "ba": chan(a[pre + "ba"], H), "bb": a[pre + "bb"], "ln_w": a[pre + "ln_w"][:, None], "ln_b": a[pre + "ln_b"][:, None],
        "f0_w1": a["L0_ffn_w1"], "f0_w2": rows(a["L0_ffn_w2"]), "f0_wr": a["L0_ffn_router_w"].T,
        "w_kv_down": a["L1_attn_w_kv_down"], "w_q": a["L1_attn_w_q"], "w_kv_up": a["L1_attn_w_kv_up"],
        "w_out": rows(a["L1_attn_w_out"]),
        "f1_w1": a["L1_ffn_W1"].transpose(1, 0, 2), "f1_w2": rows(a["L1_ffn_W2"]), "f1_wr": a["L1_ffn_W_router"],
        "f1_b1": chan(a["L1_ffn_b1"].reshape(-1), sum(F1_WIDTHS) // P), "f1_b2": a["L1_ffn_b2"], "f1_br": a["L1_ffn_b_router"],
    }


def kernel(**inputs):
    import numpy as np
    import concourse.bacc as bacc
    from concourse.bass_utils import run_bass_kernel_spmd
    nc = bacc.Bacc("TRN2", target_bir_lowering=False, num_devices=1)
    arrays = {"in_" + k: np.ascontiguousarray(v) for k, v in lay_out(inputs).items()}
    d = {k[3:]: nc.dram_tensor(k, v.shape, F32, kind="ExternalInput").ap() for k, v in arrays.items()}
    out = nc.dram_tensor("out", (P, NT, C), F32, kind="ExternalOutput").ap()
    program(nc, d, out)
    r = run_bass_kernel_spmd(nc, [arrays], core_ids=[0])
    return r.results[0]["out"].transpose(1, 0, 2).reshape(B, T, C)
```

```python
from contextlib import ExitStack

import concourse.bass as bass
from concourse import mybir

F32 = mybir.dt.float32
BF16 = mybir.dt.bfloat16
ALU = mybir.AluOpType
ACT = mybir.ActivationFunctionType
AX = mybir.AxisListType

P = 128
B, T, C = 2, 1024, 128
NT = B * T // P
H, DK, DV, TAPS = 8, 64, 128, 4
G = H * DK // P
TS = 64
NS = T // TS
CH = 16
NC = TS // CH
BK = 4
NB = CH // BK
EPS = 1e-5
LOOK = TAPS - 1


class Ring:

    def __init__(self, slots, by_vector):
        self.slots, self.by_vector = slots, by_vector
        self.names = [name for slot in slots for part in slot for name in part]
        self.order = list(dict.fromkeys(name.split(".")[0] for name in self.names))

    def done(self, f, item):
        return f * len(self.order) + self.order.index(item) + 1

    def kept(self, count):
        filled = [self.order[k % len(self.order)] for k in range(count)]
        vector = filled[-1] in self.by_vector
        return vector, sum((item in self.by_vector) == vector for item in filled)


class Chain:

    def __init__(self, engine, semaphore):
        self.engine, self.semaphore, self.count = engine, semaphore, 0

    def step(self, instruction):
        self.count += 1
        instruction.then_inc(self.semaphore, 1)
        self.engine.wait_ge(self.semaphore, self.count)


def stage_end(nc, sems):
    for s in sems:
        nc.gpsimd.sem_clear(s)
    nc.all_engine_barrier()


def constants(nc, cst):
    with nc.semaphore("cst_made") as made, nc.Block() as block:
        @block.gpsimd
        def _(pool):
            ch = Chain(pool, made)
            select = nc.gpsimd.affine_select
            for name, value in (("ident", 1.0), ("centre", 1.0 / P - 1.0)):
                fill = 0.0 if name == "ident" else 1.0 / P
                ch.step(nc.gpsimd.memset(cst[name][:, :], value))
                ch.step(select(out=cst[name][:, :], in_=cst[name][:, :], pattern=[[-1, P]], compare_op=ALU.is_equal,
                               fill=fill, base=0, channel_multiplier=1))
            ch.step(nc.gpsimd.memset(cst["eps"][:, :], EPS))
            ch.step(nc.gpsimd.memset(cst["minus_half"][:, :], -0.5))
            ch.step(nc.gpsimd.memset(cst["mean_col"][:, :], 1.0 / P))
            ch.step(nc.gpsimd.memset(cst["head_sum"][:, :, :], 0.0))
            for h in range(2):
                ch.step(nc.gpsimd.memset(cst["head_sum"][DK * h:DK * h + DK, h, :], 1.0))
            for name in ("same_head", "causal_head"):
                ch.step(nc.gpsimd.memset(cst[name][:, :], -1.0 / DK))
                for i in range(NB):
                    rows = slice(BK * H * i, BK * H * (i + 1))
                    v = cst[name][rows, :].rearrange("p (i h s) -> p i h s", i=NB, h=H)
                    ch.step(select(out=v, in_=v, pattern=[[0, NB], [-BK, H], [0, BK]], compare_op=ALU.is_ge, fill=0.0,
                                   base=0, channel_multiplier=1))
                    ch.step(select(out=v, in_=v, pattern=[[0, NB], [BK, H], [0, BK]], compare_op=ALU.is_ge, fill=0.0,
                                   base=BK - 1, channel_multiplier=-1))
                    if name == "causal_head":
                        if i:
                            ch.step(nc.gpsimd.memset(v[:, 0:i], 0.0))
                        ch.step(select(out=v[:, i], in_=v[:, i], pattern=[[BK, H], [1, BK]], compare_op=ALU.is_ge,
                                       fill=0.0, base=0, channel_multiplier=-1))
            ch.step(nc.gpsimd.memset(cst["pair_rows"][:, :], -1.0 / DK))
            for i in range(NB):
                v = cst["pair_rows"][BK * H * i:BK * H * (i + 1), :]
                ch.step(select(out=v, in_=v, pattern=[[-2 * BK, G]], compare_op=ALU.is_ge, fill=0.0, base=0,
                               channel_multiplier=1))
                ch.step(select(out=v, in_=v, pattern=[[2 * BK, G]], compare_op=ALU.is_ge, fill=0.0, base=2 * BK - 1,
                               channel_multiplier=-1))
            ch.step(nc.gpsimd.memset(cst["above_diag"][:, :], 0.0))
            ch.step(select(out=cst["above_diag"][:, :], in_=cst["above_diag"][:, :], pattern=[[-1, P]],
                           compare_op=ALU.is_ge, fill=-1e30, base=0, channel_multiplier=1))
            ch.step(nc.gpsimd.memset(cst["lower"][:, :, :], 1.0))
            ch.step(select(out=cst["lower"][:, :, :], in_=cst["lower"][:, :, :], pattern=[[1, NE], [-1, NE]],
                           compare_op=ALU.is_gt, fill=0.0, base=0, channel_multiplier=0))
            ch.step(nc.gpsimd.memset(cst["ident16"][:, :], 1.0))
            ch.step(select(out=cst["ident16"][:, :], in_=cst["ident16"][:, :], pattern=[[-1, P]],
                           compare_op=ALU.is_equal, fill=0.0, base=0, channel_multiplier=1))
    return


def delta_attention(nc, cst, ps, d, res):
    with ExitStack() as ctx:
        def sb(name, shape, dt=F32):
            return ctx.enter_context(nc.sbuf_tensor(name, shape, dt))

        def sem(name):
            return ctx.enter_context(nc.semaphore(name))

        HB = H * B
        NBLK = TS // BK
        N = B * TS
        HALF = 4 * N
        PAD = TS
        xT = sb("xT", [P, B, PAD + T + TS])
        taps = sb("taps", [P, TAPS, 2 * G * P + H * DV])
        wa = sb("wa", [P, H * DV])
        wg = sb("wg", [P, H * DV])
        wb = sb("wb", [P, H])
        wo = sb("wo", [P, H, C])
        conv_b = sb("conv_b", [P, 2 * G + H])
        bias_a = sb("bias_a", [P, 3, H])
        bias_b = sb("bias_b", [P, 2, H])
        ln_w = sb("ln_w", [P, 1])
        ln_b = sb("ln_b", [P, 1])
        state = sb("state", [P, B, G, DV])
        kq = sb("kq", [P, 2, B, NC, 2, NB, G, 2, BK])
        mt = sb("mt", [P, 2, HB * NBLK, BK, BK])
        load_x, load_w, load_b = sem("a_load_x"), sem("a_load_w"), sem("a_load_b")
        load_tap = [sem(f"a_load_tap{j}") for j in range(TAPS)]

        with ExitStack() as once:
            wraw = once.enter_context(nc.sbuf_tensor("wraw", [P, 2 * G * P + H * DV], F32))
            wtap = once.enter_context(nc.sbuf_tensor("wtap", [P, TAPS, 2 * G * P + H * DV], F32))
            with nc.Block() as block:
                @block.sync
                def _(sp):
                    for lo, hi, name in ((0, G * P, "WqT"), (G * P, 2 * G * P, "WkT"), (2 * G * P, 2 * G * P + H * DV, "WvT")):
                        sp.dma_start(wraw[:, lo:hi], d[name]).then_inc(load_x, 16)
                    for j in range(TAPS):
                        sp.dma_start(wtap[:, j, :], d["taps"][j, :].partition_broadcast(P)).then_inc(load_tap[j], 16)
                    for dst, src in ((wb[:, :], d["WbT"]), (bias_a[:, 0, :], d["ba"]),
                                     (bias_b[:, 0, :], d["bb"].partition_broadcast(P)), (wo[:, :, :], d["WoT"])):
                        sp.dma_start(dst, src).then_inc(load_b, 16)
                    for b in range(B):
                        sp.dma_start(xT[:, b, PAD:PAD + T], d["xT"][:, b, :]).then_inc(load_w, 16)
                    for dst, src in ((wa[:, :], d["WaT"]), (wg[:, :], d["WgT"]), (conv_b[:, :], d["conv_b"]),
                                     (ln_w[:, :], d["ln_w"]), (ln_b[:, :], d["ln_b"]), (res[:, 1:, :], d["x_tok"])):
                        sp.dma_start(dst, src).then_inc(load_w, 16)
                    sp.wait_ge(load_w, 16 * 8)

                @block.gpsimd
                def _(pool):
                    nc.gpsimd.memset(xT[:, :, 0:PAD], 0.0)
                    nc.gpsimd.memset(xT[:, :, PAD + T:], 0.0)
                    nc.gpsimd.memset(res[:, 0, :], 0.0)
                    nc.gpsimd.memset(state[:, :, :, :], 0.0)
                    nc.gpsimd.memset(kq[:, :, :, :, :, :, :, :, :].rearrange("p f b c q i g h s -> p (f b c q i g h s)"), 0.0)
                    nc.gpsimd.memset(mt[:, :, :, :, :], 0.0)

                @block.vector
                def _(dve):
                    dve.wait_ge(load_x, 16 * 3)
                    for j in range(TAPS):
                        dve.wait_ge(load_tap[j], 16)
                        nc.vector.tensor_tensor(taps[:, j, :], wraw[:, :], wtap[:, j, :], ALU.mult)
                    dve.wait_ge(load_b, 16 * 4)
                    nc.vector.tensor_scalar(bias_a[:, 1, :], bias_a[:, 0, :], 0.5, None, ALU.mult)
                    nc.vector.tensor_scalar(bias_a[:, 2, :], bias_a[:, 0, :], -1.0, None, ALU.mult)
                    nc.vector.tensor_scalar(bias_b[:, 1, :], bias_b[:, 0, :], 0.5, None, ALU.mult)
                    nc.vector.tensor_scalar(wo[:, :, :], wo[:, :, :], 0.5, None, ALU.mult)

        qk = sb("qk", [P, 2 * G, B, TS])
        vd = sb("vd", [P, 2, H, B, TS])
        th = sb("th", [P, H, B, TS])
        ex = sb("ex", [P, H, B, TS])
        di = sb("di", [P, 3, HB * NC, CH])
        rr = sb("rr", [P, H, B, TS])
        near = sb("near", [P, G, B, NBLK, 6])
        gn = sb("gn", [P, H, B, NBLK, 6])
        tmp = qk[:, :, :, :].rearrange("p g b (n i) -> p (g b n) i", i=BK).rearrange("p m (i j) -> p m i j", i=2)
        gm = sb("gm", [BK * H, 4, NB - 1, P])
        qkm = sb("qkm", [P, 4, P])
        kfull = sb("kfull", [P, 4, G, P])
        last = sb("last", [P, 2, H, DK])
        decay = sb("decay", [P, 4, G, P])
        prod = sb("prod", [P, B, H, BK, BK])
        w = sb("w", [P, B, NB, H, BK])
        wtb = sb("wtb", [BK * H, B, P])
        wtf = sb("wtf", [P, B, P])
        o = vd
        gate = sb("gate", [P, H * N])
        cs = sb("cs", [P, H * N])
        sq = gn[:, :, :, :, :].rearrange("p h b n e -> p (h b n e)")[:, 0:H * N]
        var = sb("var", [P, H])
        rstd = sb("rstd", [P, H])
        yT = sb("yT", [C, N])

        names = ("ring_done ring_act ring_dve near_done copied m_done normed rstd_done gated final_chain "
                 "prepared a_made d_done g_ready g_kept q_kept k_ready k_kept f_ready f_kept last_done")
        S = {n: sem("a_" + n) for n in names.split()}
        two = lambda n: [sem(f"a_{n}{b}") for b in range(B)]
        z_ready, w_ready, wt_ready, wt_kept = two("z_ready"), two("w_ready"), two("wt_ready"), two("wt_kept")
        p_ready, p_used, s_ready, o_ready, o_kept = (two("p_ready"), two("p_used"), two("s_ready"), two("o_ready"),
                                                     two("o_kept"))
        dve_chain, pool_chain = sem("a_dve_chain"), sem("a_pool_chain")
        every = list(S.values()) + [dve_chain, pool_chain]
        for pair in (z_ready, w_ready, wt_ready, wt_kept, p_ready, p_used, s_ready, o_ready, o_kept):
            every += pair

        BY_DVE = ("rs0", "rs1", "yt")
        BOTH = [[["a0"], ["g0"]], [["a1"], ["g1"]], [["a2"], ["b0", "b1"]], [["a3"], ["b2", "b3"]],
                [["c0"], ["c1"]], [["k0.0"], ["k0.1"]], [["k1.0"], ["k1.1", "var"]], [["q0.0"], ["q0.1"]],
                [["q1.0"], ["q1.1", "rs0"]], [["rs1"], ["n0", "n1"]], [["n2"], ["n3", "v0.0"]], [["v0.1"], ["v1.0"]],
                [["v1.1"], ["v2.0"]], [["v2.1"], ["v3.0"]], [["v3.1"], ["wo.0"]], [["wo.1"], ["yt"]]]
        POST = ("g0", "g1", "c0", "c1", "var", "rs0", "rs1", "wo", "yt")
        both = Ring(BOTH, BY_DVE)
        only_pre = Ring([[[x for x in part if x.split(".")[0] not in POST] for part in slot] for slot in BOTH], BY_DVE)
        only_post = Ring([[[x for x in part if x.split(".")[0] in POST] for part in slot] for slot in BOTH], BY_DVE)

        def columns(n):
            return PAD + n * TS

        def bank(ring, f, item):
            return ps[:, 6 + (ring.done(f, item) - 1) % 2, :]

        def pe_item(pe, ring, f, nx, name, at_next, at_last):
            item, _, half = name.partition(".")
            r = ring.done(f, item)
            out = bank(ring, f, item)
            if r > 2 and half != "1":
                vector, count = ring.kept(r - 2)
                pe.wait_ge(S["ring_dve" if vector else "ring_act"], count)
            kind, j = item[0], item[-1]
            if item == "var":
                for h in range(H):
                    if h == 0:
                        vector, count = ring.kept(ring.done(f, "c1"))
                        pe.wait_ge(S["ring_act"], count)
                    mm = pe.matmul(out[:, h:h + 1], lhsT=sq[:, h * N:(h + 1) * N], rhs=cst["mean_col"][:, :], start=True,
                                   stop=True, skip_group_check=True)
            elif kind == "r":
                pe.wait_ge(S["rstd_done"], f + 1)
                for u in range(4):
                    h = 4 * int(j) + u
                    mm = pe.transpose(out[:, u * P:(u + 1) * P], rstd[:, h:h + 1].to_broadcast([P, P]), cst["ident"][:, :])
            elif item == "wo":
                pe.wait_ge(S["gated"], 2 * f + 2)
                for h in {"": range(H), "0": range(H // 2), "1": range(H // 2, H)}[half]:
                    mm = pe.matmul(out[:, 0:N], lhsT=wo[:, h, :], rhs=cs[:, h * N:(h + 1) * N], start=(h == 0), stop=(h == H - 1))
            elif item == "yt":
                vector, count = ring.kept(ring.done(f, "wo"))
                pe.wait_ge(S["ring_act"], count)
                mm = pe.transpose(out[:, 0:P], yT[:, :], cst["ident"][:, :])
            elif kind == "g":
                x = xT[:, :, bass.ds(columns(at_last), TS)]
                for u in range(4):
                    h = 4 * int(j) + u
                    mm = pe.matmul(out[:, u * N:(u + 1) * N].rearrange("p (b t) -> p b t", b=B), lhsT=wg[:, h * P:(h + 1) * P],
                                   rhs=x, start=True, stop=True, skip_group_check=True)
            elif kind == "c":
                of = o[:, nx, :, :, :].rearrange("p h b t -> p (h b t)")
                mm = pe.matmul(out, lhsT=cst["centre"][:, :], rhs=of[:, int(j) * HALF:(int(j) + 1) * HALF], start=True, stop=True)
            elif kind == "n":
                if j == "0":
                    pe.wait_ge(S["near_done"], 3 * (f + 1))
                for u in range(2):
                    h = 2 * int(j) + u
                    mm = pe.matmul(out[:, u * B * NBLK * 6:(u + 1) * B * NBLK * 6], lhsT=cst["head_sum"][:, h % 2, :],
                                   rhs=near[:, h // 2, :, :, :].rearrange("p b n e -> p (b n e)"), start=True, stop=True,
                                   skip_group_check=True)
            else:
                for u in range(2) if half == "" else [int(half)]:
                    part = out[:, u * N:(u + 1) * N].rearrange("p (b t) -> p b t", b=B)
                    t = 2 * int(j) + u
                    if kind in "qkv":
                        t += {"q": 0, "k": G, "v": 2 * G}[kind]
                        for tap in range(TAPS):
                            mm = pe.matmul(part, lhsT=taps[:, tap, t * P:(t + 1) * P],
                                           rhs=xT[:, :, bass.ds(columns(at_next) - LOOK + tap, TS)], start=(tap == 0),
                                           stop=(tap == TAPS - 1), skip_group_check=True)
                    else:
                        lhs = wa[:, t * P:(t + 1) * P] if kind == "a" else wb[:, t:t + 1].to_broadcast([P, P])
                        mm = pe.matmul(part, lhsT=lhs, rhs=xT[:, :, bass.ds(columns(at_next), TS)], start=True, stop=True,
                                       skip_group_check=True)
            if half != "0":
                mm.then_inc(S["ring_done"], 1)

        def act_item(act, ring, f, nx, name):
            item, _, half = name.partition(".")
            if item in BY_DVE or half == "0":
                return
            act.wait_ge(S["ring_done"], ring.done(f, item))
            out = bank(ring, f, item)
            kind, j = item[0], item[-1]
            run = nc.scalar.activation
            if item == "var":
                last_one = nc.scalar.copy(var[:, :], out[:, 0:H])
            elif item == "wo":
                last_one = nc.scalar.copy(yT[:, :], out[:, 0:N])
            elif kind == "g":
                if f >= 1 and j == "0":
                    act.wait_ge(S["gated"], 2 * f)
                last_one = run(gate[:, int(j) * HALF:(int(j) + 1) * HALF], out, ACT.Tanh, scale=0.5)
            elif kind == "c":
                part = slice(int(j) * HALF, (int(j) + 1) * HALF)
                nc.scalar.copy(cs[:, part], out)
                last_one = run(sq[:, part], out, ACT.Square)
            elif kind == "n":
                size = B * NBLK * 6
                last_one = nc.scalar.mul(gn[:, 2 * int(j):2 * int(j) + 2, :, :, :].rearrange("p h b n e -> p (h b n e)"),
                                         out[:, 0:2 * size], 1.0 / DK)
            else:
                if item == "k0" and f >= 1:
                    act.wait_ge(S["copied"], 16 * f)
                if item == "a0" and f >= 1:
                    act.wait_ge(S["m_done"], f)
                for u in range(2):
                    part = out[:, u * N:(u + 1) * N].rearrange("p (b t) -> p b t", b=B)
                    t = 2 * int(j) + u
                    if kind == "q":
                        last_one = run(qk[:, t, :, :], part, ACT.Silu, bias=conv_b[:, t:t + 1])
                    elif kind == "k":
                        last_one = run(qk[:, G + t, :, :], part, ACT.Silu, bias=conv_b[:, G + t:G + t + 1])
                    elif kind == "v":
                        last_one = run(vd[:, nx, t, :, :], part, ACT.Silu, bias=conv_b[:, 2 * G + t:2 * G + t + 1])
                    elif kind == "b":
                        last_one = run(rr[:, t, :, :], part, ACT.Tanh, bias=bias_b[:, 1, t:t + 1], scale=0.5)
                    else:
                        run(th[:, t, :, :], part, ACT.Tanh, bias=bias_a[:, 1, t:t + 1], scale=0.5)
                        last_one = run(ex[:, t, :, :], part, ACT.Exp, bias=bias_a[:, 2, t:t + 1], scale=-1.0)
            last_one.then_inc(S["ring_act"], 1)

        flat = lambda x: x[:, :, :, :].rearrange("p h b t -> p (h b t)")

        def wait_kept(engine, ring, f, item):
            vector, count = ring.kept(ring.done(f, item))
            engine.wait_ge(S["ring_dve" if vector else "ring_act"], count)

        def dve_slot(dve, ch, ring, f, nx, slot, at_last):
            have = ring.order
            if slot == 9 and "rs0" in have:
                for j in range(2):
                    part = slice(j * HALF, (j + 1) * HALF)
                    dve.wait_ge(S["ring_done"], ring.done(f, f"rs{j}"))
                    nc.vector.tensor_tensor(cs[:, part], cs[:, part], bank(ring, f, f"rs{j}"), ALU.mult).then_inc(S["ring_dve"], 1)
            if slot == 10 and "rs0" in have:
                wait_kept(dve, ring, f, "rs1")
                nc.vector.tensor_scalar(cs[:, :], cs[:, :], ln_w[:, 0:1], ln_b[:, 0:1], ALU.mult, ALU.add).then_inc(S["normed"], 1)
            if "k0" in have and (slot != 15 or ring is only_pre):
                prepare_slot(dve, ch, ring, f, nx, slot)
            if slot == 15 and "yt" in have:
                dve.wait_ge(S["ring_done"], ring.done(f, "yt"))
                tile = res[:, bass.ds(at_last + 1, 1), :]
                nc.vector.tensor_tensor(tile, tile, bank(ring, f, "yt")[:, 0:P].unsqueeze(1), ALU.add).then_inc(S["ring_dve"], 1)

        def prepare_slot(dve, ch, ring, f, nx, slot):
            D, inv = di[:, 2 * nx, :, :], di[:, 1, :, :]
            both_d = di[:, nx:nx + 2, :, :]
            R = rr[:, :, :, :].rearrange("p h b (n i) -> p (h b n) i", i=BK)
            NN = gn[:, :, :, :, :].rearrange("p h b n e -> p (h b n) e")
            M = mt[:, nx, :, :, :].rearrange("p n i j -> p n (i j)")
            t0, t1 = tmp[:, :, 0, :], tmp[:, :, 1, :]
            tt, ts = nc.vector.tensor_tensor, nc.vector.tensor_scalar
            Df, invf = (x.rearrange("p n t -> p (n t)") for x in (D, inv))
            if slot == 4:
                wait_kept(dve, ring, f, "a3")
                ts(flat(th), flat(th), 0.5, 0.5, ALU.mult, ALU.add)
                ch.step(ts(invf, flat(ex), 1.0, None, ALU.add))
            if slot == 5:
                ch.step(tt(Df, flat(th), invf, ALU.mult))
                ch.step(ts(Df, Df, -1.0, 2.0, ALU.mult, ALU.add))
                tt(Df, Df, flat(th), ALU.mult).then_inc(S["a_made"], 1)
            if slot == 10:
                wait_kept(dve, ring, f, "b3")
                ch.step(ts(flat(rr), flat(rr), 0.5, 0.5, ALU.mult, ALU.add))
                ch.step(nc.vector.scalar_tensor_tensor(out=flat(rr), in0=flat(ex), scalar=1.0, in1=flat(rr), op0=ALU.add,
                                                       op1=ALU.mult))
            if slot == 11:
                wait_kept(dve, ring, f, "n3")
                nc.vector.tensor_copy(M[:, :, 0:16:5], R)
                ch.step(tt(NN[:, :, 0:3], NN[:, :, 0:3], R[:, :, 1:4], ALU.mult))
            if slot == 12:
                tt(NN[:, :, 3:5], NN[:, :, 3:5], R[:, :, 2:4], ALU.mult)
                ch.step(tt(NN[:, :, 5:6], NN[:, :, 5:6], R[:, :, 3:4], ALU.mult))
                ch.step(nc.vector.scalar_tensor_tensor(out=M[:, :, 4:16:5], in0=NN[:, :, 0:3], scalar=-1.0, in1=R[:, :, 0:3],
                                                       op0=ALU.mult, op1=ALU.mult))
            if slot == 13:
                dve.wait_ge(S["copied"], 16 * (f + 1))
                tt(t0, NN[:, :, 3:5], R[:, :, 0:2], ALU.mult)
                ch.step(tt(t1, NN[:, :, 1:3], M[:, :, 4:10:5], ALU.mult))
                ch.step(nc.vector.scalar_tensor_tensor(out=M[:, :, 8:14:5], in0=t0, scalar=-1.0, in1=t1, op0=ALU.mult,
                                                       op1=ALU.subtract))
            if slot == 14:
                tt(t0[:, :, 0:1], NN[:, :, 5:6], R[:, :, 0:1], ALU.mult)
                tt(t0[:, :, 1:2], NN[:, :, 4:5], M[:, :, 4:5], ALU.mult)
                ch.step(tt(t1[:, :, 0:1], NN[:, :, 2:3], M[:, :, 8:9], ALU.mult))
                ch.step(tt(t1[:, :, 1:2], t0[:, :, 0:1], t0[:, :, 1:2], ALU.add))
                nc.vector.scalar_tensor_tensor(out=M[:, :, 12:13], in0=t1[:, :, 0:1], scalar=-1.0, in1=t1[:, :, 1:2],
                                               op0=ALU.mult, op1=ALU.subtract).then_inc(S["m_done"], 1)
            if slot == 15:
                wait_kept(dve, ring, f, "v3")
                dve.wait_ge(S["d_done"], f + 1)
                vv = vd[:, nx, :, :, :].rearrange("p h b (c t) -> p (h b c) t", t=CH)
                tt(vv[:, :, 1:CH], vv[:, :, 1:CH], inv[:, :, 0:CH - 1], ALU.mult).then_inc(S["prepared"], 1)

        def pool_prepare(pool, ring, f, nx, part, ends_before=0):
            if part == "near":
                wait_kept(pool, ring, f, "k1")
                if f >= 1:
                    pool.wait_ge(S["ring_done"], ring.done(f - 1, "n3"))
                kk = qk[:, G:2 * G, :, :].rearrange("p g b (n i) -> p (g b n) i", i=BK)
                nn = near[:, :, :, :, :].rearrange("p g b n e -> p (g b n) e")
                for lo, hi, dist in ((0, 3, 1), (3, 5, 2), (5, 6, 3)):
                    nc.gpsimd.tensor_tensor(nn[:, :, lo:hi], kk[:, :, dist:BK], kk[:, :, 0:BK - dist], ALU.mult).then_inc(
                        S["near_done"], 1)
                return
            h = part
            wait_kept(pool, ring, f, "q1")
            pool.wait_ge(S["near_done"], 3 * (f + 1))
            if ends_before:
                pool.wait_ge(S["last_done"], ends_before)
                pool.wait_ge(S["rstd_done"], f + 1)
            if h:
                pool.wait_ge(S["copied"], 16 * f + 8)
            rows = slice(DK * h, DK * h + DK)
            for i in range(2):
                for g in range(G):
                    src = qk[rows, g + (0 if i else G), :, :].rearrange("p b (c i s) -> p (b c) i s", i=NB, s=BK)
                    dst = kq[rows, nx, :, :, i, :, g, h, :].rearrange("p b c i s -> p (b c) i s")
                    nc.gpsimd.tensor_copy(dst, src).then_inc(S["copied"], 1)
            if h:
                pool.wait_ge(S["copied"], 16 * (f + 1))

        def pool_scan(pool, ch, f, nx):
            both_d = di[:, nx:nx + 2, :, :]
            pool.wait_ge(S["a_made"], f + 1)
            for t in range(1, CH):
                step = nc.gpsimd.tensor_tensor(both_d[:, :, :, t:t + 1], both_d[:, :, :, t - 1:t], both_d[:, :, :, t:t + 1], ALU.mult)
                if t < CH - 1:
                    ch.step(step)
            step.then_inc(S["d_done"], 1)

        def pool_rstd(pool, ch, ring, f):
            wait_kept(pool, ring, f, "var")
            ch.step(nc.gpsimd.tensor_scalar(rstd[:, :], var[:, :], EPS / DK, None, ALU.add))
            nc.gpsimd.tensor_tensor(rstd[:, :], rstd[:, :], cst["minus_half"][:, :], ALU.pow).then_inc(S["rstd_done"], 1)

        def pool_gate(pool, ch, ring, f):
            pool.wait_ge(S["normed"], f + 1)
            ch.step(nc.gpsimd.tensor_scalar(gate[:, :], gate[:, :], 1.0, None, ALU.add))
            for j in range(2):
                part = slice(j * HALF, (j + 1) * HALF)
                nc.gpsimd.tensor_tensor(cs[:, part], cs[:, part], gate[:, part], ALU.mult).then_inc(S["gated"], 1)

        with nc.Block() as block:
            @block.tensor
            def _(pe):
                for item in only_pre.names:
                    pe_item(pe, only_pre, 0, 0, item, 0, 0)

            @block.scalar
            def _(act):
                for item in only_pre.order:
                    act_item(act, only_pre, 0, 0, item)

            @block.gpsimd
            def _(pool):
                nc.gpsimd.memset(o[:, 1, :, :, :], 0.0)
                pool_scan(pool, Chain(pool, pool_chain), 0, 0)
                pool_prepare(pool, only_pre, 0, 0, "near")
                pool_prepare(pool, only_pre, 0, 0, 0)
                pool_prepare(pool, only_pre, 0, 0, 1)

            @block.vector
            def _(dve):
                ch = Chain(dve, dve_chain)
                for slot in range(16):
                    dve_slot(dve, ch, only_pre, 0, 0, slot, 0)
        stage_end(nc, every)

        def halves(cc):
            return cc // NC % 2, cc % NC

        def kc(cc, b, i):
            f, c = halves(cc)
            return kq[:, f, b, c, i, :, :, :, :].rearrange("p i g h s -> p (i g h s)")

        def dd_of(f):
            return di[:, 2 * f, :, :].rearrange("p (h b c) (i s) -> p h b c i s", h=H, b=B, s=BK)

        def nth(cc, b, base=B):
            return B * cc + b - base

        def pe_products(pe, cc, b, base=B):
            n, k = nth(cc, b, base), kc(cc, b, 0)
            if cc and cc % NC == 0:
                pe.wait_ge(S["copied"], 16 * (cc // NC))
            if n >= 1:
                pe.wait_ge(S["k_kept"], 4 * n)
            for i in range(NB - 1):
                lo = BK * H * (i + 1)
                pe.matmul(ps[0:BK * H, 5, GM_AT[i]:GM_AT[i] + P - lo], lhsT=k[:, BK * H * i:lo], rhs=k[:, lo:P],
                          start=True, stop=True, skip_group_check=True)
            pe.matmul(ps[:, 5, QK_AT:QK_AT + P], lhsT=k, rhs=kc(cc, b, 1), start=True, stop=True, skip_group_check=True)
            pe.transpose(ps[:, 5, KT_AT:KT_AT + P], k, cst["ident"][:, :]).then_inc(S["g_ready"], 1)

        def pe_decays(pe, cc, b, base=B, finished=(0, 0)):
            n = nth(cc, b, base)
            if n >= 1:
                pe.wait_ge(S["f_kept"], n)
            for bb in range(B):
                if finished[bb]:
                    pe.wait_ge(p_used[bb], finished[bb])
            pe.wait_ge(S["last_done"], n + 1)
            for g in range(G):
                mm = pe.transpose(ps[:, 4, g * P:(g + 1) * P], last[:, b, 2 * g:2 * g + 2, :].rearrange("p h k -> p (h k)"),
                                  cst["ident"][:, :])
            mm.then_inc(S["f_ready"], 1)

        def pool_ends(pool, cc, base=B):
            f, c = halves(cc)
            for b in range(B):
                n = nth(cc, b, base)
                if n >= 2:
                    pool.wait_ge(S["f_ready"], n - 1)
                if cc and c == 0:
                    pool.wait_ge(S["d_done"], cc // NC)
                nc.gpsimd.tensor_copy(last[:, b, :, :], dd_of(f)[:, :, b, c, NB - 1, BK - 1:BK].to_broadcast(
                    [P, H, DK])).then_inc(S["last_done"], 1)

        def act_k_rows(act, cc, b, pairs, base=B):
            n = nth(cc, b, base)
            if 0 in pairs:
                act.wait_ge(S["g_ready"], n + 1)
                act.wait_ge(S["q_kept"], n + 1)
                if cc >= 2:
                    act.wait_ge(p_ready[b], cc - 1)
            for g in pairs:
                nc.scalar.activation(kfull[:, B * (cc % 2) + b, g, :], ps[:, 5, KT_AT:KT_AT + P], ACT.Copy,
                                     scale=cst["pair_rows"][:, g:g + 1]).then_inc(S["k_kept"], 1)

        def act_decays(act, cc, b, base=B):
            n = nth(cc, b, base)
            act.wait_ge(S["f_ready"], n + 1)
            if cc >= 2:
                act.wait_ge(s_ready[b], cc - 1)
            nc.scalar.copy(decay[:, B * (cc % 2) + b, :, :], ps[:, 4, :].rearrange("p (g v) -> p g v", g=G)).then_inc(
                S["f_kept"], 1)

        def dve_masks(dve, cc, b, base=B):
            n = nth(cc, b, base)
            dve.wait_ge(S["g_ready"], n + 1)
            for i in range(NB - 1):
                lo = BK * H * (i + 1)
                mm = nc.vector.tensor_tensor(gm[:, B * (cc % 2) + b, i, lo:P], ps[0:BK * H, 5, GM_AT[i]:GM_AT[i] + P - lo],
                                             cst["same_head"][0:BK * H, lo:P], ALU.mult)
            mm.then_inc(S["g_kept"], 1)
            nc.vector.tensor_tensor(qkm[:, B * (cc % 2) + b, :], ps[:, 5, QK_AT:QK_AT + P], cst["causal_head"][:, :],
                                    ALU.mult).then_inc(S["q_kept"], 1)

        GM_AT = [0, 96, 160]
        QK_AT, KT_AT = 192, 320
        with nc.Block() as block:
            @block.tensor
            def _(pe):
                for b in range(B):
                    pe_products(pe, 0, b, 0)
                    pe_decays(pe, 0, b, 0)

            @block.gpsimd
            def _(pool):
                pool_ends(pool, 0, 0)

            @block.scalar
            def _(act):
                for b in range(B):
                    act_k_rows(act, 0, b, range(G), 0)
                    act_decays(act, 0, b, 0)

            @block.vector
            def _(dve):
                for b in range(B):
                    dve_masks(dve, 0, b, 0)
        stage_end(nc, every)

        with nc.Fori(0, NS // 2) as it:
            chunks = [(f, c) for f in range(2) for c in range(NC)]

            def z_of(b):
                return ps[:, b, 0:P].rearrange("p (i h s) -> p i h s", i=NB, h=H)

            with nc.Block() as block:
                @block.tensor
                def _(pe):
                    finished = [0, 0]
                    prepared = [0]

                    def decays(cc, b):
                        pe_decays(pe, cc, b, finished=finished)
                        prepared[0] = nth(cc, b) + 1

                    def start(cc, b):
                        f, c = chunks[cc]
                        if cc >= 1:
                            pe.wait_ge(o_kept[b], cc)
                        vdc = vd[:, f, :, b, :].rearrange("p h (c i s) -> p c i h s", c=NC, s=BK)
                        pe.matmul(z_of(b), lhsT=cst["ident"][:, :], rhs=vdc[:, c], start=True, stop=False,
                                  skip_group_check=True)
                        if cc >= 1:
                            pe.wait_ge(s_ready[b], cc)
                        zo = ps[:, b, 0:2 * P].rearrange("p (i g e) -> p i g e", i=2 * NB, g=G)
                        for g in range(G):
                            mm = pe.matmul(zo[:, :, g, :], lhsT=state[:, b, g, :],
                                           rhs=kq[:, f, b, c, :, :, g, :, :].rearrange("p q i h s -> p (q i) (h s)"),
                                           start=False, stop=(g == G - 1), skip_group_check=True)
                        mm.then_inc(z_ready[b], 1)

                    def turn(cc, b, i):
                        pe.wait_ge(w_ready[b], NB * cc + i + 1)
                        if i < NB - 1:
                            pe.transpose(ps[0:BK * H, 2 + b, 0:P], w[:, b, i, :, :].rearrange("p h s -> p (h s)"),
                                         cst["ident"][:, :]).then_inc(wt_ready[b], 1)
                        else:
                            pe.transpose(ps[:, 2 + b, P:2 * P], w[:, b, :, :, :].rearrange("p i h s -> p (i h s)"),
                                         cst["ident"][:, :]).then_inc(wt_ready[b], 1)

                    def take_off(cc, b, i):
                        n = B * cc + b
                        pe.wait_ge(wt_kept[b], NB * cc + i + 1)
                        if i == 0 and cc >= 1:
                            pe.wait_ge(S["g_kept"], nth(cc, b) + 1)
                        lo = BK * H * (i + 1)
                        pe.matmul(ps[:, b, lo:P], lhsT=wtb[:, b, :], rhs=gm[:, n % 4, i, lo:P], start=False, stop=True,
                                  skip_group_check=True).then_inc(z_ready[b], 1)

                    def finish(cc, b):
                        n = B * cc + b
                        pe.wait_ge(wt_kept[b], NB * (cc + 1))
                        if cc >= 1:
                            pe.wait_ge(S["k_kept"], 4 * (nth(cc, b) + 1))
                        pe.wait_ge(S["f_kept"], prepared[0])
                        for bb in range(B):
                            if finished[bb]:
                                pe.wait_ge(p_used[bb], finished[bb])
                        for g in range(G):
                            mm = pe.matmul(ps[:, 4, g * P:(g + 1) * P], lhsT=kfull[:, n % 4, g, :], rhs=wtf[:, b, :],
                                           start=True, stop=True, skip_group_check=True)
                        mm.then_inc(p_ready[b], 1)
                        finished[b] = cc + 1
                        if cc >= 1:
                            pe.wait_ge(S["q_kept"], nth(cc, b) + 1)
                        pe.matmul(ps[:, b, P:2 * P], lhsT=wtf[:, b, :], rhs=qkm[:, n % 4, :], start=False, stop=True,
                                  skip_group_check=True).then_inc(o_ready[b], 1)

                    for cc, (f, c) in enumerate(chunks):
                        def ring(i, part):
                            for item in both.slots[NB * c + i][part]:
                                pe_item(pe, both, f, 1 - f, item, 2 * it + f + 1, 2 * it + f - 1)

                        if c == 0 and f == 1:
                            pe.wait_ge(S["prepared"], f)
                        start(cc, 0)
                        ring(0, 0)
                        start(cc, 1)
                        turn(cc, 0, 0)
                        ring(0, 1)
                        turn(cc, 1, 0)
                        take_off(cc, 0, 0)
                        pe_products(pe, cc + 1, 0)
                        turn(cc, 0, 1)
                        take_off(cc, 1, 0)
                        ring(1, 0)
                        turn(cc, 1, 1)
                        take_off(cc, 0, 1)
                        ring(1, 1)
                        decays(cc + 1, 0)
                        turn(cc, 0, 2)
                        take_off(cc, 1, 1)
                        ring(2, 0)
                        turn(cc, 1, 2)
                        take_off(cc, 0, 2)
                        pe_products(pe, cc + 1, 1)
                        ring(2, 1)
                        decays(cc + 1, 1)
                        turn(cc, 0, 3)
                        take_off(cc, 1, 2)
                        ring(3, 0)
                        turn(cc, 1, 3)
                        finish(cc, 0)
                        ring(3, 1)
                        finish(cc, 1)

                @block.gpsimd
                def _(pool):
                    ch = Chain(pool, pool_chain)

                    for f in range(2):
                        cc = NC * f
                        pool_ends(pool, cc + 1)
                        pool_ends(pool, cc + 2)
                        pool_scan(pool, ch, f, 1 - f)
                        pool_prepare(pool, both, f, 1 - f, "near")
                        pool_rstd(pool, ch, both, f)
                        pool_ends(pool, cc + 3)
                        pool_prepare(pool, both, f, 1 - f, 0, nth(cc + 4, 0))
                        pool_prepare(pool, both, f, 1 - f, 1)
                        pool_ends(pool, cc + 4)
                        pool_gate(pool, ch, both, f)

                @block.scalar
                def _(act):
                    def keep(cc, b, i):
                        act.wait_ge(wt_ready[b], NB * cc + i + 1)
                        if i < NB - 1:
                            nc.scalar.copy(wtb[:, b, :], ps[0:BK * H, 2 + b, 0:P]).then_inc(wt_kept[b], 1)
                        else:
                            if cc >= 1:
                                act.wait_ge(o_ready[b], cc)
                            nc.scalar.copy(wtf[:, b, :], ps[:, 2 + b, P:2 * P]).then_inc(wt_kept[b], 1)

                    for cc, (f, c) in enumerate(chunks):
                        def ring(i, part):
                            for item in both.slots[NB * c + i][part]:
                                act_item(act, both, f, 1 - f, item)

                        ring(0, 0)
                        keep(cc, 0, 0)
                        ring(0, 1)
                        keep(cc, 1, 0)
                        keep(cc, 0, 1)
                        act_k_rows(act, cc + 1, 0, (0, 1))
                        keep(cc, 1, 1)
                        ring(1, 0)
                        keep(cc, 0, 2)
                        act_k_rows(act, cc + 1, 0, (2, 3))
                        ring(1, 1)
                        act_decays(act, cc + 1, 0)
                        keep(cc, 1, 2)
                        ring(2, 0)
                        keep(cc, 0, 3)
                        ring(2, 1)
                        act_decays(act, cc + 1, 1)
                        keep(cc, 1, 3)
                        act_k_rows(act, cc + 1, 1, range(G))
                        ring(3, 0)
                        ring(3, 1)

                @block.vector
                def _(dve):
                    ch = Chain(dve, dve_chain)

                    def solve(cc, b, i):
                        f, c = chunks[cc]
                        dve.wait_ge(z_ready[b], NB * cc + i + 1)
                        zi = z_of(b)[:, i].unsqueeze(2).to_broadcast([P, H, BK, BK])
                        mtc = mt[:, f, :, :, :].rearrange("p (h b n) i j -> p h b n i j", h=H, b=B)
                        ch.step(nc.vector.tensor_tensor(prod[:, b, :, :, :], zi, mtc[:, :, b, NB * c + i, :, :], ALU.mult))
                        if i == 0 and cc >= 1:
                            dve.wait_ge(wt_ready[b], NB * cc)
                        nc.vector.tensor_reduce(w[:, b, i, :, :], prod[:, b, :, :, :], axis=AX.X,
                                                op=ALU.add).then_inc(w_ready[b], 1)

                    def update(cc, b):
                        f, c = chunks[cc]
                        n = B * cc + b
                        dve.wait_ge(p_ready[b], cc + 1)
                        nc.vector.tensor_tensor(state[:, b, :, :], ps[:, 4, :].rearrange("p (g v) -> p g v", g=G),
                                                state[:, b, :, :], ALU.add).then_inc(p_used[b], 1)
                        dve.wait_ge(p_used[b], cc + 1)
                        if cc >= 1:
                            dve.wait_ge(S["f_kept"], nth(cc, b) + 1)
                        nc.vector.tensor_tensor(state[:, b, :, :], state[:, b, :, :], decay[:, n % 4, :, :],
                                                ALU.mult).then_inc(s_ready[b], 1)
                        dve.wait_ge(o_ready[b], cc + 1)
                        oc = o[:, f, :, b, :].rearrange("p h (c i s) -> p c h i s", c=NC, s=BK)
                        nc.vector.tensor_tensor(oc[:, c], ps[:, b, P:2 * P].rearrange("p (i h s) -> p h i s", i=NB, h=H),
                                                dd_of(f)[:, :, b, c], ALU.mult).then_inc(o_kept[b], 1)

                    for cc, (f, c) in enumerate(chunks):
                        def work(i):
                            dve_slot(dve, ch, both, f, 1 - f, NB * c + i, 2 * it + f - 1)

                        solve(cc, 0, 0)
                        solve(cc, 1, 0)
                        work(0)
                        solve(cc, 0, 1)
                        dve_masks(dve, cc + 1, 0)
                        solve(cc, 1, 1)
                        work(1)
                        solve(cc, 0, 2)
                        solve(cc, 1, 2)
                        work(2)
                        solve(cc, 0, 3)
                        dve_masks(dve, cc + 1, 1)
                        solve(cc, 1, 3)
                        if c == NC - 1:
                            prepare_slot(dve, ch, both, f, 1 - f, 15)
                        update(cc, 0)
                        update(cc, 1)
                        work(3)
            stage_end(nc, every)

        with nc.Block() as block:
            @block.tensor
            def _(pe):
                for item in only_post.names:
                    pe_item(pe, only_post, 0, 1, item, 0, NS - 1)

            @block.scalar
            def _(act):
                for item in only_post.order:
                    act_item(act, only_post, 0, 1, item)

            @block.gpsimd
            def _(pool):
                ch = Chain(pool, pool_chain)
                pool_rstd(pool, ch, only_post, 0)
                pool_gate(pool, ch, only_post, 0)

            @block.vector
            def _(dve):
                ch = Chain(dve, dve_chain)
                for slot in range(16):
                    dve_slot(dve, ch, only_post, 0, 1, slot, NS - 1)


def layer_norm(nc, ctx, cst, ps, res, xT, name):
    with ExitStack() as own:
        def sb(n, shape, dt=F32):
            return own.enter_context(nc.sbuf_tensor(f"{name}_{n}", shape, dt))
        total, mean, var, std = (sb(n, [P, NT]) for n in ("total", "mean", "var", "std"))
        sq = sb("sq", [P, NT, C])
        centred, squared, summed, rooted, done, turned, kept, chain = (
            ctx.enter_context(nc.semaphore(f"{name}_{n}")) for n in
            ("centred", "squared", "summed", "rooted", "done", "turned", "kept", "chain"))
        wide = [P, NT, C]
        with nc.Block() as block:
            @block.vector
            def _(dve):
                ch = Chain(dve, chain)
                ch.step(nc.vector.tensor_reduce(total[:, :], res[:, :, :], axis=AX.X, op=ALU.add))
                ch.step(nc.vector.tensor_scalar(mean[:, :], total[:, :], 1.0 / C, None, ALU.mult))
                nc.vector.tensor_tensor(res[:, :, :], res[:, :, :], mean[:, :].unsqueeze(2).to_broadcast(wide),
                                        ALU.subtract).then_inc(centred, 1)
                dve.wait_ge(squared, 1)
                nc.vector.tensor_reduce(var[:, :], sq[:, :, :], axis=AX.X, op=ALU.add).then_inc(summed, 1)
                dve.wait_ge(rooted, 1)
                ch.step(nc.vector.reciprocal(std[:, :], std[:, :]))
                nc.vector.tensor_tensor(res[:, :, :], res[:, :, :], std[:, :].unsqueeze(2).to_broadcast(wide),
                                        ALU.mult).then_inc(done, 1)

            @block.scalar
            def _(act):
                act.wait_ge(centred, 1)
                nc.scalar.activation(sq[:, :, :], res[:, :, :], ACT.Square).then_inc(squared, 1)
                act.wait_ge(summed, 1)
                nc.scalar.activation(std[:, :], var[:, :], ACT.Sqrt, bias=cst["eps"][:, 0:1], scale=1.0 / C).then_inc(rooted, 1)
                if xT is not None:
                    for n in range(NT // 4):
                        act.wait_ge(turned, n + 1)
                        nc.scalar.copy(xT[:, n * 512:(n + 1) * 512], ps[:, n, :])

            @block.tensor
            def _(pe):
                if xT is not None:
                    pe.wait_ge(done, 1)
                    for n in range(NT):
                        mm = pe.transpose(ps[:, n // 4, (n % 4) * P:(n % 4 + 1) * P], res[:, n, :], cst["ident"][:, :])
                        if n % 4 == 3:
                            mm.then_inc(turned, 1)


NE = 8
TOP = 2


def route(nc, ctx, cst, ps, xT, wr, bias, comb, name):
    with ExitStack() as own:
        def sb(n, shape):
            return own.enter_context(nc.sbuf_tensor(f"{name}_{n}", shape, F32))
        score, shifted, part = sb("score", [P, NT, NE]), sb("shifted", [P, NT, NE]), sb("part", [P, NT, NE])
        above, equal = sb("above", [P, NT, NE, NE]), sb("equal", [P, NT, NE, NE])
        rank, total = sb("rank", [P, NT, NE]), sb("total", [P, NT])
        logits, scored, shift_done, exp_done, chain = (ctx.enter_context(nc.semaphore(f"{name}_{n}")) for n in
                                                       ("logits", "scored", "shift_done", "exp_done", "chain"))
        out = ps[:, 7, 0:NT * NE].rearrange("p (n e) -> p n e", n=NT)
        square = [P, NT, NE, NE]
        with nc.Block() as block:
            @block.tensor
            def _(pe):
                for n in range(NT):
                    mm = pe.matmul(out[:, n, :], lhsT=xT[:, n * P:(n + 1) * P], rhs=wr[:, :], start=True, stop=True,
                                   skip_group_check=True)
                mm.then_inc(logits, 1)

            @block.scalar
            def _(act):
                if bias is None:
                    act.wait_ge(logits, 1)
                    nc.scalar.activation(score[:, :, :], out, ACT.Sigmoid).then_inc(scored, 1)
                else:
                    act.wait_ge(shift_done, 1)
                    nc.scalar.activation(part[:, :, :], shifted[:, :, :], ACT.Exp).then_inc(exp_done, 1)

            @block.vector
            def _(dve):
                ch = Chain(dve, chain)
                if bias is None:
                    dve.wait_ge(scored, 1)
                    value = score
                else:
                    dve.wait_ge(logits, 1)
                    ch.step(nc.vector.tensor_tensor(score[:, :, :], out, bias[:, :].unsqueeze(1).to_broadcast([P, NT, NE]), ALU.add))
                    ch.step(nc.vector.tensor_reduce(total[:, :], score[:, :, :], axis=AX.X, op=ALU.max))
                    nc.vector.tensor_tensor(shifted[:, :, :], score[:, :, :], total[:, :].unsqueeze(2).to_broadcast([P, NT, NE]),
                                            ALU.subtract).then_inc(shift_done, 1)
                    value = part
                other = score[:, :, :].unsqueeze(2).to_broadcast(square)
                mine = score[:, :, :].unsqueeze(3).to_broadcast(square)
                nc.vector.tensor_tensor(above[:, :, :, :], other, mine, ALU.is_gt)
                ch.step(nc.vector.tensor_tensor(equal[:, :, :, :], other, mine, ALU.is_equal))
                ch.step(nc.vector.tensor_tensor(equal[:, :, :, :], equal[:, :, :, :],
                                                cst["lower"][:, :, :].unsqueeze(1).to_broadcast(square), ALU.mult))
                ch.step(nc.vector.tensor_tensor(above[:, :, :, :], above[:, :, :, :], equal[:, :, :, :], ALU.add))
                ch.step(nc.vector.tensor_reduce(rank[:, :, :], above[:, :, :, :], axis=AX.X, op=ALU.add))
                ch.step(nc.vector.tensor_scalar(rank[:, :, :], rank[:, :, :], TOP - 0.5, None, ALU.is_lt))
                if bias is not None:
                    dve.wait_ge(exp_done, 1)
                ch.step(nc.vector.tensor_tensor(comb[:, :, :], rank[:, :, :], value[:, :, :], ALU.mult))
                ch.step(nc.vector.tensor_reduce(total[:, :], comb[:, :, :], axis=AX.X, op=ALU.add))
                if bias is None:
                    ch.step(nc.vector.tensor_scalar(total[:, :], total[:, :], 1e-20, None, ALU.add))
                ch.step(nc.vector.reciprocal(total[:, :], total[:, :]))
                ch.step(nc.vector.tensor_tensor(comb[:, :, :], comb[:, :, :], total[:, :].unsqueeze(2).to_broadcast([P, NT, NE]),
                                                ALU.mult))


def experts(nc, ctx, cst, ps, xT, res, comb, w1, w2, widths, b1, b2, name):
    tiles = [w // P for w in widths]
    first = [sum(tiles[:e]) for e in range(NE + 1)]
    most = max(tiles)
    QT = 4
    with ExitStack() as own:
        def sb(n, shape):
            return own.enter_context(nc.sbuf_tensor(f"{name}_{n}", shape, F32))
        hT = sb("hT", [P, 2, most, 512])
        relu = sb("relu", [P, 2, 512])
        acc = sb("acc", [P, QT, C])
        now = sb("now", [P, QT, NE])
        nowT = sb("nowT", [NE, QT, P])
        sems = {n: ctx.enter_context(nc.semaphore(f"{name}_{n}")) for n in
                "up rect_a rect_v relu_done kept_v down added start turned turned_kept bias_done chain".split()}
        total = first[NE]
        squared = b1 is None
        with nc.Fori(0, NT // QT) as q:
            with nc.Block() as block:
                @block.tensor
                def _(pe):
                    def up(e):
                        for m in range(first[e], first[e + 1]):
                            if m >= 4:
                                if squared:
                                    pe.wait_ge(sems["rect_v"], m - 3)
                                elif m % 2 == 0:
                                    pe.wait_ge(sems["rect_a"], (m - 4) // 2 + 1)
                                else:
                                    pe.wait_ge(sems["rect_v"], (m - 4) // 2 + 1)
                            pe.matmul(ps[:, m % 4, :], lhsT=w1[:, m * P:(m + 1) * P], rhs=xT[:, bass.ts(q, 512)], start=True,
                                      stop=True).then_inc(sems["up"], 1)

                    def down(e):
                        if squared:
                            pe.wait_ge(sems["rect_v"], first[e + 1])
                        else:
                            pe.wait_ge(sems["rect_a"], (first[e + 1] + 1) // 2)
                            pe.wait_ge(sems["rect_v"], first[e + 1] // 2)
                        if e >= 2:
                            pe.wait_ge(sems["added"], QT * (e - 1))
                        for t in range(QT):
                            for j in range(tiles[e]):
                                mm = pe.matmul(ps[:, 4 + e % 2, t * P:(t + 1) * P], lhsT=hT[:, e % 2, j, t * P:(t + 1) * P],
                                               rhs=w2[:, first[e] + j, :], start=(j == 0), stop=(j == tiles[e] - 1),
                                               skip_group_check=True)
                        mm.then_inc(sems["down"], 1)

                    up(0)
                    if not squared:
                        pe.wait_ge(sems["start"], 1)
                        for t in range(QT):
                            mm = pe.transpose(ps[0:NE, 6, t * P:(t + 1) * P], now[:, t, :], cst["ident"][:, :])
                        mm.then_inc(sems["turned"], 1)
                        pe.wait_ge(sems["turned_kept"], 1)
                        for t in range(QT):
                            mm = pe.matmul(ps[:, 7, t * P:(t + 1) * P], lhsT=nowT[:, t, :], rhs=b2[:, :], start=True, stop=True,
                                           skip_group_check=True)
                        mm.then_inc(sems["bias_done"], 1)
                    for e in range(NE):
                        if e + 1 < NE:
                            up(e + 1)
                        down(e)

                def place(e, m):
                    return hT[:, e % 2, m - first[e], :]

                @block.scalar
                def _(act):
                    if not squared:
                        act.wait_ge(sems["turned"], 1)
                        nc.scalar.copy(nowT[:, :, :], ps[0:NE, 6, :].rearrange("p (t e) -> p t e", t=QT)).then_inc(
                            sems["turned_kept"], 1)
                    for e in range(NE):
                        for m in range(first[e], first[e + 1]):
                            if squared:
                                act.wait_ge(sems["up"], m + 1)
                                if m >= 2:
                                    act.wait_ge(sems["rect_v"], m - 1)
                                nc.scalar.activation(relu[:, m % 2, :], ps[:, m % 4, :], ACT.Relu).then_inc(sems["relu_done"], 1)
                            elif m % 2 == 0:
                                act.wait_ge(sems["up"], m + 1)
                                if e >= 2:
                                    act.wait_ge(sems["down"], e - 1)
                                nc.scalar.activation(place(e, m), ps[:, m % 4, :], ACT.Relu, bias=b1[:, m:m + 1]).then_inc(
                                    sems["rect_a"], 1)

                @block.vector
                def _(dve):
                    ch = Chain(dve, sems["chain"])

                    def rectify(e):
                        for m in range(first[e], first[e + 1]):
                            if not squared and m % 2 == 0:
                                continue
                            if e >= 2:
                                dve.wait_ge(sems["down"], e - 1)
                            if squared:
                                dve.wait_ge(sems["relu_done"], m + 1)
                                nc.vector.tensor_tensor(place(e, m), ps[:, m % 4, :], relu[:, m % 2, :], ALU.mult).then_inc(
                                    sems["rect_v"], 1)
                            else:
                                dve.wait_ge(sems["up"], m + 1)
                                nc.vector.tensor_scalar(place(e, m), ps[:, m % 4, :], b1[:, m:m + 1], 0.0, ALU.add,
                                                        ALU.max).then_inc(sems["rect_v"], 1)

                    nc.vector.tensor_copy(now[:, :, :], comb[:, bass.ts(q, QT), :]).then_inc(sems["start"], 1)
                    if squared:
                        ch.step(nc.vector.tensor_copy(acc[:, :, :], res[:, bass.ts(q, QT), :]))
                        dve.wait_ge(sems["start"], 1)
                        rectify(0)
                    else:
                        rectify(0)
                        dve.wait_ge(sems["bias_done"], 1)
                        ch.step(nc.vector.tensor_tensor(acc[:, :, :], res[:, bass.ts(q, QT), :],
                                                        ps[:, 7, :].rearrange("p (t c) -> p t c", t=QT), ALU.add))
                    for e in range(NE):
                        if e + 1 < NE:
                            rectify(e + 1)
                        dve.wait_ge(sems["down"], e + 1)
                        if e >= 1:
                            dve.wait_ge(sems["added"], QT * e)
                        for t in range(QT):
                            nc.vector.scalar_tensor_tensor(out=acc[:, t, :], in0=ps[:, 4 + e % 2, t * P:(t + 1) * P],
                                                           scalar=now[:, t, e:e + 1], in1=acc[:, t, :], op0=ALU.mult,
                                                           op1=ALU.add).then_inc(sems["added"], 1)
                    dve.wait_ge(sems["added"], QT * NE)
                    ch.step(nc.vector.tensor_copy(res[:, bass.ts(q, QT), :], acc[:, :, :]))
            stage_end(nc, list(sems.values()))


AH, AD = 16, 64
NP = AH // 2
TT = T // P


def softmax_attention(nc, ctx, cst, ps, d, xT, res):
    with ExitStack() as own:
        def sb(n, shape, dt=F32):
            return own.enter_context(nc.sbuf_tensor("b_" + n, shape, dt))

        def sem(n):
            return ctx.enter_context(nc.semaphore("b_" + n))

        HD = AH * AD
        wq = sb("wq", [P, HD + P])
        wkv = sb("wkv", [P, 2 * HD + P])
        wdown, wout = sb("wdown", [C, P]), sb("wout", [P, NP, C])
        latT = sb("latT", [P, B * T])
        yT = sb("yT", [P, NP, B * T])
        pair_w = sb("pair_w", [P, 2, 3, P])
        qT, kT = sb("qT", [P, 2, B * T]), sb("kT", [P, 2, B * T])
        v = sb("v", [P, 2, NT, P])
        prob = sb("prob", [P, 2, T])
        probT = sb("probT", [P, 4, TT, P])
        nmax, total, inv = sb("nmax", [P, 4]), sb("total", [P, 4, 2]), sb("inv", [P, 4, 2])
        spread = sb("spread", [P, 2, 2, AD])
        recipT = sb("recipT", [P, 2, P])
        x_row = xT[:, :].rearrange("c (n b t) -> c b n t", b=B, t=TS)
        y_row = yT[:, :, :].rearrange("c m (n b t) -> c m b n t", b=B, t=TS)
        loaded, lat_kept, lat_done = sem("loaded"), sem("lat_kept"), sem("lat_done")
        names = ("picked piece_done piece_kept_a piece_kept_v s_done max_done exp_done pt_done pt_kept_v pt_kept_a "
                 "recip_done spread_done o_done recip_kept y_done")
        sems = {n: sem(n) for n in names.split()}

        PIECES = [(kind, m) for kind in ("q", "k", "v") for m in range(4)]

        def project(pe, bank, f, piece):
            kind, m = piece
            if kind == "q":
                return pe.matmul(bank, lhsT=pair_w[:, f, 0, :], rhs=x_row[:, m // 2, 8 * (m % 2):8 * (m % 2) + 8, :],
                                 start=True, stop=True)
            if kind == "k":
                return pe.matmul(bank, lhsT=pair_w[:, f, 1, :], rhs=latT[:, m * 512:(m + 1) * 512], start=True, stop=True)
            for t in range(4):
                n = 4 * m + t
                mm = pe.matmul(bank[:, t * P:(t + 1) * P], lhsT=latT[:, n * P:(n + 1) * P], rhs=pair_w[:, f, 2, :],
                               start=True, stop=True, skip_group_check=True)
            return mm

        def keep_qk(bank, f, piece):
            kind, m = piece
            if kind == "q":
                return nc.scalar.mul(qT[:, f, m * 512:(m + 1) * 512], bank, AD ** -0.5)
            return nc.scalar.copy(kT[:, f, m * 512:(m + 1) * 512], bank)

        def keep_v(bank, f, piece):
            m = piece[1]
            return nc.vector.tensor_copy(v[:, f, 4 * m:4 * m + 4, :], bank.rearrange("p (t c) -> p t c", t=4))

        def pick(hp, f):
            for j, (w, at) in enumerate(((wq, 0), (wkv, 0), (wkv, HD))):
                nc.gpsimd.tensor_copy(pair_w[:, f, j, :], w[:, bass.ds(hp * P + at, P)] if not isinstance(hp, int) else
                                      w[:, hp * P + at:hp * P + at + P]).then_inc(sems["picked"], 1)

        with nc.Block() as block:
            @block.sync
            def _(sp):
                sp.dma_start(wdown[:, :], d["w_kv_down"]).then_inc(loaded, 16)
                sp.dma_start(wq[:, 0:HD], d["w_q"]).then_inc(loaded, 16)
                sp.dma_start(wkv[:, 0:2 * HD], d["w_kv_up"]).then_inc(loaded, 16)
                sp.dma_start(wout[:, :, :], d["w_out"]).then_inc(loaded, 16)
                sp.wait_ge(loaded, 64)

            @block.gpsimd
            def _(pool):
                nc.gpsimd.memset(wq[:, HD:], 0.0)
                nc.gpsimd.memset(wkv[:, 2 * HD:], 0.0)
                pool.wait_ge(loaded, 64)
                pick(0, 0)

            @block.tensor
            def _(pe):
                pe.wait_ge(loaded, 64)
                for m in range(4):
                    pe.matmul(ps[:, m, :], lhsT=wdown[:, :], rhs=x_row[:, m // 2, 8 * (m % 2):8 * (m % 2) + 8, :], start=True,
                              stop=True).then_inc(lat_done, 1)
                pe.wait_ge(sems["picked"], 3)
                for n, piece in enumerate(PIECES):
                    if n == 4:
                        pe.wait_ge(lat_kept, 4)
                    if n >= 8:
                        pe.wait_ge(sems["piece_kept_a"], n - 7)
                    project(pe, ps[:, (n + 4) % 8, :], 0, piece).then_inc(sems["piece_done"], 1)

            @block.scalar
            def _(act):
                for m in range(4):
                    act.wait_ge(lat_done, m + 1)
                    nc.scalar.copy(latT[:, m * 512:(m + 1) * 512], ps[:, m, :]).then_inc(lat_kept, 1)
                for n, piece in enumerate(PIECES[:8]):
                    act.wait_ge(sems["piece_done"], n + 1)
                    keep_qk(ps[:, (n + 4) % 8, :], 0, piece).then_inc(sems["piece_kept_a"], 1)

            @block.vector
            def _(dve):
                for n, piece in list(enumerate(PIECES))[8:]:
                    dve.wait_ge(sems["piece_done"], n + 1)
                    keep_v(ps[:, (n + 4) % 8, :], 0, piece)
        stage_end(nc, list(sems.values()))

        order = [i for k in range(TT // 2) for i in (TT - 1 - k, k)]
        pairs = [(f, b, i) for f in range(2) for b in range(B) for i in order]
        W = len(pairs)
        U = 2 * W
        UF = U // 2
        at_step = {f * UF + 2 + 2 * n: (f, n) for f in range(2) for n in range(len(PIECES))}

        def tiles(u):
            return pairs[u // 2][2] + 1

        two_chunks = [sum(tiles(x) > 4 for x in range(u + 1)) for u in range(U)]

        def turned(u):
            return u + 1 + two_chunks[u]

        with nc.Fori(0, NP // 2) as it:
            with nc.Block() as block:
                @block.gpsimd
                def _(pool):
                    pick(2 * it + 1, 1)
                    for w in range(W):
                        if w == W // 2:
                            pick(2 * it + 2, 0)
                        pool.wait_ge(sems["recip_done"], w + 1)
                        if w >= 2:
                            pool.wait_ge(sems["o_done"], w - 1)
                        nc.gpsimd.tensor_copy(spread[:, w % 2, :, :], inv[:, w % 4, :].unsqueeze(2).to_broadcast(
                            [P, 2, AD])).then_inc(sems["spread_done"], 1)

                @block.tensor
                def _(pe):
                    def scores(u):
                        f, b, i = pairs[u // 2]
                        h = u % 2
                        if u == UF:
                            pe.wait_ge(sems["piece_kept_a"], 8)
                        if u >= 2:
                            pe.wait_ge(sems["exp_done"], u - 1)
                        rows = slice(AD * h, AD * h + AD)
                        n = tiles(u) * P
                        for c0 in range(0, n, 512):
                            c1 = min(n, c0 + 512)
                            last = c1 == n
                            bank = ps[:, 2 * (u % 2) + c0 // 512, :]
                            mm = pe.matmul(bank[:, 0:c1 - c0], lhsT=qT[rows, f, b * T + i * P:b * T + (i + 1) * P],
                                           rhs=kT[rows, f, b * T + c0:b * T + c1], start=True, stop=not last,
                                           skip_group_check=True)
                            if last:
                                mm = pe.matmul(bank[:, c1 - c0 - P:c1 - c0], lhsT=cst["ident16"][:, :],
                                               rhs=cst["above_diag"][:, :], start=False, stop=True, skip_group_check=True)
                        mm.then_inc(sems["s_done"], 1)

                    def piece(u):
                        f, n = at_step[u]
                        if n == 0:
                            pe.wait_ge(sems["picked"], 3 * (f + 1))
                        a, vv = 8 * f + min(n, 8), 4 * f + max(n - 8, 0)
                        if n > 8 or (n == 0 and f):
                            pe.wait_ge(sems["piece_kept_v"], vv)
                        elif a:
                            pe.wait_ge(sems["piece_kept_a"], a)
                        project(pe, ps[:, 7, :], 1 - f, PIECES[n]).then_inc(sems["piece_done"], 1)

                    def turn(u):
                        pe.wait_ge(sems["exp_done"], u + 1)
                        if u >= 1:
                            pe.wait_ge(sems["pt_kept_v"], u)
                        for j in range(tiles(u)):
                            if j == 4 and two_chunks[u] > 1:
                                pe.wait_ge(sems["pt_kept_a"], two_chunks[u] - 1)
                            mm = pe.transpose(ps[:, 4 + j // 4, (j % 4) * P:(j % 4 + 1) * P], prob[:, u % 2, j * P:(j + 1) * P],
                                              cst["ident"][:, :])
                            if j == min(4, tiles(u)) - 1 or j == tiles(u) - 1:
                                mm.then_inc(sems["pt_done"], 1)

                    def values(w):
                        f, b, i = pairs[w]
                        pe.wait_ge(sems["pt_kept_v"], 2 * w + 2)
                        if tiles(2 * w) > 4:
                            pe.wait_ge(sems["pt_kept_a"], two_chunks[2 * w + 1])
                        if w == W // 2:
                            pe.wait_ge(sems["piece_kept_v"], 4)
                        if w >= 1:
                            pe.wait_ge(sems["y_done"], w)
                        for j in range(i + 1):
                            for h in range(2):
                                cols = slice(AD * h, AD * h + AD)
                                pe.matmul(ps[cols, 6, 0:P], lhsT=v[:, f, b * TT + j, cols], rhs=probT[:, (2 * w + h) % 4, j, :],
                                          start=(j == 0), stop=(j == i), skip_group_check=True)
                        pe.wait_ge(sems["spread_done"], w + 1)
                        pe.transpose(ps[:, 6, P:2 * P], spread[:, w % 2, :, :].rearrange("p h c -> p (h c)"),
                                     cst["ident"][:, :]).then_inc(sems["o_done"], 1)

                    scores(0)
                    for u in range(U + 1):
                        if u + 1 < U:
                            scores(u + 1)
                        if u in at_step:
                            piece(u)
                        if u < U:
                            turn(u)
                        if u >= 2 and u % 2 == 0:
                            values(u // 2 - 1)

                @block.scalar
                def _(act):
                    def exponent(u):
                        w, h = u // 2, u % 2
                        n = tiles(u) * P
                        act.wait_ge(sems["max_done"], u + 1)
                        if u >= 2:
                            act.wait_ge(sems["pt_done"], turned(u - 2))
                        if w >= 4:
                            act.wait_ge(sems["recip_done"], w - 3)
                        src = ps[:, 2 * (u % 2):2 * (u % 2) + 2, :].rearrange("p k e -> p (k e)")[:, 0:n]
                        nc.scalar.activation(prob[:, u % 2, 0:n], src, ACT.Exp, bias=nmax[:, u % 4:u % 4 + 1],
                                             accum_out=total[:, w % 4, h:h + 1]).then_inc(sems["exp_done"], 1)

                    for u in range(U + 2):
                        if u < U:
                            exponent(u)
                        if u - 1 in at_step and at_step[u - 1][1] < 8:
                            f, n = at_step[u - 1]
                            act.wait_ge(sems["piece_done"], len(PIECES) * f + n + 1)
                            keep_qk(ps[:, 7, :], 1 - f, PIECES[n]).then_inc(sems["piece_kept_a"], 1)
                        if 1 <= u <= U and tiles(u - 1) > 4:
                            x = u - 1
                            act.wait_ge(sems["pt_done"], turned(x))
                            if x >= 4:
                                act.wait_ge(sems["o_done"], x // 2 - 1)
                            rest = tiles(x) - 4
                            nc.scalar.copy(probT[:, x % 4, 4:tiles(x), :], ps[:, 5, 0:rest * P].rearrange(
                                "p (j t) -> p j t", j=rest)).then_inc(sems["pt_kept_a"], 1)
                        if u >= 3 and u % 2 == 1:
                            w = (u - 3) // 2
                            act.wait_ge(sems["o_done"], w + 1)
                            if w >= 2:
                                act.wait_ge(sems["y_done"], w - 1)
                            nc.scalar.copy(recipT[:, w % 2, :], ps[:, 6, P:2 * P]).then_inc(sems["recip_kept"], 1)

                @block.vector
                def _(dve):
                    def row_max(u):
                        n = tiles(u) * P
                        dve.wait_ge(sems["s_done"], u + 1)
                        if u >= 4:
                            dve.wait_ge(sems["exp_done"], u - 3)
                        src = ps[:, 2 * (u % 2):2 * (u % 2) + 2, :].rearrange("p k e -> p (k e)")[:, 0:n]
                        nc.vector.tensor_reduce(nmax[:, u % 4:u % 4 + 1], src, axis=AX.X, op=ALU.max, negate=True).then_inc(
                            sems["max_done"], 1)

                    row_max(0)
                    for u in range(U + 2):
                        if u + 1 < U:
                            row_max(u + 1)
                        if u < U:
                            dve.wait_ge(sems["pt_done"], u + 1 + (two_chunks[u - 1] if u else 0))
                            if u >= 4:
                                dve.wait_ge(sems["o_done"], u // 2 - 1)
                            k = min(4, tiles(u))
                            nc.vector.tensor_copy(probT[:, u % 4, 0:k, :], ps[:, 4, 0:k * P].rearrange(
                                "p (j t) -> p j t", j=k)).then_inc(sems["pt_kept_v"], 1)
                            if u % 2:
                                w = u // 2
                                dve.wait_ge(sems["exp_done"], u + 1)
                                if w >= 4:
                                    dve.wait_ge(sems["spread_done"], w - 3)
                                nc.vector.reciprocal(inv[:, w % 4, :], total[:, w % 4, :]).then_inc(sems["recip_done"], 1)
                        if u in at_step and at_step[u][1] >= 8:
                            f, n = at_step[u]
                            dve.wait_ge(sems["piece_done"], len(PIECES) * f + n + 1)
                            keep_v(ps[:, 7, :], 1 - f, PIECES[n]).then_inc(sems["piece_kept_v"], 1)
                        if u >= 3 and u % 2 == 1:
                            w = (u - 3) // 2
                            f, b, i = pairs[w]
                            dve.wait_ge(sems["recip_kept"], w + 1)
                            view = "p (m n t) -> p m n t"
                            nc.vector.tensor_tensor(y_row[:, bass.ds(2 * it + f, 1), b, 2 * i:2 * i + 2, :],
                                                    ps[:, 6, 0:P].rearrange(view, m=1, n=2),
                                                    recipT[:, w % 2, :].rearrange(view, m=1, n=2),
                                                    ALU.mult).then_inc(sems["y_done"], 1)
            stage_end(nc, list(sems.values()))

        out_done = sem("out_done")
        with nc.Block() as block:
            @block.tensor
            def _(pe):
                for n in range(NT):
                    for m in range(NP):
                        mm = pe.matmul(ps[:, n // 4, (n % 4) * P:(n % 4 + 1) * P], lhsT=yT[:, m, n * P:(n + 1) * P],
                                       rhs=wout[:, m, :], start=(m == 0), stop=(m == NP - 1), skip_group_check=True)
                    if n % 4 == 3:
                        mm.then_inc(out_done, 1)

            @block.vector
            def _(dve):
                for m in range(NT // 4):
                    dve.wait_ge(out_done, m + 1)
                    part = res[:, 4 * m:4 * m + 4, :]
                    nc.vector.tensor_tensor(part, part, ps[:, m, :].rearrange("p (t c) -> p t c", t=4), ALU.add)


F0_WIDTHS = [128] * 4 + [256] * 4
F1_WIDTHS = [512] * NE


def load(nc, ctx, name, pairs):
    loaded = ctx.enter_context(nc.semaphore(name))
    with nc.Block() as block:
        @block.sync
        def _(sp):
            for dst, src in pairs:
                sp.dma_start(dst, src).then_inc(loaded, 16)
            sp.wait_ge(loaded, 16 * len(pairs))


def program(nc, d, out):
    with ExitStack() as ctx:
        def sb(name, shape, dt=F32):
            return ctx.enter_context(nc.sbuf_tensor(name, shape, dt))
        ps = ctx.enter_context(nc.psum_tensor("ps", [P, 8, 512], F32))
        cst = {"ident": sb("ident", [P, P]), "centre": sb("centre", [P, P]), "mean_col": sb("mean_col", [P, 1]), "minus_half": sb("minus_half", [P, H]),
               "head_sum": sb("head_sum", [P, 2, P]), "same_head": sb("same_head", [P, P]), "eps": sb("eps", [P, 1]),
               "pair_rows": sb("pair_rows", [P, G]), "lower": sb("lower", [P, NE, NE]),
               "causal_head": sb("causal_head", [P, P]), "above_diag": sb("above_diag", [P, P], BF16),
               "ident16": sb("ident16", [P, P], BF16)}
        stream = sb("stream", [P, 1 + NT, C])
        res = stream[:, 1:, :]
        constants(nc, cst)
        delta_attention(nc, cst, ps, d, stream)
        xT = sb("xTn", [C, B * T])
        comb = sb("comb", [P, NT, NE])
        layer_norm(nc, ctx, cst, ps, res, xT, "n0")
        with ExitStack() as own:
            def wsb(name, shape):
                return own.enter_context(nc.sbuf_tensor(name, shape, F32))
            ff = sum(F0_WIDTHS)
            w1, w2, wr = wsb("f0_w1", [C, ff]), wsb("f0_w2", [P, ff // P, C]), wsb("f0_wr", [C, NE])
            load(nc, ctx, "f0_loaded", [(w1[:, :], d["f0_w1"]), (w2[:, :, :], d["f0_w2"]), (wr[:, :], d["f0_wr"])])
            route(nc, ctx, cst, ps, xT, wr, None, comb, "r0")
            experts(nc, ctx, cst, ps, xT, res, comb, w1, w2, F0_WIDTHS, None, None, "f0")
        layer_norm(nc, ctx, cst, ps, res, xT, "n1")
        softmax_attention(nc, ctx, cst, ps, d, xT, res)
        layer_norm(nc, ctx, cst, ps, res, xT, "n2")
        with ExitStack() as own:
            def wsb(name, shape):
                return own.enter_context(nc.sbuf_tensor(name, shape, F32))
            ff = sum(F1_WIDTHS)
            w1, w2, wr = wsb("f1_w1", [C, ff]), wsb("f1_w2", [P, ff // P, C]), wsb("f1_wr", [C, NE])
            b1, b2, br = wsb("f1_b1", [P, ff // P]), wsb("f1_b2", [NE, C]), wsb("f1_br", [P, NE])
            load(nc, ctx, "f1_loaded", [
                (w1[:, :].rearrange("c (e f) -> c e f", e=NE), d["f1_w1"]), (w2[:, :, :], d["f1_w2"]), (wr[:, :], d["f1_wr"]),
                (b1[:, :], d["f1_b1"]), (b2[:, :], d["f1_b2"]), (br[:, :], d["f1_br"].partition_broadcast(P))])
            route(nc, ctx, cst, ps, xT, wr, br, comb, "r1")
            experts(nc, ctx, cst, ps, xT, res, comb, w1, w2, F1_WIDTHS, b1, b2, "f1")
        layer_norm(nc, ctx, cst, ps, res, None, "n3")
        load(nc, ctx, "stored", [(out, res[:, :, :])])


def lay_out(i):
    import numpy as np
    a = {k: np.asarray(v) for k, v in i.items()}
    x = a["L0_attn_x"]
    pre = "L0_attn_"
    chan = lambda v, n: v.reshape(n, P).T
    taps = np.concatenate([a[pre + n + "_w"][:, 0, :] for n in ("qc", "kc", "vc")], 0).T
    rows = lambda w: w.reshape(-1, P, C).transpose(1, 0, 2)
    return {
        "xT": x.transpose(2, 0, 1), "x_tok": x.reshape(B, NT, TS, C).transpose(0, 2, 1, 3).reshape(P, NT, C),
        "WqT": a[pre + "Wq"].T, "WkT": a[pre + "Wk"].T, "WvT": a[pre + "Wv"].T, "WaT": a[pre + "Wa"].T,
        "WgT": a[pre + "Wg"].T, "WbT": a[pre + "Wb"].T,
        "WoT": a[pre + "Wo"].reshape(C, H, DV).transpose(2, 1, 0), "taps": taps,
        "conv_b": np.concatenate([chan(a[pre + n + "_b"], m) for n, m in (("qc", G), ("kc", G), ("vc", H))], 1),
        "ba": chan(a[pre + "ba"], H), "bb": a[pre + "bb"], "ln_w": a[pre + "ln_w"][:, None], "ln_b": a[pre + "ln_b"][:, None],
        "f0_w1": a["L0_ffn_w1"], "f0_w2": rows(a["L0_ffn_w2"]), "f0_wr": a["L0_ffn_router_w"].T,
        "w_kv_down": a["L1_attn_w_kv_down"], "w_q": a["L1_attn_w_q"], "w_kv_up": a["L1_attn_w_kv_up"],
        "w_out": rows(a["L1_attn_w_out"]),
        "f1_w1": a["L1_ffn_W1"].transpose(1, 0, 2), "f1_w2": rows(a["L1_ffn_W2"]), "f1_wr": a["L1_ffn_W_router"],
        "f1_b1": chan(a["L1_ffn_b1"].reshape(-1), sum(F1_WIDTHS) // P), "f1_b2": a["L1_ffn_b2"], "f1_br": a["L1_ffn_b_router"],
    }


def kernel(**inputs):
    import numpy as np
    import concourse.bacc as bacc
    from concourse.bass_utils import run_bass_kernel_spmd
    nc = bacc.Bacc("TRN2", target_bir_lowering=False, num_devices=1)
    arrays = {"in_" + k: np.ascontiguousarray(v) for k, v in lay_out(inputs).items()}
    d = {k[3:]: nc.dram_tensor(k, v.shape, F32, kind="ExternalInput").ap() for k, v in arrays.items()}
    out = nc.dram_tensor("out", (P, NT, C), F32, kind="ExternalOutput").ap()
    program(nc, d, out)
    r = run_bass_kernel_spmd(nc, [arrays], core_ids=[0])
    return r.results[0]["out"].reshape(B, TS, NT, C).transpose(0, 2, 1, 3).reshape(B, T, C)
```

```python
from contextlib import ExitStack

import concourse.bass as bass
from concourse import mybir

F32 = mybir.dt.float32
BF16 = mybir.dt.bfloat16
ALU = mybir.AluOpType
ACT = mybir.ActivationFunctionType
AX = mybir.AxisListType

P = 128
B, T, C = 2, 1024, 128
NT = B * T // P
H, DK, DV, TAPS = 8, 64, 128, 4
G = H * DK // P
TS = 64
NS = T // TS
CH = 16
NC = TS // CH
BK = 4
NB = CH // BK
EPS = 1e-5
LOOK = TAPS - 1


class Ring:

    def __init__(self, slots, by_vector):
        self.slots, self.by_vector = slots, by_vector
        self.names = [name for slot in slots for part in slot for name in part]
        self.order = list(dict.fromkeys(name.split(".")[0] for name in self.names))

    def done(self, f, item):
        return f * len(self.order) + self.order.index(item) + 1

    def kept(self, count):
        filled = [self.order[k % len(self.order)] for k in range(count)]
        vector = filled[-1] in self.by_vector
        return vector, sum((item in self.by_vector) == vector for item in filled)


class Chain:

    def __init__(self, engine, semaphore):
        self.engine, self.semaphore, self.count = engine, semaphore, 0

    def step(self, instruction):
        self.count += 1
        instruction.then_inc(self.semaphore, 1)
        self.engine.wait_ge(self.semaphore, self.count)


def stage_end(nc, sems):
    numbers = sorted(s.num for s in sems)
    first = [n for n in numbers if n - 1 not in numbers]
    last = [n for n in numbers if n + 1 not in numbers]
    for lo, hi in zip(first, last):
        nc.gpsimd.sem_clear(range(lo, hi + 1))
    nc.all_engine_barrier()


def make_constants(nc, pool, made, cst):
    ch = Chain(pool, made)
    select = nc.gpsimd.affine_select
    for name, value in (("ident", 1.0), ("centre", 1.0 / P - 1.0)):
        fill = 0.0 if name == "ident" else 1.0 / P
        ch.step(nc.gpsimd.memset(cst[name][:, :], value))
        ch.step(select(out=cst[name][:, :], in_=cst[name][:, :], pattern=[[-1, P]], compare_op=ALU.is_equal,
                       fill=fill, base=0, channel_multiplier=1))
    ch.step(nc.gpsimd.memset(cst["eps"][:, :], EPS))
    ch.step(nc.gpsimd.memset(cst["minus_half"][:, :], -0.5))
    ch.step(nc.gpsimd.memset(cst["mean_col"][:, :], 1.0 / P))
    ch.step(nc.gpsimd.memset(cst["head_sum"][:, :, :], 0.0))
    for h in range(2):
        ch.step(nc.gpsimd.memset(cst["head_sum"][DK * h:DK * h + DK, h, :], 1.0))
    for name in ("same_head", "causal_head"):
        ch.step(nc.gpsimd.memset(cst[name][:, :], -1.0 / DK))
        for i in range(NB):
            rows = slice(BK * H * i, BK * H * (i + 1))
            v = cst[name][rows, :].rearrange("p (i h s) -> p i h s", i=NB, h=H)
            ch.step(select(out=v, in_=v, pattern=[[0, NB], [-BK, H], [0, BK]], compare_op=ALU.is_ge, fill=0.0,
                           base=0, channel_multiplier=1))
            ch.step(select(out=v, in_=v, pattern=[[0, NB], [BK, H], [0, BK]], compare_op=ALU.is_ge, fill=0.0,
                           base=BK - 1, channel_multiplier=-1))
            if name == "causal_head":
                if i:
                    ch.step(nc.gpsimd.memset(v[:, 0:i], 0.0))
                ch.step(select(out=v[:, i], in_=v[:, i], pattern=[[BK, H], [1, BK]], compare_op=ALU.is_ge,
                               fill=0.0, base=0, channel_multiplier=-1))
    ch.step(nc.gpsimd.memset(cst["pair_rows"][:, :], -1.0 / DK))
    for i in range(NB):
        v = cst["pair_rows"][BK * H * i:BK * H * (i + 1), :]
        ch.step(select(out=v, in_=v, pattern=[[-2 * BK, G]], compare_op=ALU.is_ge, fill=0.0, base=0,
                       channel_multiplier=1))
        ch.step(select(out=v, in_=v, pattern=[[2 * BK, G]], compare_op=ALU.is_ge, fill=0.0, base=2 * BK - 1,
                       channel_multiplier=-1))
    ch.step(nc.gpsimd.memset(cst["above_diag"][:, :], 0.0))
    ch.step(select(out=cst["above_diag"][:, :], in_=cst["above_diag"][:, :], pattern=[[-1, P]],
                   compare_op=ALU.is_ge, fill=-1e30, base=0, channel_multiplier=1))
    ch.step(nc.gpsimd.memset(cst["lower"][:, :, :], 1.0))
    ch.step(select(out=cst["lower"][:, :, :], in_=cst["lower"][:, :, :], pattern=[[1, NE], [-1, NE]],
                   compare_op=ALU.is_gt, fill=0.0, base=0, channel_multiplier=0))
    ch.step(nc.gpsimd.memset(cst["ident16"][:, :], 1.0))
    ch.step(select(out=cst["ident16"][:, :], in_=cst["ident16"][:, :], pattern=[[-1, P]],
                   compare_op=ALU.is_equal, fill=0.0, base=0, channel_multiplier=1))


def delta_attention(nc, cst, ps, d, res):
    with ExitStack() as ctx:
        def sb(name, shape, dt=F32):
            return ctx.enter_context(nc.sbuf_tensor(name, shape, dt))

        def sem(name):
            return ctx.enter_context(nc.semaphore(name))

        HB = H * B
        NBLK = TS // BK
        N = B * TS
        HALF = 4 * N
        PAD = TS
        xT = sb("xT", [P, B, PAD + T + TS])
        taps = sb("taps", [P, TAPS, 2 * G * P + H * DV])
        wa = sb("wa", [P, H * DV])
        wg = sb("wg", [P, H * DV])
        wb = sb("wb", [P, H])
        wo = sb("wo", [P, H, C])
        conv_b = sb("conv_b", [P, 2 * G + H])
        bias_a = sb("bias_a", [P, 3, H])
        bias_b = sb("bias_b", [P, 2, H])
        ln_w = sb("ln_w", [P, 1])
        ln_b = sb("ln_b", [P, 1])
        state = sb("state", [P, B, G, DV])
        kq = sb("kq", [P, 2, B, NC, 2, NB, G, 2, BK])
        mt = sb("mt", [P, 2, HB * NBLK, BK, BK])
        load_x, load_w, load_b, cst_made = sem("a_load_x"), sem("a_load_w"), sem("a_load_b"), sem("a_cst_made")
        load_tap = [sem(f"a_load_tap{j}") for j in range(TAPS)]

        with ExitStack() as once:
            wraw = once.enter_context(nc.sbuf_tensor("wraw", [P, 2 * G * P + H * DV], F32))
            wtap = once.enter_context(nc.sbuf_tensor("wtap", [P, TAPS, 2 * G * P + H * DV], F32))
            with nc.Block() as block:
                @block.sync
                def _(sp):
                    for lo, hi, name in ((0, G * P, "WqT"), (G * P, 2 * G * P, "WkT"), (2 * G * P, 2 * G * P + H * DV, "WvT")):
                        sp.dma_start(wraw[:, lo:hi], d[name]).then_inc(load_x, 16)
                    for j in range(TAPS):
                        sp.dma_start(wtap[:, j, :], d["taps"][j, :].partition_broadcast(P)).then_inc(load_tap[j], 16)
                    for dst, src in ((wb[:, :], d["WbT"]), (bias_a[:, 0, :], d["ba"]),
                                     (bias_b[:, 0, :], d["bb"].partition_broadcast(P)), (wo[:, :, :], d["WoT"])):
                        sp.dma_start(dst, src).then_inc(load_b, 16)
                    for b in range(B):
                        sp.dma_start(xT[:, b, PAD:PAD + T], d["xT"][:, b, :]).then_inc(load_w, 16)
                    for dst, src in ((wa[:, :], d["WaT"]), (wg[:, :], d["WgT"]), (conv_b[:, :], d["conv_b"]),
                                     (ln_w[:, :], d["ln_w"]), (ln_b[:, :], d["ln_b"]), (res[:, 1:, :], d["x_tok"])):
                        sp.dma_start(dst, src).then_inc(load_w, 16)
                    sp.wait_ge(load_w, 16 * 8)

                @block.gpsimd
                def _(pool):
                    nc.gpsimd.memset(xT[:, :, 0:PAD], 0.0)
                    nc.gpsimd.memset(xT[:, :, PAD + T:], 0.0)
                    nc.gpsimd.memset(res[:, 0, :], 0.0)
                    make_constants(nc, pool, cst_made, cst)

                @block.vector
                def _(dve):
                    nc.vector.memset(state[:, :, :, :], 0.0)
                    nc.vector.memset(kq[:, :, :, :, :, :, :, :, :].rearrange("p f b c q i g h s -> p (f b c q i g h s)"), 0.0)
                    nc.vector.memset(mt[:, :, :, :, :], 0.0)
                    dve.wait_ge(load_x, 16 * 3)
                    for j in range(TAPS):
                        dve.wait_ge(load_tap[j], 16)
                        nc.vector.tensor_tensor(taps[:, j, :], wraw[:, :], wtap[:, j, :], ALU.mult)
                    dve.wait_ge(load_b, 16 * 4)
                    nc.vector.tensor_scalar(bias_a[:, 1, :], bias_a[:, 0, :], 0.5, None, ALU.mult)
                    nc.vector.tensor_scalar(bias_a[:, 2, :], bias_a[:, 0, :], -1.0, None, ALU.mult)
                    nc.vector.tensor_scalar(bias_b[:, 1, :], bias_b[:, 0, :], 0.5, None, ALU.mult)
                    nc.vector.tensor_scalar(wo[:, :, :], wo[:, :, :], 0.5, None, ALU.mult)

        qk = sb("qk", [P, 2 * G, B, TS])
        vd = sb("vd", [P, 2, H, B, TS])
        th = sb("th", [P, H, B, TS])
        ex = sb("ex", [P, H, B, TS])
        di = sb("di", [P, 3, HB * NC, CH])
        rr = sb("rr", [P, H, B, TS])
        near = sb("near", [P, G, B, NBLK, 6])
        gn = sb("gn", [P, H, B, NBLK, 6])
        tmp = qk[:, :, :, :].rearrange("p g b (n i) -> p (g b n) i", i=BK).rearrange("p m (i j) -> p m i j", i=2)
        gm = sb("gm", [BK * H, 4, NB - 1, P])
        qkm = sb("qkm", [P, 4, P])
        kfull = sb("kfull", [P, 4, G, P])
        last = sb("last", [P, 2, H, DK])
        decay = sb("decay", [P, 4, G, P])
        prod = sb("prod", [P, B, H, BK, BK])
        w = sb("w", [P, B, NB, H, BK])
        wtb = sb("wtb", [BK * H, B, P])
        wtf = sb("wtf", [P, B, P])
        o = vd
        gate = sb("gate", [P, H * N])
        cs = sb("cs", [P, H * N])
        sq = gn[:, :, :, :, :].rearrange("p h b n e -> p (h b n e)")[:, 0:H * N]
        var = sb("var", [P, H])
        rstd = sb("rstd", [P, H])
        yT = sb("yT", [C, N])

        names = ("ring_done ring_act ring_dve near_done copied m_done normed rstd_done gated "
                 "prepared a_made d_done g_ready g_kept q_kept k_kept f_ready f_kept last_done")
        S = {n: sem("a_" + n) for n in names.split()}
        two = lambda n: [sem(f"a_{n}{b}") for b in range(B)]
        z_ready, w_ready, wt_ready, wt_kept = two("z_ready"), two("w_ready"), two("wt_ready"), two("wt_kept")
        p_ready, p_used, s_ready, o_ready, o_kept = (two("p_ready"), two("p_used"), two("s_ready"), two("o_ready"),
                                                     two("o_kept"))
        dve_chain, pool_chain = sem("a_dve_chain"), sem("a_pool_chain")
        every = list(S.values()) + [dve_chain, pool_chain]
        for pair in (z_ready, w_ready, wt_ready, wt_kept, p_ready, p_used, s_ready, o_ready, o_kept):
            every += pair

        BY_DVE = ("rs0", "rs1", "yt")
        BOTH = [[["a0"], ["g0"]], [["a1"], ["a2"]], [["a3"], ["g1"]], [["b0"], ["b1", "b2", "b3"]],
                [["c0"], ["c1"]], [["k0.0"], ["k0.1"]], [["k1.0"], ["k1.1", "var"]], [["q0.0"], ["q0.1"]],
                [["q1.0"], ["q1.1", "rs0"]], [["rs1"], ["n0", "n1"]], [["n2"], ["n3", "v0.0"]], [["v0.1"], ["v1.0"]],
                [["v1.1"], ["v2.0"]], [["v2.1"], ["v3.0"]], [["v3.1"], ["wo.0"]], [["wo.1"], ["yt"]]]
        POST = ("g0", "g1", "c0", "c1", "var", "rs0", "rs1", "wo", "yt")
        both = Ring(BOTH, BY_DVE)
        only_pre = Ring([[[x for x in part if x.split(".")[0] not in POST] for part in slot] for slot in BOTH], BY_DVE)
        only_post = Ring([[[x for x in part if x.split(".")[0] in POST] for part in slot] for slot in BOTH], BY_DVE)

        def columns(n):
            return PAD + n * TS

        def bank(ring, f, item):
            return ps[:, 6 + (ring.done(f, item) - 1) % 2, :]

        def pe_item(pe, ring, f, nx, name, at_next, at_last):
            item, _, half = name.partition(".")
            r = ring.done(f, item)
            out = bank(ring, f, item)
            if r > 2 and half != "1":
                vector, count = ring.kept(r - 2)
                pe.wait_ge(S["ring_dve" if vector else "ring_act"], count)
            kind, j = item[0], item[-1]
            if item == "var":
                for h in range(H):
                    if h == 0:
                        vector, count = ring.kept(ring.done(f, "c1"))
                        pe.wait_ge(S["ring_act"], count)
                    mm = pe.matmul(out[:, h:h + 1], lhsT=sq[:, h * N:(h + 1) * N], rhs=cst["mean_col"][:, :], start=True,
                                   stop=True, skip_group_check=True)
            elif kind == "r":
                pe.wait_ge(S["rstd_done"], f + 1)
                for u in range(4):
                    h = 4 * int(j) + u
                    mm = pe.transpose(out[:, u * P:(u + 1) * P], rstd[:, h:h + 1].to_broadcast([P, P]), cst["ident"][:, :])
            elif item == "wo":
                pe.wait_ge(S["gated"], 2 * f + 2)
                for h in {"": range(H), "0": range(H // 2), "1": range(H // 2, H)}[half]:
                    mm = pe.matmul(out[:, 0:N], lhsT=wo[:, h, :], rhs=cs[:, h * N:(h + 1) * N], start=(h == 0), stop=(h == H - 1))
            elif item == "yt":
                vector, count = ring.kept(ring.done(f, "wo"))
                pe.wait_ge(S["ring_act"], count)
                mm = pe.transpose(out[:, 0:P], yT[:, :], cst["ident"][:, :])
            elif kind == "g":
                x = xT[:, :, bass.ds(columns(at_last), TS)]
                for u in range(4):
                    h = 4 * int(j) + u
                    mm = pe.matmul(out[:, u * N:(u + 1) * N].rearrange("p (b t) -> p b t", b=B), lhsT=wg[:, h * P:(h + 1) * P],
                                   rhs=x, start=True, stop=True, skip_group_check=True)
            elif kind == "c":
                of = o[:, nx, :, :, :].rearrange("p h b t -> p (h b t)")
                mm = pe.matmul(out, lhsT=cst["centre"][:, :], rhs=of[:, int(j) * HALF:(int(j) + 1) * HALF], start=True, stop=True)
            elif kind == "n":
                if j == "0":
                    pe.wait_ge(S["near_done"], 3 * (f + 1))
                for u in range(2):
                    h = 2 * int(j) + u
                    mm = pe.matmul(out[:, u * B * NBLK * 6:(u + 1) * B * NBLK * 6], lhsT=cst["head_sum"][:, h % 2, :],
                                   rhs=near[:, h // 2, :, :, :].rearrange("p b n e -> p (b n e)"), start=True, stop=True,
                                   skip_group_check=True)
            else:
                for u in range(2) if half == "" else [int(half)]:
                    part = out[:, u * N:(u + 1) * N].rearrange("p (b t) -> p b t", b=B)
                    t = 2 * int(j) + u
                    if kind in "qkv":
                        t += {"q": 0, "k": G, "v": 2 * G}[kind]
                        for tap in range(TAPS):
                            mm = pe.matmul(part, lhsT=taps[:, tap, t * P:(t + 1) * P],
                                           rhs=xT[:, :, bass.ds(columns(at_next) - LOOK + tap, TS)], start=(tap == 0),
                                           stop=(tap == TAPS - 1), skip_group_check=True)
                    else:
                        lhs = wa[:, t * P:(t + 1) * P] if kind == "a" else wb[:, t:t + 1].to_broadcast([P, P])
                        mm = pe.matmul(part, lhsT=lhs, rhs=xT[:, :, bass.ds(columns(at_next), TS)], start=True, stop=True,
                                       skip_group_check=True)
            if half != "0":
                mm.then_inc(S["ring_done"], 1)

        def act_item(act, ring, f, nx, name):
            item, _, half = name.partition(".")
            if item in BY_DVE or half == "0":
                return
            act.wait_ge(S["ring_done"], ring.done(f, item))
            out = bank(ring, f, item)
            kind, j = item[0], item[-1]
            run = nc.scalar.activation
            if item == "var":
                last_one = nc.scalar.copy(var[:, :], out[:, 0:H])
            elif item == "wo":
                last_one = nc.scalar.copy(yT[:, :], out[:, 0:N])
            elif kind == "g":
                if f >= 1 and j == "0":
                    act.wait_ge(S["gated"], 2 * f)
                last_one = run(gate[:, int(j) * HALF:(int(j) + 1) * HALF], out, ACT.Tanh, scale=0.5)
            elif kind == "c":
                part = slice(int(j) * HALF, (int(j) + 1) * HALF)
                nc.scalar.copy(cs[:, part], out)
                last_one = run(sq[:, part], out, ACT.Square)
            elif kind == "n":
                size = B * NBLK * 6
                last_one = nc.scalar.mul(gn[:, 2 * int(j):2 * int(j) + 2, :, :, :].rearrange("p h b n e -> p (h b n e)"),
                                         out[:, 0:2 * size], 1.0 / DK)
            else:
                if item == "k0" and f >= 1:
                    act.wait_ge(S["copied"], 16 * f)
                if item == "a0" and f >= 1:
                    act.wait_ge(S["m_done"], f)
                for u in range(2):
                    part = out[:, u * N:(u + 1) * N].rearrange("p (b t) -> p b t", b=B)
                    t = 2 * int(j) + u
                    if kind == "q":
                        last_one = run(qk[:, t, :, :], part, ACT.Silu, bias=conv_b[:, t:t + 1])
                    elif kind == "k":
                        last_one = run(qk[:, G + t, :, :], part, ACT.Silu, bias=conv_b[:, G + t:G + t + 1])
                    elif kind == "v":
                        last_one = run(vd[:, nx, t, :, :], part, ACT.Silu, bias=conv_b[:, 2 * G + t:2 * G + t + 1])
                    elif kind == "b":
                        last_one = run(rr[:, t, :, :], part, ACT.Tanh, bias=bias_b[:, 1, t:t + 1], scale=0.5)
                    else:
                        run(th[:, t, :, :], part, ACT.Tanh, bias=bias_a[:, 1, t:t + 1], scale=0.5)
                        last_one = run(ex[:, t, :, :], part, ACT.Exp, bias=bias_a[:, 2, t:t + 1], scale=-1.0)
            last_one.then_inc(S["ring_act"], 1)

        flat = lambda x: x[:, :, :, :].rearrange("p h b t -> p (h b t)")

        def wait_kept(engine, ring, f, item):
            vector, count = ring.kept(ring.done(f, item))
            engine.wait_ge(S["ring_dve" if vector else "ring_act"], count)

        def dve_slot(dve, ch, ring, f, nx, slot, at_last):
            have = ring.order
            if slot == 9 and "rs0" in have:
                for j in range(2):
                    part = slice(j * HALF, (j + 1) * HALF)
                    dve.wait_ge(S["ring_done"], ring.done(f, f"rs{j}"))
                    nc.vector.tensor_tensor(cs[:, part], cs[:, part], bank(ring, f, f"rs{j}"), ALU.mult).then_inc(S["ring_dve"], 1)
            if slot == 10 and "rs0" in have:
                wait_kept(dve, ring, f, "rs1")
                nc.vector.tensor_scalar(cs[:, :], cs[:, :], ln_w[:, 0:1], ln_b[:, 0:1], ALU.mult, ALU.add).then_inc(S["normed"], 1)
            if "k0" in have and (slot % NB != NB - 1 or ring is only_pre):
                prepare_slot(dve, ch, ring, f, nx, slot)
            if slot == 15 and "yt" in have:
                dve.wait_ge(S["ring_done"], ring.done(f, "yt"))
                tile = res[:, bass.ds(at_last + 1, 1), :]
                nc.vector.tensor_tensor(tile, tile, bank(ring, f, "yt")[:, 0:P].unsqueeze(1), ALU.add).then_inc(S["ring_dve"], 1)

        def prepare_slot(dve, ch, ring, f, nx, slot):
            D, inv = di[:, 2 * nx, :, :], di[:, 1, :, :]
            both_d = di[:, nx:nx + 2, :, :]
            R = rr[:, :, :, :].rearrange("p h b (n i) -> p (h b n) i", i=BK)
            NN = gn[:, :, :, :, :].rearrange("p h b n e -> p (h b n) e")
            M = mt[:, nx, :, :, :].rearrange("p n i j -> p n (i j)")
            t0, t1 = tmp[:, :, 0, :], tmp[:, :, 1, :]
            tt, ts = nc.vector.tensor_tensor, nc.vector.tensor_scalar
            Df, invf = (x.rearrange("p n t -> p (n t)") for x in (D, inv))
            if slot == 3:
                wait_kept(dve, ring, f, "a3")
                ts(flat(th), flat(th), 0.5, 0.5, ALU.mult, ALU.add)
                ch.step(ts(invf, flat(ex), 1.0, None, ALU.add))
                ch.step(tt(Df, flat(th), invf, ALU.mult))
            if slot == 4:
                ch.step(ts(Df, Df, -1.0, 2.0, ALU.mult, ALU.add))
            if slot == 5:
                tt(Df, Df, flat(th), ALU.mult).then_inc(S["a_made"], 1)
            if slot == 7:
                wait_kept(dve, ring, f, "b3")
                ch.step(ts(flat(rr), flat(rr), 0.5, 0.5, ALU.mult, ALU.add))
                ch.step(nc.vector.scalar_tensor_tensor(out=flat(rr), in0=flat(ex), scalar=1.0, in1=flat(rr), op0=ALU.add,
                                                       op1=ALU.mult))
            if slot == 11:
                wait_kept(dve, ring, f, "n3")
                nc.vector.tensor_copy(M[:, :, 0:16:5], R)
                ch.step(tt(NN[:, :, 0:3], NN[:, :, 0:3], R[:, :, 1:4], ALU.mult))
            if slot == 12:
                tt(NN[:, :, 3:5], NN[:, :, 3:5], R[:, :, 2:4], ALU.mult)
                ch.step(tt(NN[:, :, 5:6], NN[:, :, 5:6], R[:, :, 3:4], ALU.mult))
            if slot == 13:
                nc.vector.scalar_tensor_tensor(out=M[:, :, 4:16:5], in0=NN[:, :, 0:3], scalar=-1.0, in1=R[:, :, 0:3],
                                               op0=ALU.mult, op1=ALU.mult)
                dve.wait_ge(S["copied"], 16 * (f + 1))
                ch.step(tt(t0, NN[:, :, 3:5], R[:, :, 0:2], ALU.mult))
            if slot == 14:
                ch.step(tt(t1, NN[:, :, 1:3], M[:, :, 4:10:5], ALU.mult))
                ch.step(nc.vector.scalar_tensor_tensor(out=M[:, :, 8:14:5], in0=t0, scalar=-1.0, in1=t1, op0=ALU.mult,
                                                       op1=ALU.subtract))
                tt(t0[:, :, 0:1], NN[:, :, 5:6], R[:, :, 0:1], ALU.mult)
                ch.step(tt(t0[:, :, 1:2], NN[:, :, 4:5], M[:, :, 4:5], ALU.mult))
            if slot == 15:
                wait_kept(dve, ring, f, "v3")
                dve.wait_ge(S["d_done"], f + 1)
                vv = vd[:, nx, :, :, :].rearrange("p h b (c t) -> p (h b c) t", t=CH)
                tt(vv[:, :, 1:CH], vv[:, :, 1:CH], inv[:, :, 0:CH - 1], ALU.mult).then_inc(S["prepared"], 1)
            if slot == 16:
                ch.step(tt(t1[:, :, 0:1], NN[:, :, 2:3], M[:, :, 8:9], ALU.mult))
                ch.step(tt(t1[:, :, 1:2], t0[:, :, 0:1], t0[:, :, 1:2], ALU.add))
                nc.vector.scalar_tensor_tensor(out=M[:, :, 12:13], in0=t1[:, :, 0:1], scalar=-1.0, in1=t1[:, :, 1:2],
                                               op0=ALU.mult, op1=ALU.subtract).then_inc(S["m_done"], 1)

        def pool_prepare(pool, ring, f, nx, part, ends_before=0):
            if part == "near":
                wait_kept(pool, ring, f, "k1")
                if f >= 1:
                    pool.wait_ge(S["ring_done"], ring.done(f - 1, "n3"))
                kk = qk[:, G:2 * G, :, :].rearrange("p g b (n i) -> p (g b n) i", i=BK)
                nn = near[:, :, :, :, :].rearrange("p g b n e -> p (g b n) e")
                for lo, hi, dist in ((0, 3, 1), (3, 5, 2), (5, 6, 3)):
                    nc.gpsimd.tensor_tensor(nn[:, :, lo:hi], kk[:, :, dist:BK], kk[:, :, 0:BK - dist], ALU.mult).then_inc(
                        S["near_done"], 1)
                return
            h = part
            wait_kept(pool, ring, f, "q1")
            pool.wait_ge(S["near_done"], 3 * (f + 1))
            if ends_before:
                pool.wait_ge(S["last_done"], ends_before)
                pool.wait_ge(S["rstd_done"], f + 1)
            if h:
                pool.wait_ge(S["copied"], 16 * f + 8)
            rows = slice(DK * h, DK * h + DK)
            for i in range(2):
                for g in range(G):
                    src = qk[rows, g + (0 if i else G), :, :].rearrange("p b (c i s) -> p (b c) i s", i=NB, s=BK)
                    dst = kq[rows, nx, :, :, i, :, g, h, :].rearrange("p b c i s -> p (b c) i s")
                    nc.gpsimd.tensor_copy(dst, src).then_inc(S["copied"], 1)
            if h:
                pool.wait_ge(S["copied"], 16 * (f + 1))

        def scan(ch, multiply, f, nx):
            both_d = di[:, nx:nx + 2, :, :]
            ch.engine.wait_ge(S["a_made"], f + 1)
            for t in range(1, CH):
                step = multiply(both_d[:, :, :, t:t + 1], both_d[:, :, :, t - 1:t], both_d[:, :, :, t:t + 1], ALU.mult)
                if t < CH - 1:
                    ch.step(step)
            step.then_inc(S["d_done"], 1)

        def pool_rstd(pool, ch, ring, f):
            wait_kept(pool, ring, f, "var")
            ch.step(nc.gpsimd.tensor_scalar(rstd[:, :], var[:, :], EPS / DK, None, ALU.add))
            nc.gpsimd.tensor_tensor(rstd[:, :], rstd[:, :], cst["minus_half"][:, :], ALU.pow).then_inc(S["rstd_done"], 1)

        def pool_gate(pool, ch, ring, f):
            pool.wait_ge(S["normed"], f + 1)
            ch.step(nc.gpsimd.tensor_scalar(gate[:, :], gate[:, :], 1.0, None, ALU.add))
            for j in range(2):
                part = slice(j * HALF, (j + 1) * HALF)
                nc.gpsimd.tensor_tensor(cs[:, part], cs[:, part], gate[:, part], ALU.mult).then_inc(S["gated"], 1)

        def halves(cc):
            return cc // NC % 2, cc % NC

        def kc(cc, b, i):
            f, c = halves(cc)
            return kq[:, f, b, c, i, :, :, :, :].rearrange("p i g h s -> p (i g h s)")

        def dd_of(f):
            return di[:, 2 * f, :, :].rearrange("p (h b c) (i s) -> p h b c i s", h=H, b=B, s=BK)

        def nth(cc, b, base=B):
            return B * cc + b - base

        def pe_products(pe, cc, b, base=B):
            n, k = nth(cc, b, base), kc(cc, b, 0)
            if cc and cc % NC == 0:
                pe.wait_ge(S["copied"], 16 * (cc // NC))
            if n >= 1:
                pe.wait_ge(S["k_kept"], 4 * n)
            for i in range(NB - 1):
                lo = BK * H * (i + 1)
                pe.matmul(ps[0:BK * H, 5, GM_AT[i]:GM_AT[i] + P - lo], lhsT=k[:, BK * H * i:lo], rhs=k[:, lo:P],
                          start=True, stop=True, skip_group_check=True)
            pe.matmul(ps[:, 5, QK_AT:QK_AT + P], lhsT=k, rhs=kc(cc, b, 1), start=True, stop=True, skip_group_check=True)
            pe.transpose(ps[:, 5, KT_AT:KT_AT + P], k, cst["ident"][:, :]).then_inc(S["g_ready"], 1)

        def pe_decays(pe, cc, b, base=B, finished=(0, 0)):
            n = nth(cc, b, base)
            if n >= 1:
                pe.wait_ge(S["f_kept"], n)
            for bb in range(B):
                if finished[bb]:
                    pe.wait_ge(p_used[bb], finished[bb])
            pe.wait_ge(S["last_done"], n + 1)
            for g in range(G):
                mm = pe.transpose(ps[:, 4, g * P:(g + 1) * P], last[:, b, 2 * g:2 * g + 2, :].rearrange("p h k -> p (h k)"),
                                  cst["ident"][:, :])
            mm.then_inc(S["f_ready"], 1)

        def pool_ends(pool, cc, base=B):
            f, c = halves(cc)
            for b in range(B):
                n = nth(cc, b, base)
                if n >= 2:
                    pool.wait_ge(S["f_ready"], n - 1)
                if cc and c == 0:
                    pool.wait_ge(S["d_done"], cc // NC)
                nc.gpsimd.tensor_copy(last[:, b, :, :], dd_of(f)[:, :, b, c, NB - 1, BK - 1:BK].to_broadcast(
                    [P, H, DK])).then_inc(S["last_done"], 1)

        def act_k_rows(act, cc, b, pairs, base=B):
            n = nth(cc, b, base)
            if 0 in pairs:
                act.wait_ge(S["g_ready"], n + 1)
                act.wait_ge(S["q_kept"], n + 1)
                if cc >= 2:
                    act.wait_ge(p_ready[b], cc - 1)
            for g in pairs:
                nc.scalar.activation(kfull[:, B * (cc % 2) + b, g, :], ps[:, 5, KT_AT:KT_AT + P], ACT.Copy,
                                     scale=cst["pair_rows"][:, g:g + 1]).then_inc(S["k_kept"], 1)

        def act_decays(act, cc, b, base=B):
            n = nth(cc, b, base)
            act.wait_ge(S["f_ready"], n + 1)
            if cc >= 2:
                act.wait_ge(s_ready[b], cc - 1)
            nc.scalar.copy(decay[:, B * (cc % 2) + b, :, :], ps[:, 4, :].rearrange("p (g v) -> p g v", g=G)).then_inc(
                S["f_kept"], 1)

        def dve_masks(dve, cc, b, base=B):
            n = nth(cc, b, base)
            dve.wait_ge(S["g_ready"], n + 1)
            for i in range(NB - 1):
                lo = BK * H * (i + 1)
                mm = nc.vector.tensor_tensor(gm[:, B * (cc % 2) + b, i, lo:P], ps[0:BK * H, 5, GM_AT[i]:GM_AT[i] + P - lo],
                                             cst["same_head"][0:BK * H, lo:P], ALU.mult)
            mm.then_inc(S["g_kept"], 1)
            nc.vector.tensor_tensor(qkm[:, B * (cc % 2) + b, :], ps[:, 5, QK_AT:QK_AT + P], cst["causal_head"][:, :],
                                    ALU.mult).then_inc(S["q_kept"], 1)

        GM_AT = [0, 96, 160]
        QK_AT, KT_AT = 192, 320
        with nc.Block() as block:
            @block.tensor
            def _(pe):
                for item in only_pre.names:
                    pe_item(pe, only_pre, 0, 0, item, 0, 0)
                pe.wait_ge(S["copied"], 16)
                for b in range(B):
                    pe_products(pe, 0, b, 0)
                    pe_decays(pe, 0, b, 0)

            @block.scalar
            def _(act):
                for item in only_pre.order:
                    act_item(act, only_pre, 0, 0, item)
                for b in range(B):
                    act_k_rows(act, 0, b, range(G), 0)
                    act_decays(act, 0, b, 0)

            @block.gpsimd
            def _(pool):
                nc.gpsimd.memset(o[:, 1, :, :, :], 0.0)
                pool_prepare(pool, only_pre, 0, 0, "near")
                pool.wait_ge(S["d_done"], 1)
                pool_ends(pool, 0, 0)
                pool.wait_ge(S["last_done"], B)
                pool_prepare(pool, only_pre, 0, 0, 0)
                pool_prepare(pool, only_pre, 0, 0, 1)

            @block.vector
            def _(dve):
                ch = Chain(dve, dve_chain)
                for slot in range(17):
                    dve_slot(dve, ch, only_pre, 0, 0, slot, 0)
                    if slot == 7:
                        scan(ch, nc.vector.tensor_tensor, 0, 0)
                for b in range(B):
                    dve_masks(dve, 0, b, 0)
        stage_end(nc, every)

        with nc.Fori(0, NS // 2) as it:
            chunks = [(f, c) for f in range(2) for c in range(NC)]

            def z_of(b):
                return ps[:, b, 0:P].rearrange("p (i h s) -> p i h s", i=NB, h=H)

            with nc.Block() as block:
                @block.tensor
                def _(pe):
                    halves_of_v = (slice(0, DV // 2), slice(DV // 2, DV))
                    finished = [0, 0]
                    prepared = [0]

                    def decays(cc, b):
                        pe_decays(pe, cc, b, finished=finished)
                        prepared[0] = nth(cc, b) + 1

                    def start(cc, b):
                        f, c = chunks[cc]
                        if cc >= 1:
                            pe.wait_ge(o_kept[b], cc)
                        vdc = vd[:, f, :, b, :].rearrange("p h (c i s) -> p c i h s", c=NC, s=BK)
                        pe.matmul(z_of(b), lhsT=cst["ident"][:, :], rhs=vdc[:, c], start=True, stop=False,
                                  skip_group_check=True)
                        if cc >= 1:
                            pe.wait_ge(s_ready[b], cc)
                        zo = ps[:, b, 0:2 * P].rearrange("p (i g e) -> p i g e", i=2 * NB, g=G)
                        for g in range(G):
                            for half in halves_of_v:
                                mm = pe.matmul(zo[half, :, g, :], lhsT=state[:, b, g, half],
                                               rhs=kq[:, f, b, c, :, :, g, :, :].rearrange("p q i h s -> p (q i) (h s)"),
                                               start=False, stop=(g == G - 1), skip_group_check=True)
                        mm.then_inc(z_ready[b], 1)

                    def turn(cc, b, i):
                        pe.wait_ge(w_ready[b], NB * cc + i + 1)
                        if i < NB - 1:
                            pe.transpose(ps[0:BK * H, 2 + b, 0:P], w[:, b, i, :, :].rearrange("p h s -> p (h s)"),
                                         cst["ident"][:, :]).then_inc(wt_ready[b], 1)
                        else:
                            pe.transpose(ps[:, 2 + b, P:2 * P], w[:, b, :, :, :].rearrange("p i h s -> p (i h s)"),
                                         cst["ident"][:, :]).then_inc(wt_ready[b], 1)

                    def take_off(cc, b, i):
                        n = B * cc + b
                        pe.wait_ge(wt_kept[b], NB * cc + i + 1)
                        if i == 0 and cc >= 1:
                            pe.wait_ge(S["g_kept"], nth(cc, b) + 1)
                        lo = BK * H * (i + 1)
                        for half in halves_of_v:
                            mm = pe.matmul(ps[half, b, lo:P], lhsT=wtb[:, b, half], rhs=gm[:, n % 4, i, lo:P], start=False,
                                           stop=True, skip_group_check=True)
                        mm.then_inc(z_ready[b], 1)

                    def finish(cc, b):
                        n = B * cc + b
                        pe.wait_ge(wt_kept[b], NB * (cc + 1))
                        if cc >= 1:
                            pe.wait_ge(S["k_kept"], 4 * (nth(cc, b) + 1))
                        pe.wait_ge(S["f_kept"], prepared[0])
                        for bb in range(B):
                            if finished[bb]:
                                pe.wait_ge(p_used[bb], finished[bb])
                        for g in range(G):
                            mm = pe.matmul(ps[:, 4, g * P:(g + 1) * P], lhsT=kfull[:, n % 4, g, :], rhs=wtf[:, b, :],
                                           start=True, stop=True, skip_group_check=True)
                        mm.then_inc(p_ready[b], 1)
                        finished[b] = cc + 1
                        if cc >= 1:
                            pe.wait_ge(S["q_kept"], nth(cc, b) + 1)
                        pe.matmul(ps[:, b, P:2 * P], lhsT=wtf[:, b, :], rhs=qkm[:, n % 4, :], start=False, stop=True,
                                  skip_group_check=True).then_inc(o_ready[b], 1)

                    for cc, (f, c) in enumerate(chunks):
                        def ring(i, part):
                            for item in both.slots[NB * c + i][part]:
                                pe_item(pe, both, f, 1 - f, item, 2 * it + f + 1, 2 * it + f - 1)

                        if c == 0 and f == 1:
                            pe.wait_ge(S["prepared"], f)
                        start(cc, 0)
                        ring(0, 0)
                        start(cc, 1)
                        turn(cc, 0, 0)
                        ring(0, 1)
                        turn(cc, 1, 0)
                        take_off(cc, 0, 0)
                        pe_products(pe, cc + 1, 0)
                        turn(cc, 0, 1)
                        take_off(cc, 1, 0)
                        ring(1, 0)
                        turn(cc, 1, 1)
                        take_off(cc, 0, 1)
                        ring(1, 1)
                        decays(cc + 1, 0)
                        turn(cc, 0, 2)
                        take_off(cc, 1, 1)
                        ring(2, 0)
                        turn(cc, 1, 2)
                        take_off(cc, 0, 2)
                        pe_products(pe, cc + 1, 1)
                        ring(2, 1)
                        decays(cc + 1, 1)
                        turn(cc, 0, 3)
                        take_off(cc, 1, 2)
                        ring(3, 0)
                        turn(cc, 1, 3)
                        finish(cc, 0)
                        ring(3, 1)
                        finish(cc, 1)

                @block.gpsimd
                def _(pool):
                    ch = Chain(pool, pool_chain)

                    for f in range(2):
                        cc = NC * f
                        pool_ends(pool, cc + 1)
                        pool_ends(pool, cc + 2)
                        scan(ch, nc.gpsimd.tensor_tensor, f, 1 - f)
                        pool_prepare(pool, both, f, 1 - f, "near")
                        pool_rstd(pool, ch, both, f)
                        pool_ends(pool, cc + 3)
                        pool_prepare(pool, both, f, 1 - f, 0, nth(cc + 4, 0))
                        pool_prepare(pool, both, f, 1 - f, 1)
                        pool_ends(pool, cc + 4)
                        pool_gate(pool, ch, both, f)

                @block.scalar
                def _(act):
                    def keep(cc, b, i):
                        act.wait_ge(wt_ready[b], NB * cc + i + 1)
                        if i < NB - 1:
                            nc.scalar.copy(wtb[:, b, :], ps[0:BK * H, 2 + b, 0:P]).then_inc(wt_kept[b], 1)
                        else:
                            if cc >= 1:
                                act.wait_ge(o_ready[b], cc)
                            nc.scalar.copy(wtf[:, b, :], ps[:, 2 + b, P:2 * P]).then_inc(wt_kept[b], 1)

                    for cc, (f, c) in enumerate(chunks):
                        def ring(i, part):
                            for item in both.slots[NB * c + i][part]:
                                act_item(act, both, f, 1 - f, item)

                        ring(0, 0)
                        keep(cc, 0, 0)
                        ring(0, 1)
                        keep(cc, 1, 0)
                        keep(cc, 0, 1)
                        act_k_rows(act, cc + 1, 0, (0, 1))
                        ring(1, 0)
                        keep(cc, 1, 1)
                        act_k_rows(act, cc + 1, 0, (2, 3))
                        ring(1, 1)
                        act_decays(act, cc + 1, 0)
                        keep(cc, 0, 2)
                        ring(2, 0)
                        keep(cc, 1, 2)
                        ring(2, 1)
                        act_decays(act, cc + 1, 1)
                        keep(cc, 0, 3)
                        act_k_rows(act, cc + 1, 1, (0, 1))
                        ring(3, 0)
                        keep(cc, 1, 3)
                        act_k_rows(act, cc + 1, 1, (2, 3))
                        ring(3, 1)

                @block.vector
                def _(dve):
                    ch = Chain(dve, dve_chain)

                    def solve(cc, b, i):
                        f, c = chunks[cc]
                        dve.wait_ge(z_ready[b], NB * cc + i + 1)
                        if f and c == 0 and i == 0:
                            dve.wait_ge(S["m_done"], f)
                        zi = z_of(b)[:, i].unsqueeze(2).to_broadcast([P, H, BK, BK])
                        mtc = mt[:, f, :, :, :].rearrange("p (h b n) i j -> p h b n i j", h=H, b=B)
                        ch.step(nc.vector.tensor_tensor(prod[:, b, :, :, :], zi, mtc[:, :, b, NB * c + i, :, :], ALU.mult))
                        if i == 0 and cc >= 1:
                            dve.wait_ge(wt_ready[b], NB * cc)
                        nc.vector.tensor_reduce(w[:, b, i, :, :], prod[:, b, :, :, :], axis=AX.X,
                                                op=ALU.add).then_inc(w_ready[b], 1)

                    def update(cc, b):
                        f, c = chunks[cc]
                        n = B * cc + b
                        dve.wait_ge(p_ready[b], cc + 1)
                        nc.vector.tensor_tensor(state[:, b, :, :], ps[:, 4, :].rearrange("p (g v) -> p g v", g=G),
                                                state[:, b, :, :], ALU.add).then_inc(p_used[b], 1)
                        dve.wait_ge(p_used[b], cc + 1)
                        if cc >= 1:
                            dve.wait_ge(S["f_kept"], nth(cc, b) + 1)
                        nc.vector.tensor_tensor(state[:, b, :, :], state[:, b, :, :], decay[:, n % 4, :, :],
                                                ALU.mult).then_inc(s_ready[b], 1)
                        dve.wait_ge(o_ready[b], cc + 1)
                        oc = o[:, f, :, b, :].rearrange("p h (c i s) -> p c h i s", c=NC, s=BK)
                        nc.vector.tensor_tensor(oc[:, c], ps[:, b, P:2 * P].rearrange("p (i h s) -> p h i s", i=NB, h=H),
                                                dd_of(f)[:, :, b, c], ALU.mult).then_inc(o_kept[b], 1)

                    for cc, (f, c) in enumerate(chunks):
                        def work(i):
                            dve_slot(dve, ch, both, f, 1 - f, NB * c + i, 2 * it + f - 1)

                        solve(cc, 0, 0)
                        solve(cc, 1, 0)
                        work(0)
                        solve(cc, 0, 1)
                        dve_masks(dve, cc + 1, 0)
                        solve(cc, 1, 1)
                        work(1)
                        solve(cc, 0, 2)
                        solve(cc, 1, 2)
                        work(2)
                        solve(cc, 0, 3)
                        dve_masks(dve, cc + 1, 1)
                        solve(cc, 1, 3)
                        prepare_slot(dve, ch, both, f, 1 - f, NB * c + NB - 1)
                        update(cc, 0)
                        update(cc, 1)
                        work(3)
                        if c == NC - 1:
                            prepare_slot(dve, ch, both, f, 1 - f, 16)
            stage_end(nc, every)

        with nc.Block() as block:
            @block.tensor
            def _(pe):
                for item in only_post.names:
                    pe_item(pe, only_post, 0, 1, item, 0, NS - 1)

            @block.scalar
            def _(act):
                for item in only_post.order:
                    act_item(act, only_post, 0, 1, item)

            @block.gpsimd
            def _(pool):
                ch = Chain(pool, pool_chain)
                pool_rstd(pool, ch, only_post, 0)
                pool_gate(pool, ch, only_post, 0)

            @block.vector
            def _(dve):
                ch = Chain(dve, dve_chain)
                for slot in range(16):
                    dve_slot(dve, ch, only_post, 0, 1, slot, NS - 1)


def layer_norm(nc, ctx, cst, ps, res, xT, name, loads=(), arrived=(), out=None):
    GT = 4
    groups = range(NT // GT)
    with ExitStack() as own:
        def sb(n, shape, dt=F32):
            return own.enter_context(nc.sbuf_tensor(f"{name}_{n}", shape, dt))
        total, mean, var, std = (sb(n, [P, NT]) for n in ("total", "mean", "var", "std"))
        sq = sb("sq", [P, NT, C])
        centred, squared, summed, rooted, done, turned, stored, chain = (
            ctx.enter_context(nc.semaphore(f"{name}_{n}")) for n in
            ("centred", "squared", "summed", "rooted", "done", "turned", "stored", "chain"))
        wide = [P, GT, C]

        def of(x, g):
            return x[:, GT * g:GT * g + GT]

        with nc.Block() as block:
            @block.sync
            def _(sp):
                for semaphore, pairs in loads:
                    for dst, src in pairs:
                        sp.dma_start(dst, src).then_inc(semaphore, 16)
                for semaphore, transfers in arrived:
                    sp.wait_ge(semaphore, 16 * transfers)
                if out is not None:
                    for g in groups:
                        sp.wait_ge(done, g + 1)
                        sp.dma_start(of(out, g), of(res, g)).then_inc(stored, 16)
                    sp.wait_ge(stored, 16 * len(groups))

            @block.vector
            def _(dve):
                ch = Chain(dve, chain)
                for g in groups:
                    ch.step(nc.vector.tensor_reduce(of(total, g), of(res, g), axis=AX.X, op=ALU.add))
                    ch.step(nc.vector.tensor_scalar(of(mean, g), of(total, g), 1.0 / C, None, ALU.mult))
                    nc.vector.tensor_tensor(of(res, g), of(res, g), of(mean, g).unsqueeze(2).to_broadcast(wide),
                                            ALU.subtract).then_inc(centred, 1)
                for g in groups:
                    dve.wait_ge(squared, g + 1)
                    nc.vector.tensor_reduce(of(var, g), of(sq, g), axis=AX.X, op=ALU.add).then_inc(summed, 1)
                for g in groups:
                    dve.wait_ge(rooted, g + 1)
                    ch.step(nc.vector.reciprocal(of(std, g), of(std, g)))
                    nc.vector.tensor_tensor(of(res, g), of(res, g), of(std, g).unsqueeze(2).to_broadcast(wide),
                                            ALU.mult).then_inc(done, 1)

            @block.scalar
            def _(act):
                for g in groups:
                    act.wait_ge(centred, g + 1)
                    nc.scalar.activation(of(sq, g), of(res, g), ACT.Square).then_inc(squared, 1)
                for g in groups:
                    act.wait_ge(summed, g + 1)
                    nc.scalar.activation(of(std, g), of(var, g), ACT.Sqrt, bias=cst["eps"][:, 0:1], scale=1.0 / C).then_inc(
                        rooted, 1)
                if xT is not None:
                    for g in groups:
                        act.wait_ge(turned, g + 1)
                        nc.scalar.copy(xT[:, g * GT * P:(g + 1) * GT * P], ps[:, g, :])

            @block.tensor
            def _(pe):
                if xT is not None:
                    for g in groups:
                        pe.wait_ge(done, g + 1)
                        for t in range(GT):
                            mm = pe.transpose(ps[:, g, t * P:(t + 1) * P], res[:, GT * g + t, :], cst["ident"][:, :])
                        mm.then_inc(turned, 1)


NE = 8
TOP = 2


def route(nc, ctx, cst, ps, xT, wr, bias, comb, name):
    with ExitStack() as own:
        def sb(n, shape):
            return own.enter_context(nc.sbuf_tensor(f"{name}_{n}", shape, F32))
        score, shifted, part = sb("score", [P, NT, NE]), sb("shifted", [P, NT, NE]), sb("part", [P, NT, NE])
        above, equal = sb("above", [P, NT, NE, NE]), sb("equal", [P, NT, NE, NE])
        rank, total = sb("rank", [P, NT, NE]), sb("total", [P, NT])
        logits, scored, shift_done, exp_done, chain = (ctx.enter_context(nc.semaphore(f"{name}_{n}")) for n in
                                                       ("logits", "scored", "shift_done", "exp_done", "chain"))
        out = ps[:, 7, 0:NT * NE].rearrange("p (n e) -> p n e", n=NT)
        square = [P, NT, NE, NE]
        with nc.Block() as block:
            @block.tensor
            def _(pe):
                for n in range(NT):
                    mm = pe.matmul(out[:, n, :], lhsT=xT[:, n * P:(n + 1) * P], rhs=wr[:, :], start=True, stop=True,
                                   skip_group_check=True)
                mm.then_inc(logits, 1)

            @block.scalar
            def _(act):
                if bias is None:
                    act.wait_ge(logits, 1)
                    nc.scalar.activation(score[:, :, :], out, ACT.Sigmoid).then_inc(scored, 1)
                else:
                    act.wait_ge(shift_done, 1)
                    nc.scalar.activation(part[:, :, :], shifted[:, :, :], ACT.Exp).then_inc(exp_done, 1)

            @block.vector
            def _(dve):
                ch = Chain(dve, chain)
                if bias is None:
                    dve.wait_ge(scored, 1)
                    value = score
                else:
                    dve.wait_ge(logits, 1)
                    ch.step(nc.vector.tensor_tensor(score[:, :, :], out, bias[:, :].unsqueeze(1).to_broadcast([P, NT, NE]), ALU.add))
                    ch.step(nc.vector.tensor_reduce(total[:, :], score[:, :, :], axis=AX.X, op=ALU.max))
                    nc.vector.tensor_tensor(shifted[:, :, :], score[:, :, :], total[:, :].unsqueeze(2).to_broadcast([P, NT, NE]),
                                            ALU.subtract).then_inc(shift_done, 1)
                    value = part
                other = score[:, :, :].unsqueeze(2).to_broadcast(square)
                mine = score[:, :, :].unsqueeze(3).to_broadcast(square)
                nc.vector.tensor_tensor(above[:, :, :, :], other, mine, ALU.is_gt)
                ch.step(nc.vector.tensor_tensor(equal[:, :, :, :], other, mine, ALU.is_equal))
                ch.step(nc.vector.tensor_tensor(equal[:, :, :, :], equal[:, :, :, :],
                                                cst["lower"][:, :, :].unsqueeze(1).to_broadcast(square), ALU.mult))
                ch.step(nc.vector.tensor_tensor(above[:, :, :, :], above[:, :, :, :], equal[:, :, :, :], ALU.add))
                ch.step(nc.vector.tensor_reduce(rank[:, :, :], above[:, :, :, :], axis=AX.X, op=ALU.add))
                ch.step(nc.vector.tensor_scalar(rank[:, :, :], rank[:, :, :], TOP - 0.5, None, ALU.is_lt))
                if bias is not None:
                    dve.wait_ge(exp_done, 1)
                ch.step(nc.vector.tensor_tensor(comb[:, :, :], rank[:, :, :], value[:, :, :], ALU.mult))
                ch.step(nc.vector.tensor_reduce(total[:, :], comb[:, :, :], axis=AX.X, op=ALU.add))
                if bias is None:
                    ch.step(nc.vector.tensor_scalar(total[:, :], total[:, :], 1e-20, None, ALU.add))
                ch.step(nc.vector.reciprocal(total[:, :], total[:, :]))
                ch.step(nc.vector.tensor_tensor(comb[:, :, :], comb[:, :, :], total[:, :].unsqueeze(2).to_broadcast([P, NT, NE]),
                                                ALU.mult))


def experts(nc, ctx, cst, ps, xT, res, comb, w1, w2, widths, b1, b2, name):
    tiles = [w // P for w in widths]
    first = [sum(tiles[:e]) for e in range(NE + 1)]
    most = max(tiles)
    QT = 4
    PASSES = 2
    with ExitStack() as own:
        def sb(n, shape):
            return own.enter_context(nc.sbuf_tensor(f"{name}_{n}", shape, F32))
        hT = sb("hT", [P, 2, most, 512])
        relu = sb("relu", [P, 2, 512])
        acc = sb("acc", [P, QT, C])
        now = sb("now", [P, PASSES, QT, NE])
        nowT = sb("nowT", [NE, QT, P])
        sems = {n: ctx.enter_context(nc.semaphore(f"{name}_{n}")) for n in
                "up rect_a rect_v relu_done kept_v down added start turned turned_kept bias_done chain".split()}
        total = first[NE]
        squared = b1 is None
        with nc.Fori(0, NT // QT // PASSES) as it:
            def part(s):
                return PASSES * it + s

            def hidden(E):
                s, e = divmod(E, NE)
                return [(m, s * total + m) for m in range(first[e], first[e + 1])]

            def hidden_until(E):
                return E // NE * total + first[E % NE + 1]

            with nc.Block() as block:
                @block.tensor
                def _(pe):
                    def up(E):
                        for m, M in hidden(E):
                            if M >= 4:
                                if squared:
                                    pe.wait_ge(sems["rect_v"], M - 3)
                                else:
                                    pe.wait_ge(sems["rect_v" if m % 2 else "rect_a"], (M - 4) // 2 + 1)
                            pe.matmul(ps[:, m % 4, :], lhsT=w1[:, m * P:(m + 1) * P], rhs=xT[:, bass.ts(part(E // NE), 512)],
                                      start=True, stop=True).then_inc(sems["up"], 1)

                    def down(E):
                        e = E % NE
                        if squared:
                            pe.wait_ge(sems["rect_v"], hidden_until(E))
                        else:
                            pe.wait_ge(sems["rect_a"], (hidden_until(E) + 1) // 2)
                            pe.wait_ge(sems["rect_v"], hidden_until(E) // 2)
                        if E >= 2:
                            pe.wait_ge(sems["added"], QT * (E - 1))
                        for t in range(QT):
                            for j in range(tiles[e]):
                                mm = pe.matmul(ps[:, 4 + e % 2, t * P:(t + 1) * P], lhsT=hT[:, e % 2, j, t * P:(t + 1) * P],
                                               rhs=w2[:, first[e] + j, :], start=(j == 0), stop=(j == tiles[e] - 1),
                                               skip_group_check=True)
                        mm.then_inc(sems["down"], 1)

                    def bias(s):
                        pe.wait_ge(sems["start"], 1)
                        for t in range(QT):
                            mm = pe.transpose(ps[0:NE, 6, t * P:(t + 1) * P], now[:, s, t, :], cst["ident"][:, :])
                        mm.then_inc(sems["turned"], 1)
                        pe.wait_ge(sems["turned_kept"], s + 1)
                        for t in range(QT):
                            mm = pe.matmul(ps[:, 7, t * P:(t + 1) * P], lhsT=nowT[:, t, :], rhs=b2[:, :], start=True, stop=True,
                                           skip_group_check=True)
                        mm.then_inc(sems["bias_done"], 1)

                    up(0)
                    if not squared:
                        bias(0)
                    for E in range(PASSES * NE):
                        if E + 1 < PASSES * NE:
                            up(E + 1)
                            if (E + 1) % NE == 0 and not squared:
                                bias((E + 1) // NE)
                        down(E)

                def place(e, m):
                    return hT[:, e % 2, m - first[e], :]

                @block.scalar
                def _(act):
                    for E in range(PASSES * NE):
                        e = E % NE
                        if e == 0 and not squared:
                            act.wait_ge(sems["turned"], E // NE + 1)
                            nc.scalar.copy(nowT[:, :, :], ps[0:NE, 6, :].rearrange("p (t e) -> p t e", t=QT)).then_inc(
                                sems["turned_kept"], 1)
                        for m, M in hidden(E):
                            if squared:
                                act.wait_ge(sems["up"], M + 1)
                                if M >= 2:
                                    act.wait_ge(sems["rect_v"], M - 1)
                                nc.scalar.activation(relu[:, m % 2, :], ps[:, m % 4, :], ACT.Relu).then_inc(sems["relu_done"], 1)
                            elif m % 2 == 0:
                                act.wait_ge(sems["up"], M + 1)
                                if E >= 2:
                                    act.wait_ge(sems["down"], E - 1)
                                nc.scalar.activation(place(e, m), ps[:, m % 4, :], ACT.Relu, bias=b1[:, m:m + 1]).then_inc(
                                    sems["rect_a"], 1)

                @block.vector
                def _(dve):
                    ch = Chain(dve, sems["chain"])

                    def rectify(E):
                        e = E % NE
                        for m, M in hidden(E):
                            if not squared and m % 2 == 0:
                                continue
                            if E >= 2:
                                dve.wait_ge(sems["down"], E - 1)
                            if squared:
                                dve.wait_ge(sems["relu_done"], M + 1)
                                nc.vector.tensor_tensor(place(e, m), ps[:, m % 4, :], relu[:, m % 2, :], ALU.mult).then_inc(
                                    sems["rect_v"], 1)
                            else:
                                dve.wait_ge(sems["up"], M + 1)
                                nc.vector.tensor_scalar(place(e, m), ps[:, m % 4, :], b1[:, m:m + 1], 0.0, ALU.add,
                                                        ALU.max).then_inc(sems["rect_v"], 1)

                    def begin(s):
                        mine = res[:, bass.ts(part(s), QT), :]
                        if squared:
                            ch.step(nc.vector.tensor_copy(acc[:, :, :], mine))
                        else:
                            dve.wait_ge(sems["bias_done"], s + 1)
                            ch.step(nc.vector.tensor_tensor(acc[:, :, :], mine, ps[:, 7, :].rearrange("p (t c) -> p t c", t=QT),
                                                            ALU.add))

                    nc.vector.tensor_copy(now[:, :, :, :], comb[:, bass.ts(it, PASSES * QT), :].rearrange(
                        "p (s t) e -> p s t e", s=PASSES)).then_inc(sems["start"], 1)
                    dve.wait_ge(sems["start"], 1)
                    rectify(0)
                    begin(0)
                    for E in range(PASSES * NE):
                        s, e = divmod(E, NE)
                        if E + 1 < PASSES * NE:
                            rectify(E + 1)
                        dve.wait_ge(sems["down"], E + 1)
                        if E >= 1:
                            dve.wait_ge(sems["added"], QT * E)
                        for t in range(QT):
                            nc.vector.scalar_tensor_tensor(out=acc[:, t, :], in0=ps[:, 4 + e % 2, t * P:(t + 1) * P],
                                                           scalar=now[:, s, t, e:e + 1], in1=acc[:, t, :], op0=ALU.mult,
                                                           op1=ALU.add).then_inc(sems["added"], 1)
                        if e == NE - 1:
                            dve.wait_ge(sems["added"], QT * (E + 1))
                            ch.step(nc.vector.tensor_copy(res[:, bass.ts(part(s), QT), :], acc[:, :, :]))
                            if s + 1 < PASSES:
                                begin(s + 1)
            stage_end(nc, list(sems.values()))


AH, AD = 16, 64
NP = AH // 2
TT = T // P


def softmax_attention(nc, ctx, cst, ps, weights, xT, yT):
    with ExitStack() as own:
        def sb(n, shape, dt=F32):
            return own.enter_context(nc.sbuf_tensor("b_" + n, shape, dt))

        def sem(n):
            return ctx.enter_context(nc.semaphore("b_" + n))

        HD = AH * AD
        wdown, wq, wkv = weights
        latT = sb("latT", [P, B * T])
        pair_w = sb("pair_w", [P, 2, 3, P])
        qT, kT = sb("qT", [P, 2, B * T]), sb("kT", [P, 2, B * T])
        v = sb("v", [P, 2, NT, P])
        prob = sb("prob", [P, 2, T])
        probT = sb("probT", [P, 4, TT, P])
        nmax, total, inv = sb("nmax", [P, 4]), sb("total", [P, 4, 2]), sb("inv", [P, 4, 2])
        spread = sb("spread", [P, 2, 2, AD])
        recipT = sb("recipT", [P, 2, P])
        x_row = xT[:, :].rearrange("c (n b t) -> c b n t", b=B, t=TS)
        y_row = yT[:, :, :].rearrange("c m (n b t) -> c m b n t", b=B, t=TS)
        lat_kept, lat_done = sem("lat_kept"), sem("lat_done")
        names = ("picked piece_done piece_kept_a piece_kept_v s_done max_done exp_done pt_done pt_kept_v pt_kept_a "
                 "recip_done spread_done o_done recip_kept y_done")
        sems = {n: sem(n) for n in names.split()}

        PIECES = [(kind, m) for kind in ("q", "k", "v") for m in range(4)]

        def project(pe, bank, f, piece):
            kind, m = piece
            if kind == "q":
                return pe.matmul(bank, lhsT=pair_w[:, f, 0, :], rhs=x_row[:, m // 2, 8 * (m % 2):8 * (m % 2) + 8, :],
                                 start=True, stop=True)
            if kind == "k":
                return pe.matmul(bank, lhsT=pair_w[:, f, 1, :], rhs=latT[:, m * 512:(m + 1) * 512], start=True, stop=True)
            for t in range(4):
                n = 4 * m + t
                mm = pe.matmul(bank[:, t * P:(t + 1) * P], lhsT=latT[:, n * P:(n + 1) * P], rhs=pair_w[:, f, 2, :],
                               start=True, stop=True, skip_group_check=True)
            return mm

        def keep_qk(bank, f, piece):
            kind, m = piece
            if kind == "q":
                return nc.scalar.mul(qT[:, f, m * 512:(m + 1) * 512], bank, AD ** -0.5)
            return nc.scalar.copy(kT[:, f, m * 512:(m + 1) * 512], bank)

        def keep_v(bank, f, piece):
            m = piece[1]
            return nc.vector.tensor_copy(v[:, f, 4 * m:4 * m + 4, :], bank.rearrange("p (t c) -> p t c", t=4))

        def pick(hp, f):
            for j, (w, at) in enumerate(((wq, 0), (wkv, 0), (wkv, HD))):
                nc.gpsimd.tensor_copy(pair_w[:, f, j, :], w[:, bass.ds(hp * P + at, P)] if not isinstance(hp, int) else
                                      w[:, hp * P + at:hp * P + at + P]).then_inc(sems["picked"], 1)

        with nc.Block() as block:
            @block.gpsimd
            def _(pool):
                nc.gpsimd.memset(wq[:, HD:], 0.0)
                nc.gpsimd.memset(wkv[:, 2 * HD:], 0.0)
                pick(0, 0)

            @block.tensor
            def _(pe):
                for m in range(4):
                    pe.matmul(ps[:, m, :], lhsT=wdown[:, :], rhs=x_row[:, m // 2, 8 * (m % 2):8 * (m % 2) + 8, :], start=True,
                              stop=True).then_inc(lat_done, 1)
                pe.wait_ge(sems["picked"], 3)
                for n, piece in enumerate(PIECES):
                    if n == 4:
                        pe.wait_ge(lat_kept, 4)
                    if n >= 8:
                        pe.wait_ge(sems["piece_kept_a"], n - 7)
                    project(pe, ps[:, (n + 4) % 8, :], 0, piece).then_inc(sems["piece_done"], 1)

            @block.scalar
            def _(act):
                for m in range(4):
                    act.wait_ge(lat_done, m + 1)
                    nc.scalar.copy(latT[:, m * 512:(m + 1) * 512], ps[:, m, :]).then_inc(lat_kept, 1)
                for n, piece in enumerate(PIECES[:8]):
                    act.wait_ge(sems["piece_done"], n + 1)
                    keep_qk(ps[:, (n + 4) % 8, :], 0, piece).then_inc(sems["piece_kept_a"], 1)

            @block.vector
            def _(dve):
                for n, piece in list(enumerate(PIECES))[8:]:
                    dve.wait_ge(sems["piece_done"], n + 1)
                    keep_v(ps[:, (n + 4) % 8, :], 0, piece)
        stage_end(nc, list(sems.values()))

        order = [i for k in range(TT // 2) for i in (TT - 1 - k, k)]
        pairs = [(f, b, i) for f in range(2) for b in range(B) for i in order]
        W = len(pairs)
        U = 2 * W
        UF = U // 2
        at_step = {f * UF + 2 + 2 * n: (f, n) for f in range(2) for n in range(len(PIECES))}

        def tiles(u):
            return pairs[u // 2][2] + 1

        two_chunks = [sum(tiles(x) > 4 for x in range(u + 1)) for u in range(U)]

        def turned(u):
            return u + 1 + two_chunks[u]

        with nc.Fori(0, NP // 2) as it:
            with nc.Block() as block:
                @block.gpsimd
                def _(pool):
                    pick(2 * it + 1, 1)
                    for w in range(W):
                        if w == W // 2:
                            pick(2 * it + 2, 0)
                        pool.wait_ge(sems["recip_done"], w + 1)
                        if w >= 2:
                            pool.wait_ge(sems["o_done"], w - 1)
                        nc.gpsimd.tensor_copy(spread[:, w % 2, :, :], inv[:, w % 4, :].unsqueeze(2).to_broadcast(
                            [P, 2, AD])).then_inc(sems["spread_done"], 1)

                @block.tensor
                def _(pe):
                    def scores(u):
                        f, b, i = pairs[u // 2]
                        h = u % 2
                        if u == UF:
                            pe.wait_ge(sems["piece_kept_a"], 8)
                        if u >= 2:
                            pe.wait_ge(sems["exp_done"], u - 1)
                        rows = slice(AD * h, AD * h + AD)
                        n = tiles(u) * P
                        for c0 in range(0, n, 512):
                            c1 = min(n, c0 + 512)
                            last = c1 == n
                            bank = ps[:, 2 * (u % 2) + c0 // 512, :]
                            mm = pe.matmul(bank[:, 0:c1 - c0], lhsT=qT[rows, f, b * T + i * P:b * T + (i + 1) * P],
                                           rhs=kT[rows, f, b * T + c0:b * T + c1], start=True, stop=not last,
                                           skip_group_check=True)
                            if last:
                                mm = pe.matmul(bank[:, c1 - c0 - P:c1 - c0], lhsT=cst["ident16"][:, :],
                                               rhs=cst["above_diag"][:, :], start=False, stop=True, skip_group_check=True)
                        mm.then_inc(sems["s_done"], 1)

                    def piece(u):
                        f, n = at_step[u]
                        if n == 0:
                            pe.wait_ge(sems["picked"], 3 * (f + 1))
                        a, vv = 8 * f + min(n, 8), 4 * f + max(n - 8, 0)
                        if n > 8 or (n == 0 and f):
                            pe.wait_ge(sems["piece_kept_v"], vv)
                        elif a:
                            pe.wait_ge(sems["piece_kept_a"], a)
                        project(pe, ps[:, 7, :], 1 - f, PIECES[n]).then_inc(sems["piece_done"], 1)

                    def turn(u):
                        pe.wait_ge(sems["exp_done"], u + 1)
                        if u >= 1:
                            pe.wait_ge(sems["pt_kept_v"], u)
                        for j in range(tiles(u)):
                            if j == 4 and two_chunks[u] > 1:
                                pe.wait_ge(sems["pt_kept_a"], two_chunks[u] - 1)
                            mm = pe.transpose(ps[:, 4 + j // 4, (j % 4) * P:(j % 4 + 1) * P], prob[:, u % 2, j * P:(j + 1) * P],
                                              cst["ident"][:, :])
                            if j == min(4, tiles(u)) - 1 or j == tiles(u) - 1:
                                mm.then_inc(sems["pt_done"], 1)

                    def values(w):
                        f, b, i = pairs[w]
                        pe.wait_ge(sems["pt_kept_v"], 2 * w + 2)
                        if tiles(2 * w) > 4:
                            pe.wait_ge(sems["pt_kept_a"], two_chunks[2 * w + 1])
                        if w == W // 2:
                            pe.wait_ge(sems["piece_kept_v"], 4)
                        if w >= 1:
                            pe.wait_ge(sems["y_done"], w)
                        for j in range(i + 1):
                            for h in range(2):
                                cols = slice(AD * h, AD * h + AD)
                                pe.matmul(ps[cols, 6, 0:P], lhsT=v[:, f, b * TT + j, cols], rhs=probT[:, (2 * w + h) % 4, j, :],
                                          start=(j == 0), stop=(j == i), skip_group_check=True)
                        pe.wait_ge(sems["spread_done"], w + 1)
                        pe.transpose(ps[:, 6, P:2 * P], spread[:, w % 2, :, :].rearrange("p h c -> p (h c)"),
                                     cst["ident"][:, :]).then_inc(sems["o_done"], 1)

                    scores(0)
                    for u in range(U + 1):
                        if u + 1 < U:
                            scores(u + 1)
                        if u in at_step:
                            piece(u)
                        if u < U:
                            turn(u)
                        if u >= 2 and u % 2 == 0:
                            values(u // 2 - 1)

                @block.scalar
                def _(act):
                    def exponent(u):
                        w, h = u // 2, u % 2
                        n = tiles(u) * P
                        act.wait_ge(sems["max_done"], u + 1)
                        if u >= 2:
                            act.wait_ge(sems["pt_done"], turned(u - 2))
                        if w >= 4:
                            act.wait_ge(sems["recip_done"], w - 3)
                        src = ps[:, 2 * (u % 2):2 * (u % 2) + 2, :].rearrange("p k e -> p (k e)")[:, 0:n]
                        nc.scalar.activation(prob[:, u % 2, 0:n], src, ACT.Exp, bias=nmax[:, u % 4:u % 4 + 1],
                                             accum_out=total[:, w % 4, h:h + 1]).then_inc(sems["exp_done"], 1)

                    for u in range(U + 2):
                        if u < U:
                            exponent(u)
                        if u - 1 in at_step and at_step[u - 1][1] < 8:
                            f, n = at_step[u - 1]
                            act.wait_ge(sems["piece_done"], len(PIECES) * f + n + 1)
                            keep_qk(ps[:, 7, :], 1 - f, PIECES[n]).then_inc(sems["piece_kept_a"], 1)
                        if 1 <= u <= U and tiles(u - 1) > 4:
                            x = u - 1
                            act.wait_ge(sems["pt_done"], turned(x))
                            if x >= 4:
                                act.wait_ge(sems["o_done"], x // 2 - 1)
                            rest = tiles(x) - 4
                            nc.scalar.copy(probT[:, x % 4, 4:tiles(x), :], ps[:, 5, 0:rest * P].rearrange(
                                "p (j t) -> p j t", j=rest)).then_inc(sems["pt_kept_a"], 1)
                        if u >= 3 and u % 2 == 1:
                            w = (u - 3) // 2
                            act.wait_ge(sems["o_done"], w + 1)
                            if w >= 2:
                                act.wait_ge(sems["y_done"], w - 1)
                            nc.scalar.copy(recipT[:, w % 2, :], ps[:, 6, P:2 * P]).then_inc(sems["recip_kept"], 1)

                @block.vector
                def _(dve):
                    def row_max(u):
                        n = tiles(u) * P
                        dve.wait_ge(sems["s_done"], u + 1)
                        if u >= 4:
                            dve.wait_ge(sems["exp_done"], u - 3)
                        src = ps[:, 2 * (u % 2):2 * (u % 2) + 2, :].rearrange("p k e -> p (k e)")[:, 0:n]
                        nc.vector.tensor_reduce(nmax[:, u % 4:u % 4 + 1], src, axis=AX.X, op=ALU.max, negate=True).then_inc(
                            sems["max_done"], 1)

                    row_max(0)
                    for u in range(U + 2):
                        if u + 1 < U:
                            row_max(u + 1)
                        if u < U:
                            dve.wait_ge(sems["pt_done"], u + 1 + (two_chunks[u - 1] if u else 0))
                            if u >= 4:
                                dve.wait_ge(sems["o_done"], u // 2 - 1)
                            k = min(4, tiles(u))
                            nc.vector.tensor_copy(probT[:, u % 4, 0:k, :], ps[:, 4, 0:k * P].rearrange(
                                "p (j t) -> p j t", j=k)).then_inc(sems["pt_kept_v"], 1)
                            if u % 2:
                                w = u // 2
                                dve.wait_ge(sems["exp_done"], u + 1)
                                if w >= 4:
                                    dve.wait_ge(sems["spread_done"], w - 3)
                                nc.vector.reciprocal(inv[:, w % 4, :], total[:, w % 4, :]).then_inc(sems["recip_done"], 1)
                        if u in at_step and at_step[u][1] >= 8:
                            f, n = at_step[u]
                            dve.wait_ge(sems["piece_done"], len(PIECES) * f + n + 1)
                            keep_v(ps[:, 7, :], 1 - f, PIECES[n]).then_inc(sems["piece_kept_v"], 1)
                        if u >= 3 and u % 2 == 1:
                            w = (u - 3) // 2
                            f, b, i = pairs[w]
                            dve.wait_ge(sems["recip_kept"], w + 1)
                            view = "p (m n t) -> p m n t"
                            nc.vector.tensor_tensor(y_row[:, bass.ds(2 * it + f, 1), b, 2 * i:2 * i + 2, :],
                                                    ps[:, 6, 0:P].rearrange(view, m=1, n=2),
                                                    recipT[:, w % 2, :].rearrange(view, m=1, n=2),
                                                    ALU.mult).then_inc(sems["y_done"], 1)
            stage_end(nc, list(sems.values()))


def project_out(nc, ctx, ps, wout, yT, res, loads):
    out_done = ctx.enter_context(nc.semaphore("b_out_done"))
    with nc.Block() as block:
        @block.sync
        def _(sp):
            for semaphore, pairs in loads:
                for dst, src in pairs:
                    sp.dma_start(dst, src).then_inc(semaphore, 16)

        @block.tensor
        def _(pe):
            for n in range(NT):
                for m in range(NP):
                    mm = pe.matmul(ps[:, n // 4, (n % 4) * P:(n % 4 + 1) * P], lhsT=yT[:, m, n * P:(n + 1) * P],
                                   rhs=wout[:, m, :], start=(m == 0), stop=(m == NP - 1), skip_group_check=True)
                if n % 4 == 3:
                    mm.then_inc(out_done, 1)

        @block.vector
        def _(dve):
            for m in range(NT // 4):
                dve.wait_ge(out_done, m + 1)
                part = res[:, 4 * m:4 * m + 4, :]
                nc.vector.tensor_tensor(part, part, ps[:, m, :].rearrange("p (t c) -> p t c", t=4), ALU.add)


F0_WIDTHS = [128] * 4 + [256] * 4
F1_WIDTHS = [512] * NE


def program(nc, d, out):
    with ExitStack() as ctx:
        def sb(name, shape, dt=F32):
            return ctx.enter_context(nc.sbuf_tensor(name, shape, dt))
        ps = ctx.enter_context(nc.psum_tensor("ps", [P, 8, 512], F32))
        cst = {"ident": sb("ident", [P, P]), "centre": sb("centre", [P, P]), "mean_col": sb("mean_col", [P, 1]), "minus_half": sb("minus_half", [P, H]),
               "head_sum": sb("head_sum", [P, 2, P]), "same_head": sb("same_head", [P, P]), "eps": sb("eps", [P, 1]),
               "pair_rows": sb("pair_rows", [P, G]), "lower": sb("lower", [P, NE, NE]),
               "causal_head": sb("causal_head", [P, P]), "above_diag": sb("above_diag", [P, P], BF16),
               "ident16": sb("ident16", [P, P], BF16)}
        stream = sb("stream", [P, 1 + NT, C])
        res = stream[:, 1:, :]
        delta_attention(nc, cst, ps, d, stream)
        xT = sb("xTn", [C, B * T])
        comb = sb("comb", [P, NT, NE])
        HD = AH * AD
        wdown, wout = sb("wdown", [C, P]), sb("wout", [P, NP, C])
        wq, wkv = sb("wq", [C, HD + P]), sb("wkv", [P, 2 * HD + P])
        f0_loaded, attention_loaded, f1_loaded = (ctx.enter_context(nc.semaphore(n)) for n in
                                                  ("f0_loaded", "attention_loaded", "f1_loaded"))
        with ExitStack() as own:
            ff = sum(F0_WIDTHS)
            w1, w2, wr = (own.enter_context(nc.sbuf_tensor(n, shape, F32)) for n, shape in
                          (("f0_w1", [C, ff]), ("f0_w2", [P, ff // P, C]), ("f0_wr", [C, NE])))
            layer_norm(nc, ctx, cst, ps, res, xT, "n0", arrived=[(f0_loaded, 3)], loads=[
                (f0_loaded, [(wr[:, :], d["f0_wr"]), (w1[:, :], d["f0_w1"]), (w2[:, :, :], d["f0_w2"])]),
                (attention_loaded, [(wdown[:, :], d["w_kv_down"]), (wq[:, 0:HD], d["w_q"]), (wkv[:, 0:2 * HD], d["w_kv_up"]),
                                    (wout[:, :, :], d["w_out"])])])
            route(nc, ctx, cst, ps, xT, wr, None, comb, "r0")
            experts(nc, ctx, cst, ps, xT, res, comb, w1, w2, F0_WIDTHS, None, None, "f0")
        layer_norm(nc, ctx, cst, ps, res, xT, "n1", arrived=[(attention_loaded, 4)])
        yT = sb("b_yT", [P, NP, B * T])
        softmax_attention(nc, ctx, cst, ps, (wdown, wq, wkv), xT, yT)
        ff = sum(F1_WIDTHS)
        w1, w2, wr = sb("f1_w1", [C, ff]), sb("f1_w2", [P, ff // P, C]), sb("f1_wr", [C, NE])
        b1, b2, br = sb("f1_b1", [P, ff // P]), sb("f1_b2", [NE, C]), sb("f1_br", [P, NE])
        f1_pairs = [(wr[:, :], d["f1_wr"]), (br[:, :], d["f1_br"].partition_broadcast(P)),
                    (w1[:, :].rearrange("c (e f) -> c e f", e=NE), d["f1_w1"]), (w2[:, :, :], d["f1_w2"]),
                    (b1[:, :], d["f1_b1"]), (b2[:, :], d["f1_b2"])]
        project_out(nc, ctx, ps, wout, yT, res, [(f1_loaded, f1_pairs)])
        layer_norm(nc, ctx, cst, ps, res, xT, "n2", arrived=[(f1_loaded, len(f1_pairs))])
        route(nc, ctx, cst, ps, xT, wr, br, comb, "r1")
        experts(nc, ctx, cst, ps, xT, res, comb, w1, w2, F1_WIDTHS, b1, b2, "f1")
        layer_norm(nc, ctx, cst, ps, res, None, "n3", out=out)


def lay_out(i):
    import numpy as np
    a = {k: np.asarray(v) for k, v in i.items()}
    x = a["L0_attn_x"]
    pre = "L0_attn_"
    chan = lambda v, n: v.reshape(n, P).T
    taps = np.concatenate([a[pre + n + "_w"][:, 0, :] for n in ("qc", "kc", "vc")], 0).T
    rows = lambda w: w.reshape(-1, P, C).transpose(1, 0, 2)
    return {
        "xT": x.transpose(2, 0, 1), "x_tok": x.reshape(B, NT, TS, C).transpose(0, 2, 1, 3).reshape(P, NT, C),
        "WqT": a[pre + "Wq"].T, "WkT": a[pre + "Wk"].T, "WvT": a[pre + "Wv"].T, "WaT": a[pre + "Wa"].T,
        "WgT": a[pre + "Wg"].T, "WbT": a[pre + "Wb"].T,
        "WoT": a[pre + "Wo"].reshape(C, H, DV).transpose(2, 1, 0), "taps": taps,
        "conv_b": np.concatenate([chan(a[pre + n + "_b"], m) for n, m in (("qc", G), ("kc", G), ("vc", H))], 1),
        "ba": chan(a[pre + "ba"], H), "bb": a[pre + "bb"], "ln_w": a[pre + "ln_w"][:, None], "ln_b": a[pre + "ln_b"][:, None],
        "f0_w1": a["L0_ffn_w1"], "f0_w2": rows(a["L0_ffn_w2"]), "f0_wr": a["L0_ffn_router_w"].T,
        "w_kv_down": a["L1_attn_w_kv_down"], "w_q": a["L1_attn_w_q"], "w_kv_up": a["L1_attn_w_kv_up"],
        "w_out": rows(a["L1_attn_w_out"]),
        "f1_w1": a["L1_ffn_W1"].transpose(1, 0, 2), "f1_w2": rows(a["L1_ffn_W2"]), "f1_wr": a["L1_ffn_W_router"],
        "f1_b1": chan(a["L1_ffn_b1"].reshape(-1), sum(F1_WIDTHS) // P), "f1_b2": a["L1_ffn_b2"], "f1_br": a["L1_ffn_b_router"],
    }


def kernel(**inputs):
    import numpy as np
    import concourse.bacc as bacc
    from concourse.bass_utils import run_bass_kernel_spmd
    nc = bacc.Bacc("TRN2", target_bir_lowering=False, num_devices=1)
    arrays = {"in_" + k: np.ascontiguousarray(v) for k, v in lay_out(inputs).items()}
    d = {k[3:]: nc.dram_tensor(k, v.shape, F32, kind="ExternalInput").ap() for k, v in arrays.items()}
    out = nc.dram_tensor("out", (P, NT, C), F32, kind="ExternalOutput").ap()
    program(nc, d, out)
    r = run_bass_kernel_spmd(nc, [arrays], core_ids=[0])
    return r.results[0]["out"].reshape(B, TS, NT, C).transpose(0, 2, 1, 3).reshape(B, T, C)
```
